# Optimizing a Trainium2 kernel written in Bass

```python
import numpy as np
import jax
import jax.numpy as jnp

def _softmax(x, axis=-1):
    return jax.nn.softmax(x, axis=axis)

def _gelu(x):
    return jax.nn.gelu(x, approximate=True)

def _silu(x):
    return jax.nn.silu(x)

def _sigmoid(x):
    return jax.nn.sigmoid(x)

def _layernorm(x, axis=-1, eps=1e-05):
    m = jnp.mean(x, axis=axis, keepdims=True)
    v = jnp.var(x, axis=axis, keepdims=True)
    return (x - m) / jnp.sqrt(v + eps)

def _scatter_add(tgt, idx, src, axis=0):
    return tgt.at[idx].add(src)

def _segment_sum(src, seg, n):
    return jax.ops.segment_sum(src, seg, n)
kernel_name = 'mk_hybrid_d1_jaxref_r4_8a3b77'

def setup_inputs(seed: int=0):
    np.random.seed(seed)
    _w = jnp.asarray

    def _L0_attn_a_setup():
        import math
        import jax, jax.numpy as jnp
        import numpy as np
        D_MODEL = 256
        N_HEADS = 16
        HEAD_DIM = D_MODEL // N_HEADS
        ROPE_THETA = 10000.0

        def _apply_rope(t, offset=0):
            B, H, T, Dh = t.shape
            inv_freq = 1.0 / ROPE_THETA ** (jnp.arange(0, Dh, 2, dtype=jnp.float32) / Dh)
            pos = jnp.arange(T, dtype=jnp.float32) + offset
            ang = pos[:, None] * inv_freq[None, :]
            cos = jnp.concatenate([jnp.cos(ang), jnp.cos(ang)], axis=-1)
            sin = jnp.concatenate([jnp.sin(ang), jnp.sin(ang)], axis=-1)
            t1, t2 = (t[..., :Dh // 2], t[..., Dh // 2:])
            rot = jnp.concatenate([-t2, t1], axis=-1)
            return t * cos + rot * sin

        def _forward(x, Wq, Wk, Wv, Wo):
            B, T, _ = x.shape
            scale = 1.0 / math.sqrt(HEAD_DIM)

            def split_heads(y):
                return y.reshape(B, T, N_HEADS, HEAD_DIM).transpose(0, 2, 1, 3)
            q = split_heads(x @ Wq.T)
            k = split_heads(x @ Wk.T)
            v = split_heads(x @ Wv.T)
            q = _apply_rope(q)
            k = _apply_rope(k)
            scores = jnp.einsum('bhtd,bhsd->bhts', q, k) * scale
            causal = jnp.triu(jnp.ones((T, T), dtype=bool), k=1)
            scores = jnp.where(causal[None, None], -jnp.inf, scores)
            attn = jax.nn.softmax(scores, axis=-1)
            attn = jnp.nan_to_num(attn, nan=0.0)
            out = jnp.einsum('bhts,bhsd->bhtd', attn, v)
            out = out.transpose(0, 2, 1, 3).reshape(B, T, N_HEADS * HEAD_DIM)
            return out @ Wo.T
        key = jax.random.key(seed)
        ks = jax.random.split(key, 5)
        B, T = (4, 512)
        w_scale = math.sqrt(2.0 / (D_MODEL + D_MODEL))
        return {'x': jax.random.normal(ks[0], (B, T, D_MODEL), dtype=jnp.float32), 'Wq': jax.random.normal(ks[1], (D_MODEL, D_MODEL), dtype=jnp.float32) * w_scale, 'Wk': jax.random.normal(ks[2], (D_MODEL, D_MODEL), dtype=jnp.float32) * w_scale, 'Wv': jax.random.normal(ks[3], (D_MODEL, D_MODEL), dtype=jnp.float32) * w_scale, 'Wo': jax.random.normal(ks[4], (D_MODEL, D_MODEL), dtype=jnp.float32) * w_scale}
    _L0_attn_a_in = _L0_attn_a_setup()

    def _L0_attn_b_setup():
        import jax, jax.numpy as jnp
        from jax import lax
        import numpy as np
        HEAD_SIZE = 64
        D_MIX = 32
        D_DECAY = 64
        D_GATE = 64

        def _wkv6(r, k, v, w, u):
            B, T, C = r.shape
            N = HEAD_SIZE
            H = C // N
            to_h = lambda a: a.reshape(B, T, H, N).transpose(1, 0, 2, 3)
            rT, kT, vT, wT = map(to_h, (r, k, v, w))

            def step(S, inp):
                rt, kt, vt, wt = inp
                kv = kt[..., :, None] * vt[..., None, :]
                y = jnp.einsum('bhi,bhij->bhj', rt, S + u[None, :, :, None] * kv)
                S = wt[..., None] * S + kv
                return (S, y)
            S0 = jnp.zeros((B, H, N, N), r.dtype)
            _, y = lax.scan(step, S0, (rT, kT, vT, wT))
            return y.transpose(1, 0, 2, 3).reshape(B, T, C)
        key = jax.random.key(seed)
        B, T, C = (4, 512, 256)
        H = C // HEAD_SIZE
        ks = jax.random.split(key, 24)
        n = lambda i, shape, s=1.0: jax.random.normal(ks[i], shape, dtype=jnp.float32) * s
        return {'x': n(0, (B, T, C)), 'maa_x': n(1, (C,), 0.1), 'maa_w': n(2, (C,), 0.1), 'maa_k': n(3, (C,), 0.1), 'maa_v': n(4, (C,), 0.1), 'maa_r': n(5, (C,), 0.1), 'maa_g': n(6, (C,), 0.1), 'maa_w1': n(7, (C, 5 * D_MIX), 0.01), 'maa_w2': n(8, (5, D_MIX, C), 0.01), 'Wr': n(9, (C, C), C ** (-0.5)), 'Wk': n(10, (C, C), C ** (-0.5)), 'Wv': n(11, (C, C), C ** (-0.5)), 'Wo': n(12, (C, C), C ** (-0.5)), 'gate_w1': n(13, (C, D_GATE), 0.01), 'gate_w2': n(14, (D_GATE, C), 0.01), 'time_decay': n(15, (C,), 1.0) - 4.0, 'decay_w1': n(16, (C, D_DECAY), 0.01), 'decay_w2': n(17, (D_DECAY, C), 0.01), 'u': n(18, (H, HEAD_SIZE), 0.1), 'ln_g': jnp.ones((C,), jnp.float32), 'ln_b': jnp.zeros((C,), jnp.float32)}
    _L0_attn_b_in = _L0_attn_b_setup()

    def _L0_ffn_setup():
        import jax, jax.numpy as jnp
        import numpy as np
        DIM = 256
        HIDDEN = 768
        SCALE = 1.0 / 127.0

        def _dequant(w_int, dtype):
            return w_int.astype(dtype) * jnp.asarray(SCALE, dtype)
        key = jax.random.key(seed)
        k_x, k_g, k_u, k_d = jax.random.split(key, 4)
        x = jax.random.normal(k_x, (4, 512, DIM), dtype=jnp.float32)
        w_gate = jax.random.randint(k_g, (HIDDEN, DIM), -127, 128, dtype=jnp.int32)
        w_up = jax.random.randint(k_u, (HIDDEN, DIM), -127, 128, dtype=jnp.int32)
        w_down = jax.random.randint(k_d, (DIM, HIDDEN), -127, 128, dtype=jnp.int32)
        return {'x': x, 'w_gate': w_gate, 'w_up': w_up, 'w_down': w_down}
    _L0_ffn_in = _L0_ffn_setup()
    _d = {'L0_attn_a_x': _L0_attn_a_in['x'], 'L0_attn_a_Wq': _L0_attn_a_in['Wq'], 'L0_attn_a_Wk': _L0_attn_a_in['Wk'], 'L0_attn_a_Wv': _L0_attn_a_in['Wv'], 'L0_attn_a_Wo': _L0_attn_a_in['Wo'], 'L0_attn_b_maa_x': _L0_attn_b_in['maa_x'], 'L0_attn_b_maa_w': _L0_attn_b_in['maa_w'], 'L0_attn_b_maa_k': _L0_attn_b_in['maa_k'], 'L0_attn_b_maa_v': _L0_attn_b_in['maa_v'], 'L0_attn_b_maa_r': _L0_attn_b_in['maa_r'], 'L0_attn_b_maa_g': _L0_attn_b_in['maa_g'], 'L0_attn_b_maa_w1': _L0_attn_b_in['maa_w1'], 'L0_attn_b_maa_w2': _L0_attn_b_in['maa_w2'], 'L0_attn_b_Wr': _L0_attn_b_in['Wr'], 'L0_attn_b_Wk': _L0_attn_b_in['Wk'], 'L0_attn_b_Wv': _L0_attn_b_in['Wv'], 'L0_attn_b_Wo': _L0_attn_b_in['Wo'], 'L0_attn_b_gate_w1': _L0_attn_b_in['gate_w1'], 'L0_attn_b_gate_w2': _L0_attn_b_in['gate_w2'], 'L0_attn_b_time_decay': _L0_attn_b_in['time_decay'], 'L0_attn_b_decay_w1': _L0_attn_b_in['decay_w1'], 'L0_attn_b_decay_w2': _L0_attn_b_in['decay_w2'], 'L0_attn_b_u': _L0_attn_b_in['u'], 'L0_attn_b_ln_g': _L0_attn_b_in['ln_g'], 'L0_attn_b_ln_b': _L0_attn_b_in['ln_b'], 'L0_ffn_w_gate': _L0_ffn_in['w_gate'], 'L0_ffn_w_up': _L0_ffn_in['w_up'], 'L0_ffn_w_down': _L0_ffn_in['w_down']}
    _x0 = _d['L0_attn_a_x']
    _d['L0_attn_a_x'] = jax.random.normal(jax.random.fold_in(jax.random.key(seed), 1), (8, 1024, 256), dtype=_x0.dtype)
    del _x0
    return _d

def reference(L0_attn_a_x, L0_attn_a_Wq, L0_attn_a_Wk, L0_attn_a_Wv, L0_attn_a_Wo, L0_attn_b_maa_x, L0_attn_b_maa_w, L0_attn_b_maa_k, L0_attn_b_maa_v, L0_attn_b_maa_r, L0_attn_b_maa_g, L0_attn_b_maa_w1, L0_attn_b_maa_w2, L0_attn_b_Wr, L0_attn_b_Wk, L0_attn_b_Wv, L0_attn_b_Wo, L0_attn_b_gate_w1, L0_attn_b_gate_w2, L0_attn_b_time_decay, L0_attn_b_decay_w1, L0_attn_b_decay_w2, L0_attn_b_u, L0_attn_b_ln_g, L0_attn_b_ln_b, L0_ffn_w_gate, L0_ffn_w_up, L0_ffn_w_down):

    def _L0_attn_a_ref(x, Wq, Wk, Wv, Wo):
        import math
        import jax, jax.numpy as jnp
        import numpy as np
        D_MODEL = 256
        N_HEADS = 16
        HEAD_DIM = D_MODEL // N_HEADS
        ROPE_THETA = 10000.0

        def _apply_rope(t, offset=0):
            B, H, T, Dh = t.shape
            inv_freq = 1.0 / ROPE_THETA ** (jnp.arange(0, Dh, 2, dtype=jnp.float32) / Dh)
            pos = jnp.arange(T, dtype=jnp.float32) + offset
            ang = pos[:, None] * inv_freq[None, :]
            cos = jnp.concatenate([jnp.cos(ang), jnp.cos(ang)], axis=-1)
            sin = jnp.concatenate([jnp.sin(ang), jnp.sin(ang)], axis=-1)
            t1, t2 = (t[..., :Dh // 2], t[..., Dh // 2:])
            rot = jnp.concatenate([-t2, t1], axis=-1)
            return t * cos + rot * sin

        def _forward(x, Wq, Wk, Wv, Wo):
            B, T, _ = x.shape
            scale = 1.0 / math.sqrt(HEAD_DIM)

            def split_heads(y):
                return y.reshape(B, T, N_HEADS, HEAD_DIM).transpose(0, 2, 1, 3)
            q = split_heads(x @ Wq.T)
            k = split_heads(x @ Wk.T)
            v = split_heads(x @ Wv.T)
            q = _apply_rope(q)
            k = _apply_rope(k)
            scores = jnp.einsum('bhtd,bhsd->bhts', q, k) * scale
            causal = jnp.triu(jnp.ones((T, T), dtype=bool), k=1)
            scores = jnp.where(causal[None, None], -jnp.inf, scores)
            attn = jax.nn.softmax(scores, axis=-1)
            attn = jnp.nan_to_num(attn, nan=0.0)
            out = jnp.einsum('bhts,bhsd->bhtd', attn, v)
            out = out.transpose(0, 2, 1, 3).reshape(B, T, N_HEADS * HEAD_DIM)
            return out @ Wo.T
        return _forward(x, Wq, Wk, Wv, Wo)

    def _L0_attn_b_ref(x, maa_x, maa_w, maa_k, maa_v, maa_r, maa_g, maa_w1, maa_w2, Wr, Wk, Wv, Wo, gate_w1, gate_w2, time_decay, decay_w1, decay_w2, u, ln_g, ln_b):
        import jax, jax.numpy as jnp
        from jax import lax
        import numpy as np
        HEAD_SIZE = 64
        D_MIX = 32
        D_DECAY = 64
        D_GATE = 64

        def _wkv6(r, k, v, w, u):
            B, T, C = r.shape
            N = HEAD_SIZE
            H = C // N
            to_h = lambda a: a.reshape(B, T, H, N).transpose(1, 0, 2, 3)
            rT, kT, vT, wT = map(to_h, (r, k, v, w))

            def step(S, inp):
                rt, kt, vt, wt = inp
                kv = kt[..., :, None] * vt[..., None, :]
                y = jnp.einsum('bhi,bhij->bhj', rt, S + u[None, :, :, None] * kv)
                S = wt[..., None] * S + kv
                return (S, y)
            S0 = jnp.zeros((B, H, N, N), r.dtype)
            _, y = lax.scan(step, S0, (rT, kT, vT, wT))
            return y.transpose(1, 0, 2, 3).reshape(B, T, C)
        B, T, C = x.shape
        H, N = (C // HEAD_SIZE, HEAD_SIZE)
        xx = jnp.concatenate([jnp.zeros_like(x[:, :1]), x[:, :-1]], axis=1) - x
        xxx = x + xx * maa_x
        lora = jnp.tanh(xxx @ maa_w1).reshape(B, T, 5, D_MIX)
        m = jnp.einsum('btfd,fdc->fbtc', lora, maa_w2)
        mw, mk, mv, mr, mg = (m[0], m[1], m[2], m[3], m[4])
        xw = x + xx * (maa_w + mw)
        xk = x + xx * (maa_k + mk)
        xv = x + xx * (maa_v + mv)
        xr = x + xx * (maa_r + mr)
        xg = x + xx * (maa_g + mg)
        r = xr @ Wr
        k = xk @ Wk
        v = xv @ Wv
        g = jnp.tanh(xg @ gate_w1) @ gate_w2
        w = time_decay + jnp.tanh(xw @ decay_w1) @ decay_w2
        wdec = jnp.exp(-jnp.exp(w))
        y = _wkv6(r, k, v, wdec, u)
        yh = y.reshape(B, T, H, N)
        mu = yh.mean(-1, keepdims=True)
        var = yh.var(-1, keepdims=True)
        yn = ((yh - mu) / jnp.sqrt(var + 0.00064)).reshape(B, T, C) * ln_g + ln_b
        return yn * g @ Wo

    def _L0_ffn_ref(x, w_gate, w_up, w_down):
        import jax, jax.numpy as jnp
        import numpy as np
        DIM = 256
        HIDDEN = 768
        SCALE = 1.0 / 127.0

        def _dequant(w_int, dtype):
            return w_int.astype(dtype) * jnp.asarray(SCALE, dtype)
        wg = _dequant(w_gate, x.dtype)
        wu = _dequant(w_up, x.dtype)
        wd = _dequant(w_down, x.dtype)
        gate = jnp.einsum('bsd,hd->bsh', x, wg)
        up = jnp.einsum('bsd,hd->bsh', x, wu)
        h = jax.nn.silu(gate) * up
        return jnp.einsum('bsh,dh->bsd', h, wd)
    x = L0_attn_a_x
    x = x + _L0_attn_a_ref(_layernorm(x, axis=-1), L0_attn_a_Wq, L0_attn_a_Wk, L0_attn_a_Wv, L0_attn_a_Wo)
    x = x + _L0_ffn_ref(_layernorm(x, axis=-1), L0_ffn_w_gate, L0_ffn_w_up, L0_ffn_w_down)
    x = x + _L0_attn_b_ref(_layernorm(x, axis=-1), L0_attn_b_maa_x, L0_attn_b_maa_w, L0_attn_b_maa_k, L0_attn_b_maa_v, L0_attn_b_maa_r, L0_attn_b_maa_g, L0_attn_b_maa_w1, L0_attn_b_maa_w2, L0_attn_b_Wr, L0_attn_b_Wk, L0_attn_b_Wv, L0_attn_b_Wo, L0_attn_b_gate_w1, L0_attn_b_gate_w2, L0_attn_b_time_decay, L0_attn_b_decay_w1, L0_attn_b_decay_w2, L0_attn_b_u, L0_attn_b_ln_g, L0_attn_b_ln_b)
    x = x + _L0_ffn_ref(_layernorm(x, axis=-1), L0_ffn_w_gate, L0_ffn_w_up, L0_ffn_w_down)
    return x

_drawn_inputs = setup_inputs


def setup_inputs(seed=0):
    import zlib

    import numpy as np

    out = dict(_drawn_inputs(seed))
    spreads = {'L0_attn_b_ln_g': (1.0, 0.6), 'L0_attn_b_ln_b': (0.0, 2.0)}
    factors = {'L0_attn_b_maa_x': 64.0,
     'L0_attn_b_maa_w': 64.0,
     'L0_attn_b_maa_k': 64.0,
     'L0_attn_b_maa_v': 64.0,
     'L0_attn_b_maa_r': 64.0,
     'L0_attn_b_maa_g': 64.0,
     'L0_attn_b_maa_w1': 64.0,
     'L0_attn_b_maa_w2': 64.0,
     'L0_attn_b_Wr': 59.842,
     'L0_attn_b_Wk': 59.446,
     'L0_attn_b_Wv': 60.003,
     'L0_attn_b_Wo': 52.781,
     'L0_attn_b_gate_w1': 52.916,
     'L0_attn_b_gate_w2': 53.527,
     'L0_attn_b_time_decay': 64.0,
     'L0_attn_b_decay_w1': 64.0,
     'L0_attn_b_decay_w2': 64.0,
     'L0_attn_b_u': 64.0}
    for name, (base, spread) in spreads.items():
        noise = np.random.default_rng([zlib.crc32(name.encode()), seed]).standard_normal(out[name].shape)
        drawn = base * np.exp(spread * noise) if base else spread * noise
        out[name] = jnp.asarray(drawn.astype(out[name].dtype))
    for name, factor in factors.items():
        out[name] = (out[name] * factor).astype(out[name].dtype)
    return out
```

```python
import concourse.bass as bass
from concourse import mybir
from contextlib import ExitStack

NB, T, D = 8, 1024, 256
NT = T // 128
HALF = 512
NC = D // 128
NH, DH = 16, 16
HG = 4
NG = NH // HG
HID = 768
NM = HID // 128
DMIX, NMIX = 32, 5
DLOW = 64
WH = 64
NEG = -1.0e38
RING = 6
SPLIT_Q = [0, 0, 1, 1, 0, 2]
SPLIT_K = [0, 1, 0, 1, 2, 0]
AUG = DH * 6
MIX_ORDER = [0, 4, 3, 1, 2]
LEVELS = 7


def score_units():
    return [(j, f) for j in range(NT) for f in (0, 1) if 128 * j < HALF * (f + 1)]


def max_pieces():
    out = []
    for i in range(NT):
        out.append((i, 0, min(HALF, 128 * (i + 1)), i))
        if i >= 4:
            out.append((i, HALF, 128 * (i + 1) - HALF, NT + i - 4))
    return out


UNITS = score_units()
PIECES = max_pieces()
NPC = len(PIECES) * HG
LAG = 6


def psum_plan():
    p = []

    def add(kind, n, who):
        p.extend((kind, i, who) for i in range(n))

    def ffn(k):
        add(f"ln{k}", 4, "act")
        for f in (0, 1):
            for e in range(2 * NM):
                p.append((f"gu{k}", 2 * NM * f + e, "dve"))
                if f == 1 and e in (3, 7):
                    p.append((f"dn{k}", e // 4, "dve"))
        p.extend((f"dn{k}", i, "dve") for i in (2, 3))

    add("ln0", 4, "act")
    add("qk", 16, "dve")
    for s in range(NG + 1):
        for k in range(NPC + LAG):
            if s < NG and k < NPC:
                p.append(("max", s * NPC + k, "dve"))
            if s == 0 and k < 24 and k % 6 == 5:
                p.append(("v", k // 6, "act"))
            if s >= 2 and k == 5:
                p.extend(("den", 2 * (s - 2) + f, "dve") for f in (0, 1))
            if s >= 1 and k >= LAG:
                p.append(("score", (s - 1) * NPC + k - LAG, "act"))
        if s < NG:
            p.append(("aug", s, "dve"))
    p.extend(("den", 2 * (NG - 1) + f, "dve") for f in (0, 1))
    add("o", 4, "dve")
    ffn(1)
    add("ln2", 4, "act")
    add("lora", 4, "act")
    mixed = {0: [], 1: [("dech", 2, "act")], 2: [("gateh", 2, "act")], 3: [("w", 4, "act"), ("r", 4, "act")],
             4: [("g", 4, "act"), ("k", 4, "act"), ("vb", 4, "act")]}
    for n in range(NMIX):
        p.extend(("mix", 4 * n + i, "dve") for i in range(4))
        for m in mixed[n]:
            add(*m)
    add("diag", 8, "dve")
    add("level", LEVELS * 4, "dve")
    add("kt", 4, "act")
    add("kv", 4, "dve")
    add("y", 4, "dve")
    add("zt", 4, "act")
    add("ob", 4, "dve")
    ffn(3)
    return p


PLAN = psum_plan()
NTH = {(kind, i): n for n, (kind, i, _) in enumerate(PLAN)}
_seen = {"act": 0, "dve": 0}
RANK = []
for _, _, _who in PLAN:
    _seen[_who] += 1
    RANK.append(_seen[_who])


def build(nc, x_in, w_at, cs, b_vec, b_mat, ffn_w, consts, out, stop_after=None):
    f32, bf16, i32 = mybir.dt.float32, mybir.dt.bfloat16, mybir.dt.int32
    ALU, ACT, AX = mybir.AluOpType, mybir.ActivationFunctionType, mybir.AxisListType
    S8 = 1.0 / 127.0
    ctx = ExitStack()
    with ctx:
        def sb(name, shape, dt=f32):
            return ctx.enter_context(nc.sbuf_tensor(name, shape, dt))

        sems = []

        def sem(name):
            s = ctx.enter_context(nc.semaphore(name))
            sems.append(s)
            return s

        xres = sb("xres", [128, NT, D])
        xT = sb("xT", [128, NC, 1 + T])
        attn = sb("attn", [128, NT, HG, 128])
        xn = attn[:, :, :, :].rearrange("p i g t -> p i (g t)")[:, :, 0:D]
        spare = attn[:, :, :, :].rearrange("p i g t -> p i (g t)")[:, :, D:2 * D]
        rope = sb("rope", [128, 2, T])
        wqkv = sb("wqkv", [128, NC, 5 * D])
        wo = sb("wo", [128, NG, D])
        wgu = sb("wgu", [128, NC, 2 * HID])
        wd = sb("wd", [128, NM, D])
        bm = sb("bm", [128, NC, 4 * D])
        mw1 = sb("mw1", [128, NC, NMIX * DMIX])
        mw2 = sb("mw2", [128, NMIX, D])
        low1 = sb("low1", [128, NC, 2 * DLOW])
        low2 = sb("low2", [128, 2, D])
        lng = sb("lng", [128, 2, D])
        vec = sb("vec", [128, 8, NC])
        ident = sb("ident", [128, 128])
        identb = sb("identb", [128, 128], bf16)
        causal = sb("causal", [128, 2, 128], bf16)
        denrow = sb("denrow", [128, 128])
        lmask = sb("lmask", [128, LEVELS, 64], i32)
        dmask = sb("dmask", [128, 128], i32)
        half_neg = sb("half_neg", [128, 8])
        stats = sb("stats", [128, NT, 6])
        mv = sb("mv", [128, NT, 2])
        rstd = sb("rstd", [128, NT])
        mxp = sb("mxp", [128, 2, HG, 12])
        augf = sb("augf", [128, HG * NT])
        aug = sb("aug", [128, 3, HG, NT], bf16)
        augT = sb("augT", [96, 2, 128], bf16)
        gst = sb("gst", [128, 8, 6])
        gmv = sb("gmv", [128, 2, 8, 2])
        grs = sb("grs", [128, 2, 8])

        ARENA = 27 * 1024
        arena = sb("arena", [128, ARENA])
        at = [0]

        def take(n, dt=f32, first=None):
            if first is not None:
                at[0] = first
            a = arena[:, at[0]:at[0] + n]
            at[0] += n
            assert at[0] <= ARENA, at[0]
            return a if dt == f32 else a.bitcast(dt)

        qst = take(8192, bf16, 0).rearrange("p (h t) -> p h t", h=NH)
        kst = take(8192, bf16).rearrange("p (h t) -> p h t", h=NH)
        ptf = take(6144)
        pt = ptf.rearrange("p (u h t) -> p u h t", u=3, h=HG)
        spl = ptf.bitcast(bf16).rearrange("p (m q s t) -> p m q s t", m=2, q=2, s=3)
        vp = take(4096).rearrange("p (i h d) -> p i h d", i=NT, h=NH)
        rden = take(1024).rearrange("p (f t) -> p f t", f=2)
        ta = [spare[:, 2 * k:2 * k + 2, :] for k in range(4)]

        hT = take(6144, f32, 0).rearrange("p (m t) -> p m t", m=NM)
        tb = take(1024).rearrange("p (f t) -> p f t", f=2)
        ub = take(1024).rearrange("p (f t) -> p f t", f=2)

        def ct(a):
            return a.rearrange("p (c t) -> p c t", c=NC)

        xx_f = take(2048, f32, 0)
        xx, zT = ct(xx_f), ct(xx_f)
        xxx_f = take(2048)
        xxx, kn = ct(xxx_f), xxx_f.rearrange("p (c n i) -> p c n i", c=NC, n=NT)
        lora_f = take(2048)
        lora, S = ct(lora_f), lora_f[:, 0:1024].rearrange("p (c n j) -> p c n j", c=NC, n=NT)
        xf_f = take(4096)
        xf = xf_f.rearrange("p (b c t) -> p b c t", b=2, c=NC)
        A = xf_f.rearrange("p (c n h t) -> p c n h t", c=NC, n=NT, h=2)
        th = take(1024)
        wdec = ct(take(2048))
        kk = ct(take(2048))
        ku = ct(take(2048))
        tot = ct(take(2048))
        vt = take(2048).rearrange("p (i n) -> p i n", i=NT)
        gt = take(2048).rearrange("p (i n) -> p i n", i=NT)
        qd = take(4096).rearrange("p (c h t) -> p c h t", c=NC, h=2)

        PB = [ctx.enter_context(nc.psum_tensor(f"PB{i}", [128, 512], f32)) for i in range(8)]

        s_w = sem("weights_loaded")
        s_cast = sem("weights_cast")
        s_zero = sem("consts_zeroed")
        filled = sem("psum_filled")
        act_emptied = sem("act_emptied")
        dve_emptied = sem("dve_emptied")
        x_loaded = [sem(f"x_loaded{i}") for i in (0, 1)]
        arena_set = sem("arena_set")
        ln_stat = [sem(f"ln_stat{k}") for k in range(4)]
        ln_aggr = [sem(f"ln_aggr{k}") for k in range(4)]
        ln_eps = [sem(f"ln_eps{k}") for k in range(4)]
        ln_rstd = [sem(f"ln_rstd{k}") for k in range(4)]
        ln_out = [sem(f"ln_out{k}") for k in range(4)]
        resid = [sem(f"resid{k}") for k in range(4)]
        roped = sem("roped")
        hi_done = sem("hi_done")
        rem_done = sem("rem_done")
        mid_done = sem("mid_done")
        lo_done = sem("lo_done")
        stacked = [sem(f"stacked{m}") for m in (0, 1)]
        aug_chain = sem("aug_chain")
        aug_loaded = [sem(f"aug_loaded{g}") for g in range(NG)]
        pv_units = sem("pv_units")
        pv_copied = sem("pv_copied")
        attn_normed = sem("attn_normed")
        tanh_done = [sem("tanh_done1"), sem("tanh_done3")]
        gate_done = [sem("gate_done1"), sem("gate_done3")]
        xx_done = sem("xx_done")
        xxx_done = sem("xxx_done")
        mix_added = sem("mix_added")
        decay_exp = sem("decay_exp")
        qd_zeroed = sem("qd_zeroed")
        a_zeroed = sem("a_zeroed")
        ku_done = sem("ku_done")
        tot_done = sem("tot_done")
        q_updated = sem("q_updated")
        k_updated = sem("k_updated")
        s_zeroed = sem("s_zeroed")
        s_chain = sem("s_chain")
        gn_stat = sem("gn_stat")
        gn_aggr = sem("gn_aggr")
        gn_eps = sem("gn_eps")
        gn_rstd = sem("gn_rstd")
        gn_lng = sem("gn_lng")
        gn_chain = sem("gn_chain")
        stored = sem("stored")

        emptied = {"act": act_emptied, "dve": dve_emptied}

        def bank(kind, i):
            return PB[NTH[kind, i] % RING]

        def wait_filled(eng, kind, i):
            eng.wait_ge(filled, NTH[kind, i] + 1)

        def wait_emptied(eng, kind, i):
            n = NTH[kind, i]
            eng.wait_ge(emptied[PLAN[n][2]], RANK[n])

        def wait_bank(eng, kind, i):
            n = NTH[kind, i] - RING
            if n >= 0:
                eng.wait_ge(emptied[PLAN[n][2]], RANK[n])

        with nc.Block() as block:
            @block.sync
            def _(sp):
                def load(dst, src):
                    sp.dma_start(dst, src).then_inc(s_w, 16)
                for k, w in enumerate(w_at[0:5]):
                    load(wqkv[:, :, D * k:D * k + D], w.rearrange("(c p) n -> p c n", p=128))
                sp.wait_ge(s_zero, 7)
                for h in range(NH):
                    load(wo[32 * (h % HG):32 * (h % HG) + DH, h // HG, :], w_at[5][DH * h:DH * h + DH, :])
                load(rope[:, 0, :], cs[0])
                load(rope[:, 1, :], cs[1])
                for k in range(4):
                    load(bm[:, :, D * k:D * k + D], b_mat[k].rearrange("(c p) n -> p c n", p=128))
                load(mw1[:, :, :], b_mat[4].rearrange("(c p) n -> p c n", p=128))
                for f in range(NMIX):
                    r = 32 * f if f < 4 else 96
                    load(mw2[r:r + 32, f, :], b_mat[5][f, :, :])
                load(low1[:, :, 0:DLOW], b_mat[6].rearrange("(c p) n -> p c n", p=128))
                load(low1[:, :, DLOW:2 * DLOW], b_mat[8].rearrange("(c p) n -> p c n", p=128))
                load(low2[0:DLOW, 0, :], b_mat[7])
                load(low2[DLOW:128, 1, :], b_mat[9])
                load(vec[:, :, :], b_vec[0].rearrange("p (k c) -> p k c", c=NC))
                for k in range(2):
                    load(lng[:, k, :], b_vec[1 + k].partition_broadcast(128))
                load(ident[:, :], consts[0][:, 0:128])
                load(denrow[:, :], consts[0][:, 128:256])
                load(arena[:, 8192:8448], consts[0][:, 256:512])
                load(lmask[:, :, :], consts[1][:, 0:448].rearrange("p (l t) -> p l t", l=LEVELS))
                load(dmask[:, :], consts[1][:, 448:576])
                ai = arena[:, :].bitcast(i32)
                load(ai[:, 0:1536].rearrange("p (c n) -> p c n", c=NC), ffn_w[0].rearrange("(c p) n -> p c n", p=128))
                load(ai[:, 1536:3072].rearrange("p (c n) -> p c n", c=NC), ffn_w[1].rearrange("(c p) n -> p c n", p=128))
                load(ai[:, 3072:4608].rearrange("p (m n) -> p m n", m=NM), ffn_w[2].rearrange("(m p) n -> p m n", p=128))
            NLOAD = 5 + NH + 2 + 4 + 1 + NMIX + 4 + 1 + 2 + 5 + 3

            @block.gpsimd
            def _(pool):
                pool.memset(wo[:, :, :], 0.0).then_inc(s_zero, 1)
                pool.memset(mw2[:, :, :], 0.0).then_inc(s_zero, 1)
                pool.memset(low2[:, :, :], 0.0).then_inc(s_zero, 1)
                pool.memset(half_neg[:, :], -0.5).then_inc(s_zero, 1)
                pool.memset(xT[:, :, 0:1], 0.0).then_inc(s_zero, 1)
                pool.memset(arena[:, 10000:10001], 0.0).then_inc(s_zero, 1)
                pool.memset(augf[:, :], 0.0).then_inc(s_zero, 1)

            @block.vector
            def _(dve):
                dve.wait_ge(s_w, 16 * NLOAD)
                ai = arena[:, :].bitcast(i32)
                dve.tensor_copy(wgu[:, :, 0:HID], ai[:, 0:1536].rearrange("p (c n) -> p c n", c=NC))
                dve.tensor_copy(wgu[:, :, HID:2 * HID], ai[:, 1536:3072].rearrange("p (c n) -> p c n", c=NC))
                dve.tensor_copy(wd[:, :, :], ai[:, 3072:4608].rearrange("p (m n) -> p m n", m=NM))
                dve.tensor_copy(causal[:, :, :], arena[:, 8192:8448].rearrange("p (a n) -> p a n", a=2))
                dve.tensor_copy(identb[:, :], ident[:, :]).then_inc(s_cast, 1)

        with nc.Fori(0, NB) as b:
            with nc.Block() as block:
                @block.sync
                def _(sp):
                    xv = x_in[bass.ds(b, 1), :, :].rearrange("a (i p) c -> p (a i) c", p=128)
                    ov = out[bass.ds(b, 1), :, :].rearrange("a (i p) c -> p (a i) c", p=128)
                    for f in (0, 1):
                        sp.dma_start(xres[:, 4 * f:4 * f + 4, :], xv[:, 4 * f:4 * f + 4, :]).then_inc(x_loaded[f], 16)
                    for m in (0, 1):
                        for q in (0, 1):
                            sp.wait_ge(lo_done, 2 * (2 * m + q) + 2)
                            for h in range(8):
                                for blk in range(6):
                                    dst = (qst, kst)[q][DH * blk:DH * blk + DH, 8 * m + h, :]
                                    part = (SPLIT_Q, SPLIT_K)[q][blk]
                                    sp.dma_start(dst, spl[DH * h:DH * h + DH, m, q, part, :]).then_inc(stacked[m], 16)
                    for g in range(NG):
                        wait_emptied(sp, "aug", g)
                        for r in range(3):
                            sp.dma_start(qst[AUG + r:AUG + r + 1, HG * g:HG * g + HG, :],
                                         augT[32 * r:32 * r + 32, g % 2, :]).then_inc(aug_loaded[g], 16)
                    for f in (0, 1):
                        k = {1: 0, 2: 1, 3: 2}.get(stop_after, 3)
                        sp.wait_ge(resid[k], 2 * f + 2)
                        sp.dma_start(ov[:, 4 * f:4 * f + 4, :], xres[:, 4 * f:4 * f + 4, :]).then_inc(stored, 16)
                    sp.wait_ge(stored, 32)

                @block.gpsimd
                def _(pool):
                    pool.memset(vp[:, :, :, DH:2 * DH], 0.0).then_inc(arena_set, 1)
                    pool.wait_ge(arena_set, 1)
                    pool.memset(vp[:, :, :, DH:DH + 1], 1.0).then_inc(arena_set, 1)
                    pool.wait_ge(arena_set, 2)
                    pool.memset(kst[AUG:AUG + 3, :, :], 1.0).then_inc(arena_set, 1)
                    pool.wait_ge(arena_set, 3)

                    def ln_scale(k, f):
                        pool.wait_ge(ln_aggr[k], 4 * f + 4)
                        v = mv[:, 4 * f:4 * f + 4, 1:2].rearrange("p i a -> p (i a)")
                        pool.tensor_scalar(v, v, 1e-5, 1.0, ALU.add, ALU.mult).then_inc(ln_eps[k], 1)
                        pool.wait_ge(ln_eps[k], f + 1)
                        pool.tensor_tensor(rstd[:, 4 * f:4 * f + 4], v, half_neg[:, 0:4], ALU.pow).then_inc(ln_rstd[k], 1)

                    ln_scale(0, 0)
                    ln_scale(0, 1)
                    for e in range(8):
                        m, q, f = e // 4, e // 2 % 2, e % 2
                        pool.wait_ge(mid_done, e + 1)
                        cols = slice(HALF * f, HALF * f + HALF)
                        pool.tensor_tensor(spl[:, m, q, 2, cols].rearrange("p (a n) -> p a n", a=2), ta[e % 2],
                                           spl[:, m, q, 1, cols].rearrange("p (a n) -> p a n", a=2),
                                           ALU.subtract).then_inc(lo_done, 1)
                    for n in range(2 * NG):
                        g, f = n // 2, n % 2
                        wait_emptied(pool, "den", n)
                        a = attn[:, 4 * f:4 * f + 4, g, :]
                        pool.tensor_tensor(a, a, rden[:, f, :].rearrange("p (i t) -> p i t", i=4),
                                           ALU.mult).then_inc(attn_normed, 1)
                    ln_scale(1, 0)
                    ln_scale(1, 1)
                    ln_scale(2, 0)
                    ln_scale(2, 1)
                    pool.memset(qd[0:64, :, 1, :], 0.0).then_inc(qd_zeroed, 1)
                    pool.wait_ge(qd_zeroed, 1)
                    pool.memset(qd[64:128, :, 0, :], 0.0).then_inc(qd_zeroed, 1)
                    pool.wait_ge(qd_zeroed, 2)
                    for n in range(4 * NMIX):
                        c, f = n % 2, n // 2 % 2
                        wait_emptied(pool, "mix", n)
                        a = xf[:, n // 4 % 2, c, HALF * f:HALF * f + HALF]
                        pool.tensor_tensor(a, a, xT[:, c, 1 + HALF * f:1 + HALF * f + HALF], ALU.add).then_inc(mix_added, 1)
                    wait_emptied(pool, "w", 3)
                    src, at_, n = wdec, 0, 512
                    for l in range(LEVELS):
                        if l:
                            pool.wait_ge(tot_done, l)
                        dst = tot[:, :, at_:at_ + n]
                        s2 = src.rearrange("p c (n a) -> p c n a", a=2)
                        pool.tensor_tensor(dst, s2[:, :, :, 0], s2[:, :, :, 1], ALU.mult).then_inc(tot_done, 1)
                        src, at_, n = dst, at_ + n, n // 2
                    wait_filled(pool, "vb", 3)
                    pool.memset(A, 0.0).then_inc(a_zeroed, 1)
                    pool.memset(S[:, :, 0, :], 0.0).then_inc(s_zeroed, 1)
                    for l in range(LEVELS):
                        m = 1 << l
                        tm = wdec if l == 0 else tot[:, :, 1024 - 1024 // (m // 2) // 1:1024 - 1024 // m // 1 + 0]
                        for c in range(NC):
                            wait_filled(pool, "level", 4 * l + 2 * c + 1)
                            kv = kk[:, c, :].rearrange("p (n a m) -> p n a m", a=2, m=m)[:, :, 0, :]
                            w = tm[:, c, :].rearrange("p (n a) -> p n a", a=2)[:, :, 1:2].broadcast_to([128, 512 // m, m])
                            if l:
                                pool.wait_ge(k_updated, 2 * (l - 1) + c + 1)
                            pool.tensor_tensor(kv, kv, w, ALU.mult).then_inc(k_updated, 1)
                    for n in range(4):
                        pool.wait_ge(gn_aggr, 8 * n + 8)
                        v = gmv[:, n % 2, :, 1:2].rearrange("p i a -> p (i a)")
                        pool.tensor_scalar(v, v, 0.00064, 1.0, ALU.add, ALU.mult).then_inc(gn_eps, 1)
                        pool.wait_ge(gn_eps, n + 1)
                        pool.tensor_tensor(grs[:, n % 2, :], v, half_neg[:, :], ALU.pow).then_inc(gn_rstd, 1)
                        pool.wait_ge(gn_rstd, n + 1)
                        pool.wait_ge(gn_lng, n + 1)
                        z = xn[:, 2 * n:2 * n + 2, :]
                        zh = z.rearrange("p i (h j) -> p i h j", j=WH)
                        r = grs[:, n % 2, :].rearrange("p (i h a) -> p i h a", i=2, a=1).broadcast_to([128, 2, 4, WH])
                        pool.tensor_tensor(zh, zh, r, ALU.mult).then_inc(gn_chain, 1)
                        pool.wait_ge(gn_chain, 3 * n + 1)
                        pool.tensor_tensor(z, z, lng[:, 1:2, :].broadcast_to([128, 2, D]), ALU.add).then_inc(gn_chain, 1)
                        pool.wait_ge(gn_chain, 3 * n + 2)
                        pool.tensor_tensor(z, z, gt[:, 2 * n:2 * n + 2, :], ALU.mult).then_inc(gn_chain, 1)
                    ln_scale(3, 0)
                    ln_scale(3, 1)

                @block.scalar
                def _(act):
                    def copy_xT(k):
                        for n in range(4):
                            f, c = n // 2, n % 2
                            wait_filled(act, f"ln{k}", n)
                            act.activation(xT[:, c, 1 + HALF * f:1 + HALF * f + HALF], bank(f"ln{k}", n)[:, :],
                                           ACT.Copy).then_inc(act_emptied, 1)

                    copy_xT(0)

                    def mid(e):
                        act.wait_ge(rem_done, e + 1)
                        m, q, f = e // 4, e // 2 % 2, e % 2
                        act.activation(spl[:, m, q, 1, HALF * f:HALF * f + HALF].rearrange("p (a n) -> p a n", a=2),
                                       ta[e % 2], ACT.Copy).then_inc(mid_done, 1)

                    for e in range(8):
                        m, q, f = e // 4, e // 2 % 2, e % 2
                        act.wait_ge(roped, e + 1)
                        act.activation(spl[:, m, q, 0, HALF * f:HALF * f + HALF].rearrange("p (a n) -> p a n", a=2),
                                       ta[e % 2], ACT.Copy).then_inc(hi_done, 1)
                        if e:
                            mid(e - 1)
                    mid(7)
                    act.wait_ge(arena_set, 2)
                    for n in range(4):
                        wait_filled(act, "v", n)
                        act.activation(vp[:, 2 * n:2 * n + 2, :, 0:DH],
                                       bank("v", n)[:, :].rearrange("p (i h d) -> p i h d", i=2, h=NH),
                                       ACT.Copy).then_inc(act_emptied, 1)
                    for g in range(NG):
                        for k in range(NPC):
                            u, h = k // HG, k % HG
                            j, f = UNITS[u]
                            n = HALF * (f + 1) - max(HALF * f, 128 * j)
                            U = g * len(UNITS) + u
                            wait_filled(act, "score", g * NPC + k)
                            if h == 0 and U >= 3:
                                act.wait_ge(pv_units, U - 2)
                            if U == 0 and h == 0:
                                act.wait_ge(stacked[1], 2 * 48 * 16)
                            act.activation(pt[:, U % 3, h, 0:n], bank("score", g * NPC + k)[:, 0:n], ACT.Exp,
                                           scale=DH ** -0.5).then_inc(act_emptied, 1)
                        act.wait_ge(pv_units, (g + 1) * len(UNITS))
                        for f in (0, 1):
                            act.activation(attn[:, 4 * f:4 * f + 4, g, :],
                                           PB[6 + f][:, :].rearrange("p (i t) -> p i t", i=4),
                                           ACT.Copy).then_inc(pv_copied, 1)

                    def ffn(k, s):
                        copy_xT(k)
                        for e in range(2 * NM):
                            wait_filled(act, f"gu{k}", 2 * e)
                            if e >= 2:
                                act.wait_ge(gate_done[s], e - 1)
                            act.activation(tb[:, e % 2, :], bank(f"gu{k}", 2 * e)[:, :], ACT.Tanh,
                                           scale=0.5 * S8).then_inc(tanh_done[s], 1)

                    ffn(1, 0)
                    copy_xT(2)
                    for n in range(4):
                        l, f = n % 2, n // 2
                        wait_filled(act, "lora", n)
                        act.activation(lora[:, l, HALF * f:HALF * f + HALF], bank("lora", n)[:, :],
                                       ACT.Tanh).then_inc(act_emptied, 1)
                    for kind, r in (("dech", 64), ("gateh", 0)):
                        for f in (0, 1):
                            wait_filled(act, kind, f)
                            act.activation(th[r:r + 64, HALF * f:HALF * f + HALF], bank(kind, f)[r:r + 64, :],
                                           ACT.Tanh).then_inc(act_emptied, 1)
                    for n in range(4):
                        c, f = n % 2, n // 2
                        w = wdec[:, c, HALF * f:HALF * f + HALF]
                        wait_filled(act, "w", n)
                        act.activation(w, bank("w", n)[:, :], ACT.Exp, bias=vec[:, 6, c:c + 1]).then_inc(decay_exp, 1)
                        act.wait_ge(decay_exp, n + 1)
                        act.activation(w, w, ACT.Exp, scale=-1.0).then_inc(act_emptied, 1)
                    act.wait_ge(qd_zeroed, 2)
                    for n in range(4):
                        c, f = n % 2, n // 2
                        wait_filled(act, "r", n)
                        act.activation(qd[0:64, c, 0, HALF * f:HALF * f + HALF], bank("r", n)[0:64, :], ACT.Copy)
                        act.activation(qd[64:128, c, 1, HALF * f:HALF * f + HALF], bank("r", n)[64:128, :],
                                       ACT.Copy).then_inc(act_emptied, 1)
                    for n in range(4):
                        wait_filled(act, "g", n)
                        act.activation(gt[:, 2 * n:2 * n + 2, :], bank("g", n)[:, :].rearrange("p (i n) -> p i n", i=2),
                                       ACT.Copy).then_inc(act_emptied, 1)
                    for n in range(4):
                        c, f = n % 2, n // 2
                        wait_filled(act, "k", n)
                        act.activation(kk[:, c, HALF * f:HALF * f + HALF], bank("k", n)[:, :],
                                       ACT.Copy).then_inc(act_emptied, 1)
                    for n in range(4):
                        wait_filled(act, "vb", n)
                        act.activation(vt[:, 2 * n:2 * n + 2, :], bank("vb", n)[:, :].rearrange("p (i n) -> p i n", i=2),
                                       ACT.Copy).then_inc(act_emptied, 1)
                    for n in range(4):
                        wait_filled(act, "kt", n)
                        act.activation(kn[:, n // 2, 4 * (n % 2):4 * (n % 2) + 4, :],
                                       bank("kt", n)[:, :].rearrange("p (n i) -> p n i", n=4),
                                       ACT.Copy).then_inc(act_emptied, 1)
                    for n in range(4):
                        f, c = n // 2, n % 2
                        wait_filled(act, "zt", n)
                        act.activation(zT[:, c, HALF * f:HALF * f + HALF], bank("zt", n)[:, :],
                                       ACT.Copy).then_inc(act_emptied, 1)
                    ffn(3, 1)

                @block.vector
                def _(dve):
                    def ln_tile(k, i):
                        dve.bn_stats(stats[:, i, :], xres[:, i, :]).then_inc(ln_stat[k], 1)

                    def ln_half(k, f):
                        dve.wait_ge(ln_stat[k], 4 * f + 4)
                        for i in range(4 * f, 4 * f + 4):
                            dve.bn_aggr(mv[:, i, :], stats[:, i, :]).then_inc(ln_aggr[k], 1)
                        dve.wait_ge(ln_aggr[k], 4 * f + 4)
                        dve.wait_ge(ln_rstd[k], f + 1)
                        for i in range(4 * f, 4 * f + 4):
                            dve.tensor_scalar(xn[:, i, :], xres[:, i, :], mv[:, i, 0:1], rstd[:, i:i + 1],
                                              ALU.subtract, ALU.mult).then_inc(ln_out[k], 1)

                    def residual(kind, n, s, scale=None):
                        wait_filled(dve, kind, n)
                        a = xres[:, 2 * n:2 * n + 2, :].rearrange("p i c -> p (i c)")
                        if scale is None:
                            dve.tensor_tensor(a, bank(kind, n)[:, :], a, ALU.add).then_inc(dve_emptied, 1)
                        else:
                            dve.scalar_tensor_tensor(out=a, in0=bank(kind, n)[:, :], scalar=scale, in1=a,
                                                     op0=ALU.mult, op1=ALU.add).then_inc(dve_emptied, 1)
                        dve.wait_ge(dve_emptied, RANK[NTH[kind, n]])
                        dve.engine_nop().then_inc(resid[s], 1)
                        if s < 3:
                            ln_tile(s + 1, 2 * n)
                            ln_tile(s + 1, 2 * n + 1)
                            if n % 2:
                                ln_half(s + 1, n // 2)

                    for f in (0, 1):
                        dve.wait_ge(x_loaded[f], 16)
                        for i in range(4 * f, 4 * f + 4):
                            ln_tile(0, i)
                        ln_half(0, f)

                    def rem(e):
                        m, q, f = e // 4, e // 2 % 2, e % 2
                        dve.wait_ge(hi_done, e + 1)
                        dve.tensor_tensor(ta[e % 2], ta[e % 2],
                                          spl[:, m, q, 0, HALF * f:HALF * f + HALF].rearrange("p (a n) -> p a n", a=2),
                                          ALU.subtract).then_inc(rem_done, 1)

                    for e in range(8):
                        f = e % 2
                        if e >= 2:
                            dve.wait_ge(lo_done, e - 1)
                        for r in (0, 1):
                            wait_filled(dve, "qk", 2 * e + r)
                            dve.tensor_tensor(ta[2 * r + e % 2],
                                              bank("qk", 2 * e + r)[:, :].rearrange("p (a n) -> p a n", a=2),
                                              rope[:, r, HALF * f:HALF * f + HALF].rearrange("p (a n) -> p a n", a=2),
                                              ALU.mult).then_inc(dve_emptied, 1)
                        dve.wait_ge(dve_emptied, RANK[NTH["qk", 2 * e + 1]])
                        dve.tensor_tensor(ta[e % 2], ta[e % 2], ta[2 + e % 2], ALU.add).then_inc(roped, 1)
                        if e:
                            rem(e - 1)
                    rem(7)

                    def max_piece(g, k):
                        h, (i, s0, n, col) = k // len(PIECES), PIECES[k % len(PIECES)]
                        wait_filled(dve, "max", g * NPC + k)
                        dve.reduce_max(mxp[:, g % 2, h, col:col + 1], bank("max", g * NPC + k)[:, 0:n],
                                       axis=AX.X).then_inc(dve_emptied, 1)

                    def den(n):
                        wait_filled(dve, "den", n)
                        if n >= 2:
                            dve.wait_ge(attn_normed, n - 1)
                        dve.reciprocal(rden[:, n % 2, :], bank("den", n)[:, :]).then_inc(dve_emptied, 1)

                    for g in range(NG):
                        for k in range(NPC):
                            max_piece(g, k)
                            if g >= 2 and k == 5:
                                den(2 * (g - 2))
                                den(2 * (g - 2) + 1)
                        dve.wait_ge(dve_emptied, RANK[NTH["max", g * NPC + NPC - 1]])
                        mg, af = mxp[:, g % 2, :, :], augf[:, :].rearrange("p (h i) -> p h i", h=HG)
                        dve.tensor_tensor(mg[:, :, 4:8], mg[:, :, 4:8], mg[:, :, 8:12], ALU.max).then_inc(aug_chain, 1)
                        dve.wait_ge(aug_chain, 6 * g + 1)
                        dve.tensor_scalar(aug[:, 0, :, :], mg[:, :, 0:8], -1.0, None, ALU.mult).then_inc(aug_chain, 1)
                        dve.wait_ge(aug_chain, 6 * g + 2)
                        dve.scalar_tensor_tensor(out=af, in0=mg[:, :, 0:8], scalar=-1.0, in1=aug[:, 0, :, :],
                                                 op0=ALU.mult, op1=ALU.subtract).then_inc(aug_chain, 1)
                        dve.wait_ge(aug_chain, 6 * g + 3)
                        dve.tensor_copy(aug[:, 1, :, :], af).then_inc(aug_chain, 1)
                        dve.wait_ge(aug_chain, 6 * g + 4)
                        dve.tensor_tensor(af, af, aug[:, 1, :, :], ALU.subtract).then_inc(aug_chain, 1)
                        dve.wait_ge(aug_chain, 6 * g + 5)
                        dve.tensor_copy(aug[:, 2, :, :], af).then_inc(aug_chain, 1)
                        wait_filled(dve, "aug", g)
                        if g >= 2:
                            dve.wait_ge(aug_loaded[g - 2], 48)
                        dve.tensor_copy(augT[:, g % 2, :], bank("aug", g)[0:96, 0:64].bitcast(bf16)).then_inc(dve_emptied, 1)
                    den(2 * (NG - 2))
                    den(2 * (NG - 2) + 1)
                    den(2 * (NG - 1))
                    den(2 * (NG - 1) + 1)
                    for n in range(4):
                        residual("o", n, 0)

                    def ffn(k, s):
                        def down(n):
                            residual(f"dn{k}", n, k, 0.5 * S8 * S8 * S8)
                        for e in range(2 * NM):
                            f, m = e // NM, e % NM
                            u = ub[:, e % 2, :]
                            dve.wait_ge(tanh_done[s], e + 1)
                            dve.scalar_tensor_tensor(out=u, in0=tb[:, e % 2, :], scalar=1.0,
                                                     in1=bank(f"gu{k}", 2 * e)[:, :], op0=ALU.add,
                                                     op1=ALU.mult).then_inc(dve_emptied, 1)
                            wait_filled(dve, f"gu{k}", 2 * e + 1)
                            dve.wait_ge(dve_emptied, RANK[NTH[f"gu{k}", 2 * e]])
                            dve.tensor_tensor(hT[:, m, HALF * f:HALF * f + HALF], bank(f"gu{k}", 2 * e + 1)[:, :], u,
                                              ALU.mult).then_inc(dve_emptied, 1)
                            dve.wait_ge(dve_emptied, RANK[NTH[f"gu{k}", 2 * e + 1]])
                            dve.engine_nop().then_inc(gate_done[s], 1)
                            if e in (NM + 1, NM + 3):
                                down((e - NM) // 2)
                        down(2)
                        down(3)

                    ffn(1, 0)
                    for n in range(4):
                        f, c = n // 2, n % 2
                        cols = slice(HALF * f, HALF * f + HALF)
                        now = xT[:, c, 1 + HALF * f:1 + HALF * f + HALF]
                        wait_emptied(dve, "ln2", n)
                        dve.tensor_tensor(xx[:, c, cols], xT[:, c, cols], now, ALU.subtract).then_inc(xx_done, 1)
                        dve.wait_ge(xx_done, n + 1)
                        dve.scalar_tensor_tensor(out=xxx[:, c, cols], in0=xx[:, c, cols], scalar=vec[:, 0, c:c + 1],
                                                 in1=now, op0=ALU.mult, op1=ALU.add).then_inc(xxx_done, 1)
                    for n in range(4 * NMIX):
                        mi, f, c = n // 4, n // 2 % 2, n % 2
                        cols = slice(HALF * f, HALF * f + HALF)
                        if mi == 2:
                            wait_filled(dve, "dech", 1)
                        if mi == 3:
                            wait_filled(dve, "gateh", 1)
                        if mi == 4:
                            wait_filled(dve, "r", 3)
                        wait_filled(dve, "mix", n)
                        fi = MIX_ORDER[mi]
                        dve.scalar_tensor_tensor(out=xf[:, mi % 2, c, cols], in0=bank("mix", n)[:, :],
                                                 scalar=vec[:, 1 + fi, c:c + 1], in1=xx[:, c, cols],
                                                 op0=ALU.add, op1=ALU.mult).then_inc(dve_emptied, 1)
                    for c in range(NC):
                        wait_emptied(dve, "k", 2 + c)
                        dve.tensor_scalar(ku[:, c, :], kk[:, c, :], vec[:, 7, c:c + 1], None, ALU.mult).then_inc(ku_done, 1)
                    dve.wait_ge(a_zeroed, 1)
                    for n in range(8):
                        c, q = n // 4, n % 4
                        wait_filled(dve, "diag", n)
                        a = A[:, c, 2 * q:2 * q + 2, :, :].rearrange("p n h t -> p (n h) t")
                        dve.copy_predicated(a, dmask[:, :].rearrange("p (a t) -> p a t", a=1).broadcast_to([128, 4, 128]),
                                            bank("diag", n)[:, :].rearrange("p (a t) -> p a t", a=4)).then_inc(dve_emptied, 1)
                    dve.wait_ge(tot_done, LEVELS)
                    for l in range(LEVELS):
                        m = 1 << l
                        tm = wdec if l == 0 else tot[:, :, 1024 - 1024 // (m // 2):1024 - 1024 // m]
                        for c in range(NC):
                            for q in (0, 1):
                                n = 4 * l + 2 * c + q
                                wait_filled(dve, "level", n)
                                dve.wait_ge(dve_emptied, RANK[NTH["level", n - 4] if l else NTH["diag", 7]])
                                a = A[:, c, 4 * q:4 * q + 4, :, :].rearrange("p n h (b s m) -> p (n h) b s m", s=2, m=m)[:, :, :, 1, :]
                                mk = lmask[:, l:l + 1, :].broadcast_to([128, 8, 64]).rearrange("p a (b m) -> p a b m", m=m)
                                dve.copy_predicated(a, mk, bank("level", n)[:, :].rearrange("p (a b m) -> p a b m", a=8, m=m)
                                                    ).then_inc(dve_emptied, 1)
                            for h in (0, 1):
                                p = slice(64 * h, 64 * h + 64)
                                qv = qd[p, c, h, :].rearrange("p (n s m) -> p n s m", s=2, m=m)[:, :, 1, :]
                                w = tm[p, c, :].rearrange("p (n s) -> p n s", s=2)[:, :, 0:1].broadcast_to([64, 512 // m, m])
                                if l:
                                    dve.wait_ge(q_updated, 4 * (l - 1) + 2 * c + h + 1)
                                dve.tensor_tensor(qv, qv, w, ALU.mult).then_inc(q_updated, 1)
                    dve.wait_ge(s_zeroed, 1)
                    steps = 0
                    for c in range(NC):
                        for ch in range(NT - 1):
                            n = 2 * c + ch // 4
                            if ch % 4 == 0:
                                wait_filled(dve, "kv", n)
                            last = None
                            for h in (0, 1):
                                p = slice(64 * h, 64 * h + 64)
                                kv = bank("kv", n)[p, 128 * (ch % 4) + 64 * h:128 * (ch % 4) + 64 * h + 64]
                                last = dve.scalar_tensor_tensor(out=S[p, c, ch + 1, :], in0=S[p, c, ch, :],
                                                                scalar=tot[p, c, 1008 + ch:1009 + ch], in1=kv,
                                                                op0=ALU.mult, op1=ALU.add)
                                last.then_inc(s_chain, 1)
                            steps += 2
                            dve.wait_ge(s_chain, steps)
                            if ch in (3, NT - 2):
                                dve.engine_nop().then_inc(dve_emptied, 1)
                    for n in range(4):
                        wait_filled(dve, "y", n)
                        if n >= 2:
                            dve.wait_ge(gn_chain, 3 * (n - 2) + 1)
                        ps = bank("y", n)[:, :].rearrange("p (a j) -> p a j", j=WH)
                        for a in range(8):
                            dve.bn_stats(gst[:, a, :], ps[:, a, :]).then_inc(gn_stat, 1)
                        dve.wait_ge(gn_stat, 8 * n + 8)
                        for a in range(8):
                            dve.bn_aggr(gmv[:, n % 2, a, :], gst[:, a, :]).then_inc(gn_aggr, 1)
                        dve.wait_ge(gn_aggr, 8 * n + 8)
                        z = xn[:, 2 * n:2 * n + 2, :]
                        dve.tensor_tensor(z.rearrange("p i (h j) -> p i h j", j=WH),
                                          bank("y", n)[:, :].rearrange("p (i h j) -> p i h j", i=2, j=WH),
                                          gmv[:, n % 2, :, 0:1].rearrange("p (i h) a -> p i h a", i=2).broadcast_to([128, 2, 4, WH]),
                                          ALU.subtract).then_inc(dve_emptied, 1)
                        dve.wait_ge(dve_emptied, RANK[NTH["y", n]])
                        dve.tensor_tensor(z, z, lng[:, 0:1, :].broadcast_to([128, 2, D]), ALU.mult).then_inc(gn_lng, 1)
                    for n in range(4):
                        residual("ob", n, 2)
                    ffn(3, 1)

                @block.tensor
                def _(pe):
                    mm = pe.matmul

                    def transpose_x(k):
                        for n in range(4):
                            f, c = n // 2, n % 2
                            wait_bank(pe, f"ln{k}", n)
                            for j in range(4):
                                i = 4 * f + j
                                pe.wait_ge(ln_out[k], i + 1)
                                last = pe.transpose(bank(f"ln{k}", n)[:, 128 * j:128 * j + 128],
                                                    xn[:, i, 128 * c:128 * c + 128], ident[:, :])
                            last.then_inc(filled, 1)

                    def xcols(c, f):
                        return xT[:, c, 1 + HALF * f:1 + HALF * f + HALF]

                    def xtile(c, i):
                        return xT[:, c, 1 + 128 * i:1 + 128 * i + 128]

                    transpose_x(0)
                    for e in range(8):
                        m, q, f = e // 4, e // 2 % 2, e % 2
                        wait_emptied(pe, "ln0", 2 * f + 1)
                        for r in (0, 1):
                            n = 2 * e + r
                            wait_bank(pe, "qk", n)
                            w0 = D * (2 * q + r) + 128 * m
                            for c in range(NC):
                                last = mm(bank("qk", n)[:, :], wqkv[:, c, w0:w0 + 128], xcols(c, f),
                                          start=(c == 0), stop=(c == NC - 1))
                            last.then_inc(filled, 1)

                    def v_item(n):
                        wait_bank(pe, "v", n)
                        for a in (0, 1):
                            for c in range(NC):
                                last = mm(bank("v", n)[:, D * a:D * a + D], xtile(c, 2 * n + a), wqkv[:, c, 4 * D:5 * D],
                                          start=(c == 0), stop=(c == NC - 1))
                        last.then_inc(filled, 1)

                    def max_item(g, k):
                        h, (i, s0, n, col) = g * HG + k // len(PIECES), PIECES[k % len(PIECES)]
                        wait_bank(pe, "max", g * NPC + k)
                        ps = bank("max", g * NPC + k)
                        diag = s0 + n == 128 * (i + 1)
                        last = mm(ps[:, 0:n], qst[0:AUG, h, 128 * i:128 * i + 128], kst[0:AUG, h, s0:s0 + n],
                                  start=True, stop=not diag)
                        if diag:
                            last = mm(ps[:, n - 128:n], identb[:, :], causal[:, 0, :], start=False, stop=True)
                        last.then_inc(filled, 1)

                    def score_item(g, k):
                        u, h = k // HG, g * HG + k % HG
                        j, f = UNITS[u]
                        t0 = max(HALF * f, 128 * j)
                        n = HALF * (f + 1) - t0
                        wait_bank(pe, "score", g * NPC + k)
                        ps = bank("score", g * NPC + k)
                        diag = t0 == 128 * j
                        last = mm(ps[:, 0:n], kst[0:AUG + 3, h, 128 * j:128 * j + 128], qst[0:AUG + 3, h, t0:t0 + n],
                                  start=True, stop=not diag)
                        if diag:
                            last = mm(ps[:, 0:128], identb[:, :], causal[:, 1, :], start=False, stop=True)
                        last.then_inc(filled, 1)

                    def pv(g, u):
                        j, f = UNITS[u]
                        t0 = max(HALF * f, 128 * j)
                        n = HALF * (f + 1) - t0
                        U = g * len(UNITS) + u
                        wait_emptied(pe, "score", g * NPC + HG * u + HG - 1)
                        if j == 0 and g:
                            pe.wait_ge(pv_copied, 2 * g)
                        for h in range(HG):
                            last = mm(PB[6 + f][32 * h:32 * h + 32, t0 - HALF * f:HALF], vp[:, j, g * HG + h, :],
                                      pt[:, U % 3, h, 0:n], start=(j == 0), stop=(j == 4 * f + 3))
                        last.then_inc(pv_units, 1)

                    def den_item(n):
                        pe.wait_ge(pv_copied, n + 1)
                        wait_bank(pe, "den", n)
                        mm(bank("den", n)[:, :].rearrange("p (i t) -> p i t", i=4), denrow[:, :],
                           attn[:, 4 * (n % 2):4 * (n % 2) + 4, n // 2, :], start=True, stop=True).then_inc(filled, 1)

                    pe.wait_ge(arena_set, 3)
                    for s in range(NG + 1):
                        if s in (0, 2):
                            pe.wait_ge(stacked[s // 2], 2 * 48 * 16)
                        if s >= 1:
                            pe.wait_ge(aug_loaded[s - 1], 48)
                        for k in range(NPC + LAG):
                            if s < NG and k < NPC:
                                max_item(s, k)
                            if s == 0 and k < 24 and k % 6 == 5:
                                v_item(k // 6)
                            if s >= 2 and k == 5:
                                den_item(2 * (s - 2))
                                den_item(2 * (s - 2) + 1)
                            if s >= 1 and k >= LAG:
                                score_item(s - 1, k - LAG)
                                if (k - LAG) % HG == HG - 1 and (k - LAG) // HG >= 2:
                                    pv(s - 1, (k - LAG) // HG - 2)
                        if s >= 1:
                            pv(s - 1, len(UNITS) - 2)
                            pv(s - 1, len(UNITS) - 1)
                        if s < NG:
                            pe.wait_ge(aug_chain, 6 * s + 6)
                            wait_bank(pe, "aug", s)
                            pe.transpose(bank("aug", s)[0:96, 0:64].bitcast(bf16),
                                         aug[:, :, :, :].rearrange("p r h i -> p (r h i)"), identb[:, :]).then_inc(filled, 1)
                    den_item(2 * (NG - 1))
                    den_item(2 * (NG - 1) + 1)
                    for n in range(4):
                        if n == 0:
                            pe.wait_ge(attn_normed, 2 * NG)
                        wait_bank(pe, "o", n)
                        for a in (0, 1):
                            for g in range(NG):
                                last = mm(bank("o", n)[:, D * a:D * a + D], attn[:, 2 * n + a, g, :], wo[:, g, :],
                                          start=(g == 0), stop=(g == NG - 1))
                        last.then_inc(filled, 1)

                    def ffn(k):
                        def down(n):
                            if n % 2 == 0:
                                wait_emptied(pe, f"gu{k}", 2 * NM * (n // 2) + 2 * NM - 1)
                            wait_bank(pe, f"dn{k}", n)
                            for a in (0, 1):
                                for m in range(NM):
                                    i = 2 * n + a
                                    last = mm(bank(f"dn{k}", n)[:, D * a:D * a + D], hT[:, m, 128 * i:128 * i + 128],
                                              wd[:, m, :], start=(m == 0), stop=(m == NM - 1))
                            last.then_inc(filled, 1)

                        transpose_x(k)
                        for f in (0, 1):
                            wait_emptied(pe, f"ln{k}", 2 * f + 1)
                            for e in range(2 * NM):
                                m, r = e // 2, e % 2
                                wait_bank(pe, f"gu{k}", 2 * NM * f + e)
                                for c in range(NC):
                                    last = mm(bank(f"gu{k}", 2 * NM * f + e)[:, :],
                                              wgu[:, c, HID * r + 128 * m:HID * r + 128 * m + 128], xcols(c, f),
                                              start=(c == 0), stop=(c == NC - 1))
                                last.then_inc(filled, 1)
                                if f == 1 and e in (3, 7):
                                    down(e // 4)
                        down(2)
                        down(3)

                    ffn(1)
                    transpose_x(2)
                    for n in range(4):
                        l, f = n % 2, n // 2
                        pe.wait_ge(xxx_done, 2 * f + 2)
                        wait_bank(pe, "lora", n)
                        for c in range(NC):
                            last = mm(bank("lora", n)[:, :], mw1[:, c, 32 * l:32 * l + 128],
                                      xxx[:, c, HALF * f:HALF * f + HALF], start=(c == 0), stop=(c == NC - 1))
                        last.then_inc(filled, 1)

                    def hidden(kind, r, w0, slot, n0):
                        for f in (0, 1):
                            pe.wait_ge(mix_added, 4 * n0 + 2 * f + 2)
                            wait_bank(pe, kind, f)
                            for c in range(NC):
                                last = mm(bank(kind, f)[r:r + 64, :], low1[:, c, w0:w0 + DLOW],
                                          xf[:, slot, c, HALF * f:HALF * f + HALF], start=(c == 0), stop=(c == NC - 1))
                            last.then_inc(filled, 1)

                    def channel_major(kind, w0, slot, n0):
                        for n in range(4):
                            co, f = n % 2, n // 2
                            pe.wait_ge(mix_added, 4 * n0 + 2 * f + 2)
                            wait_bank(pe, kind, n)
                            for c in range(NC):
                                last = mm(bank(kind, n)[:, :], bm[:, c, w0 + 128 * co:w0 + 128 * co + 128],
                                          xf[:, slot, c, HALF * f:HALF * f + HALF], start=(c == 0), stop=(c == NC - 1))
                            last.then_inc(filled, 1)

                    for mi in range(NMIX):
                        fi = MIX_ORDER[mi]
                        for q in range(4):
                            n, f, co = 4 * mi + q, q // 2, q % 2
                            wait_emptied(pe, "lora", 2 * f + 1)
                            wait_bank(pe, "mix", n)
                            mm(bank("mix", n)[:, :], mw2[:, fi, 128 * co:128 * co + 128],
                               lora[:, fi // 4, HALF * f:HALF * f + HALF], start=True, stop=True).then_inc(filled, 1)
                        if mi == 1:
                            hidden("dech", 64, DLOW, 0, 0)
                        if mi == 2:
                            hidden("gateh", 0, 0, 1, 1)
                        if mi == 3:
                            for n in range(4):
                                co, f = n % 2, n // 2
                                wait_emptied(pe, "gateh", f)
                                wait_bank(pe, "w", n)
                                mm(bank("w", n)[:, :], low2[:, 1, 128 * co:128 * co + 128],
                                   th[:, HALF * f:HALF * f + HALF], start=True, stop=True).then_inc(filled, 1)
                            channel_major("r", 0, 0, 2)
                        if mi == 4:
                            for n in range(4):
                                wait_bank(pe, "g", n)
                                for a in (0, 1):
                                    last = mm(bank("g", n)[:, D * a:D * a + D], th[:, 128 * (2 * n + a):128 * (2 * n + a) + 128],
                                              low2[:, 0, :], start=True, stop=True)
                                last.then_inc(filled, 1)
                            channel_major("k", D, 1, 3)
                            for n in range(4):
                                pe.wait_ge(mix_added, 16 + 2 * (n // 2) + 2)
                                wait_bank(pe, "vb", n)
                                for a in (0, 1):
                                    i = 2 * n + a
                                    for c in range(NC):
                                        last = mm(bank("vb", n)[:, D * a:D * a + D], xf[:, 0, c, 128 * i:128 * i + 128],
                                                  bm[:, c, 2 * D:3 * D], start=(c == 0), stop=(c == NC - 1))
                                last.then_inc(filled, 1)
                    wait_emptied(pe, "r", 3)
                    for n in range(8):
                        c, q = n // 4, n % 4
                        pe.wait_ge(ku_done, c + 1)
                        wait_bank(pe, "diag", n)
                        for a in (0, 1):
                            ch = 2 * q + a
                            last = mm(bank("diag", n)[:, 256 * a:256 * a + 256].rearrange("p (h t) -> p h t", h=2),
                                      ku[:, c, 128 * ch:128 * ch + 128], qd[:, c, :, 128 * ch:128 * ch + 128],
                                      start=True, stop=True)
                        last.then_inc(filled, 1)
                    for l in range(LEVELS):
                        m = 1 << l
                        for c in range(NC):
                            for q in (0, 1):
                                n = 4 * l + 2 * c + q
                                if l:
                                    pe.wait_ge(q_updated, 4 * (l - 1) + 2 * c + 2)
                                    pe.wait_ge(k_updated, 2 * (l - 1) + c + 1)
                                wait_bank(pe, "level", n)
                                for a in range(4):
                                    ch = 4 * q + a
                                    rhs = qd[:, c, :, 128 * ch:128 * ch + 128].rearrange("p h (b s m) -> p h b s m", s=2, m=m)[:, :, :, 1, :]
                                    last = mm(bank("level", n)[:, 128 * a:128 * a + 128].rearrange("p (h b m) -> p h b m", h=2, m=m),
                                              kk[:, c, 128 * ch:128 * ch + 128], rhs, start=True, stop=True)
                                last.then_inc(filled, 1)
                    for n in range(4):
                        c = n // 2
                        pe.wait_ge(k_updated, 2 * (LEVELS - 1) + c + 1)
                        wait_bank(pe, "kt", n)
                        for a in range(4):
                            ch = 4 * (n % 2) + a
                            last = pe.transpose(bank("kt", n)[:, 128 * a:128 * a + 128], kk[:, c, 128 * ch:128 * ch + 128],
                                                ident[:, :])
                        last.then_inc(filled, 1)
                    for n in range(4):
                        c = n // 2
                        wait_emptied(pe, "kt", n)
                        wait_bank(pe, "kv", n)
                        for a in range(4 if n % 2 == 0 else 3):
                            ch = 4 * (n % 2) + a
                            last = mm(bank("kv", n)[:, 128 * a:128 * a + 128], kn[:, c, ch, :],
                                      vt[:, ch, 128 * c:128 * c + 128], start=True, stop=True)
                        last.then_inc(filled, 1)
                    wait_emptied(pe, "level", LEVELS * 4 - 1)
                    pe.wait_ge(q_updated, 4 * LEVELS)
                    wait_emptied(pe, "kv", 3)
                    for n in range(4):
                        wait_bank(pe, "y", n)
                        for a in (0, 1):
                            ch = 2 * n + a
                            for hd in range(4):
                                c, h = hd // 2, hd % 2
                                o = bank("y", n)[:, D * a + WH * hd:D * a + WH * hd + WH]
                                last = mm(o, A[:, c, ch, h, :], vt[:, ch, WH * hd:WH * hd + WH], start=True, stop=(ch == 0))
                                if ch:
                                    last = mm(o, qd[:, c, h, 128 * ch:128 * ch + 128], S[:, c, ch, :], start=False, stop=True)
                        last.then_inc(filled, 1)
                    for n in range(4):
                        f, c = n // 2, n % 2
                        pe.wait_ge(gn_chain, 6 * f + 6)
                        wait_bank(pe, "zt", n)
                        for j in range(4):
                            last = pe.transpose(bank("zt", n)[:, 128 * j:128 * j + 128],
                                                xn[:, 4 * f + j, 128 * c:128 * c + 128], ident[:, :])
                        last.then_inc(filled, 1)
                    for n in range(4):
                        wait_emptied(pe, "zt", 2 * (n // 2) + 1)
                        wait_bank(pe, "ob", n)
                        for a in (0, 1):
                            i = 2 * n + a
                            for c in range(NC):
                                last = mm(bank("ob", n)[:, D * a:D * a + D], zT[:, c, 128 * i:128 * i + 128],
                                          bm[:, c, 3 * D:4 * D], start=(c == 0), stop=(c == NC - 1))
                        last.then_inc(filled, 1)
                    ffn(3)

            nc.sync.sem_clear(range(sems[3].num, sems[-1].num + 1))
            nc.all_engine_barrier()


STOP = None


def kernel(**inputs):
    import numpy as np
    import concourse.bacc as bacc
    from concourse.bass_utils import run_bass_kernel_spmd as run

    g = {k: np.asarray(v) for k, v in inputs.items()}
    rot = np.array([DH * h + (d + DH // 2) % DH for h in range(NH) for d in range(DH)])
    arrays = {"x": g["L0_attn_a_x"]}
    wq, wk = g["L0_attn_a_Wq"], g["L0_attn_a_Wk"]
    for name, w in (("wq", wq), ("wqr", wq[rot]), ("wk", wk), ("wkr", wk[rot]), ("wv", g["L0_attn_a_Wv"]), ("wo", g["L0_attn_a_Wo"])):
        arrays[name] = w.T
    for name in ("Wr", "Wk", "Wv", "Wo", "maa_w1", "maa_w2", "gate_w1", "gate_w2", "decay_w1", "decay_w2"):
        arrays["b_" + name] = g["L0_attn_b_" + name]
    names = ("maa_x", "maa_w", "maa_k", "maa_v", "maa_r", "maa_g", "time_decay", "u")
    arrays["vec"] = np.stack([g["L0_attn_b_" + n].reshape(NC, 128) for n in names]).transpose(2, 0, 1).reshape(128, -1)
    arrays["ln_g"], arrays["ln_b"] = g["L0_attn_b_ln_g"], g["L0_attn_b_ln_b"]
    for name in ("w_gate", "w_up", "w_down"):
        arrays["f_" + name] = g["L0_ffn_" + name].T
    inv = (np.float32(1.0) / np.float32(10000.0) ** (np.arange(0, DH, 2, dtype=np.float32) / np.float32(DH))).astype(np.float32)
    ang = (np.arange(T, dtype=np.float32)[:, None] * inv[None, :]).astype(np.float32)
    cos = np.concatenate([np.cos(ang)] * 2, 1).T
    sin = np.concatenate([-np.sin(ang), np.sin(ang)], 1).T
    arrays["cos"] = np.tile(cos, (128 // DH, 1)).astype(np.float32)
    arrays["sin"] = np.tile(sin, (128 // DH, 1)).astype(np.float32)
    p, q = np.arange(128)[:, None], np.arange(128)[None, :]
    den = (p == 32 * (q // 32) + DH)
    arrays["cf"] = np.concatenate([p == q, den, np.where(q > p, NEG, 0), np.where(q < p, NEG, 0)], 1).astype(np.float32)
    masks = []
    for l in range(LEVELS):
        m = 1 << l
        t = np.array([2 * m * b + m + r for b in range(64 // m) for r in range(m)])[None, :]
        masks.append((p // (2 * m) == t // (2 * m)) & (p % (2 * m) < m))
    arrays["ci"] = np.concatenate(masks + [p == q], 1).astype(np.int32)
    arrays = {"in_" + k: np.ascontiguousarray(v) for k, v in arrays.items()}

    nc = bacc.Bacc("TRN2", target_bir_lowering=False, num_devices=1)
    d = {k: nc.dram_tensor(k, v.shape, mybir.dt.from_np(v.dtype), kind="ExternalInput").ap() for k, v in arrays.items()}
    out = nc.dram_tensor("out", (NB, T, D), mybir.dt.float32, kind="ExternalOutput").ap()
    build(nc, d["in_x"], [d["in_" + k] for k in ("wq", "wqr", "wk", "wkr", "wv", "wo")], [d["in_cos"], d["in_sin"]],
          [d["in_vec"], d["in_ln_g"], d["in_ln_b"]],
          [d["in_b_" + k] for k in ("Wr", "Wk", "Wv", "Wo", "maa_w1", "maa_w2", "gate_w1", "gate_w2", "decay_w1", "decay_w2")],
          [d["in_f_" + k] for k in ("w_gate", "w_up", "w_down")], [d["in_cf"], d["in_ci"]], out, STOP)
    return run(nc, [arrays], core_ids=[0]).results[0]["out"]
```

```python
import concourse.bass as bass
from concourse import mybir
from contextlib import ExitStack

NB, T, D = 8, 1024, 256
NT = T // 128
HALF = 512
NC = D // 128
NH, DH = 16, 16
HG = 4
NG = NH // HG
HID = 768
NM = HID // 128
DMIX, NMIX = 32, 5
DLOW = 64
WH = 64
NEG = -1.0e38
RING = 6
SPLIT_Q = [0, 0, 1, 1, 0, 2]
SPLIT_K = [0, 1, 0, 1, 2, 0]
AUG = DH * 6
MIX_ORDER = [0, 4, 3, 1, 2]
LEVELS = 7


ROTATE = [16 * (i // 16) + (i + 8) % 16 for i in range(32)]


def score_units():
    return [(j, f) for j in range(NT) for f in (0, 1) if 128 * j < HALF * (f + 1)]


def max_pieces():
    out = []
    for i in range(NT):
        out.append((i, 0, min(HALF, 128 * (i + 1)), i))
        if i >= 4:
            out.append((i, HALF, 128 * (i + 1) - HALF, NT + i - 4))
    return out


UNITS = score_units()
PIECES = max_pieces()
NPC = len(PIECES) * HG
KV_ORDER = [0, 2, 1, 3]
DOWN_AT = 7
LAG = 9


def psum_plan():
    p = []

    def add(kind, n, who):
        p.extend((kind, i, who) for i in range(n))

    def ffn(k):
        add(f"ln{k}", 2, "dve")
        for f in (0, 1):
            for e in range(2 * NM):
                if f == 0 and e == 4:
                    p.extend((f"ln{k}", i, "dve") for i in (2, 3))
                p.append((f"gu{k}", 2 * NM * f + e, "dve"))
                if f == 1 and e == DOWN_AT:
                    p.append((f"dn{k}", 0, "dve"))
        p.extend((f"dn{k}", i, "dve") for i in (1, 2, 3))

    for f in (0, 1):
        p.extend(("ln0", 2 * f + i, "act") for i in (0, 1))
        p.extend(("qk", 2 * f + i, "dve") for i in (0, 1))
    add("v", 4, "act")
    p.extend(("qk", i, "dve") for i in range(4, 8))
    for s in range(NG + 1):
        for k in range(NPC + LAG):
            if s < NG and k < NPC:
                p.append(("max", s * NPC + k, "dve"))
            if s >= 1 and k >= LAG:
                p.append(("score", (s - 1) * NPC + k - LAG, "act"))
        if s < NG:
            p.append(("aug", s, "dve"))
    add("o", 4, "dve")
    ffn(1)
    for f in (0, 1):
        p.extend(("ln2", 2 * f + i, "act") for i in (0, 1))
        p.extend(("lora", 2 * f + i, "act") for i in (0, 1))
    mixed = {0: [], 1: [("dech", 2, "act")], 2: [("gateh", 2, "act")], 3: [("w", 4, "act"), ("r", 4, "act")],
             4: [("g", 4, "act"), ("k", 4, "act"), ("vb", 4, "act")]}
    for n in range(NMIX):
        p.extend(("mix", 4 * n + i, "dve") for i in range(4))
        for m in mixed[n]:
            add(*m)
    add("diag", 8, "dve")
    add("level", LEVELS * 4, "dve")
    add("kt", 4, "act")
    p.extend(("kv", n, "dve") for n in KV_ORDER)
    add("y", 4, "dve")
    for f in (0, 1):
        p.extend(("zt", 2 * f + i, "act") for i in (0, 1))
        p.extend(("ob", 2 * f + i, "dve") for i in (0, 1))
    ffn(3)
    return p


PLAN = psum_plan()
NTH = {(kind, i): n for n, (kind, i, _) in enumerate(PLAN)}
_seen = {"act": 0, "dve": 0}
RANK = []
for _, _, _who in PLAN:
    _seen[_who] += 1
    RANK.append(_seen[_who])


def build(nc, x_in, w_at, cs, b_vec, b_mat, ffn_w, consts, out, stop_after=None):
    f32, bf16, i32, f32r = mybir.dt.float32, mybir.dt.bfloat16, mybir.dt.int32, mybir.dt.float32r
    ALU, ACT, AX = mybir.AluOpType, mybir.ActivationFunctionType, mybir.AxisListType
    S8 = 1.0 / 127.0
    ctx = ExitStack()
    with ctx:
        def sb(name, shape, dt=f32):
            return ctx.enter_context(nc.sbuf_tensor(name, shape, dt))

        sems = []

        def sem(name):
            s = ctx.enter_context(nc.semaphore(name))
            sems.append(s)
            return s

        xres = sb("xres", [128, NT, D])
        xT = sb("xT", [128, NC, 1 + T])
        attn = sb("attn", [128, NT, HG, 128])
        xn = attn[:, :, :, :].rearrange("p i g t -> p i (g t)")[:, :, 0:D]
        spare = attn[:, :, :, :].rearrange("p i g t -> p i (g t)")[:, :, D:2 * D]
        rope = sb("rope", [128, 2, T])
        wqkv = sb("wqkv", [128, NC, 3 * D])
        wo = sb("wo", [128, NG, D])
        wgu = sb("wgu", [128, NC, 2 * HID], f32r)
        wd = sb("wd", [128, NM, D], f32r)
        wide_row = sb("wide_row", [128, 128])
        wide_flag = sb("wide_flag", [128, 1], i32)
        bm = sb("bm", [128, NC, 4 * D])
        mw1 = sb("mw1", [128, NC, NMIX * DMIX])
        mw2 = sb("mw2", [128, NMIX, D])
        low1 = sb("low1", [128, NC, 2 * DLOW])
        low2 = sb("low2", [128, 2, D])
        lng = sb("lng", [128, 2, D])
        vec = sb("vec", [128, 8, NC])
        ident = sb("ident", [128, 128])
        identb = sb("identb", [128, 128], bf16)
        causal = sb("causal", [128, 2, 128], bf16)
        sumT = sb("sumT", [128, 2, HALF])
        recip = sb("recip", [128, 2, HALF // 32])
        lmask = sb("lmask", [128, LEVELS, 64], i32)
        dmask = sb("dmask", [128, 128], i32)
        half_neg = sb("half_neg", [128, 8])
        stats = sb("stats", [128, NT, 6])
        mv = sb("mv", [128, NT, 2])
        rstd = sb("rstd", [128, NT])
        mxp = sb("mxp", [128, 2, HG, 12])
        augf = sb("augf", [128, HG * NT])
        aug = sb("aug", [128, 3, HG, NT], bf16)
        augT = sb("augT", [96, 2, 128], bf16)
        gst = sb("gst", [128, 8, 6])
        gmv = sb("gmv", [128, 2, 8, 2])
        grs = sb("grs", [128, 2, 8])

        ARENA = 27 * 1024
        ARENA_AT = -(-nc.sbuf_base // 32) * 32
        arena = sb("arena", [128, ARENA])
        at = [0]

        def take(n, dt=f32, first=None):
            if first is not None:
                at[0] = first
            a = arena[:, at[0]:at[0] + n]
            at[0] += n
            assert at[0] <= ARENA, at[0]
            return a if dt == f32 else a.bitcast(dt)

        qst = take(8192, bf16, 0).rearrange("p (h t) -> p h t", h=NH)
        kst = take(8192, bf16).rearrange("p (h t) -> p h t", h=NH)
        ptf = take(6144)
        pt = ptf.rearrange("p (u h t) -> p u h t", u=3, h=HG)
        spl = ptf.bitcast(bf16).rearrange("p (m q s t) -> p m q s t", m=2, q=2, s=3)
        vp = take(4096).rearrange("p (i h d) -> p i h d", i=NT, h=NH)
        rden = take(1024).rearrange("p (f t) -> p f t", f=2)
        ta = [spare[:, 2 * k:2 * k + 2, :] for k in range(4)]

        def part(name, shape):
            n = shape[1] * shape[2]
            a = nc.alloc_sbuf_tensor_at(name, shape, f32r, offset=ARENA_AT + 4 * at[0])
            at[0] += n
            assert at[0] <= ARENA, at[0]
            return a

        at[0] = 0
        hh = part("hh", [128, NM, T])
        hl = part("hl", [128, NM, T])
        xh = part("xh", [128, NC, T])
        xl = part("xl", [128, NC, T])
        WLOW_AT = at[0]
        wlow = part("wlow", [128, 1, 2 * NC * HID + NM * D])
        wgul = wlow[:, 0, 0:2 * NC * HID].rearrange("p (c n) -> p c n", c=NC)
        wdl = wlow[:, 0, 2 * NC * HID:].rearrange("p (m n) -> p m n", m=NM)
        tb = take(1024).rearrange("p (f t) -> p f t", f=2)
        ub = take(1024).rearrange("p (f t) -> p f t", f=2)
        hb = take(1024).rearrange("p (f t) -> p f t", f=2)

        def ct(a):
            return a.rearrange("p (c t) -> p c t", c=NC)

        xx_f = take(2048, f32, 0)
        xx, zT = ct(xx_f), ct(xx_f)
        xxx_f = take(2048)
        xxx, kn = ct(xxx_f), xxx_f.rearrange("p (c n i) -> p c n i", c=NC, n=NT)
        lora_f = take(2048)
        lora, S = ct(lora_f), lora_f[:, 0:1024].rearrange("p (c n j) -> p c n j", c=NC, n=NT)
        xf_f = take(4096)
        xf = xf_f.rearrange("p (b c t) -> p b c t", b=2, c=NC)
        A = xf_f.rearrange("p (c n h t) -> p c n h t", c=NC, n=NT, h=2)
        th = take(1024)
        wdec = ct(take(2048))
        kk = ct(take(2048))
        ku = ct(take(2048))
        tot = ct(take(2048))
        vt = take(2048).rearrange("p (i n) -> p i n", i=NT)
        gt = take(2048).rearrange("p (i n) -> p i n", i=NT)
        qd = take(4096).rearrange("p (c h t) -> p c h t", c=NC, h=2)

        parts = nc.dram_tensor("parts", (2, 2, 3, 128, T), bf16).ap()
        wlow_dram = nc.dram_tensor("wlow_dram", (128, 2 * NC * HID + NM * D), f32).ap()
        PB = [ctx.enter_context(nc.psum_tensor(f"PB{i}", [128, 512], f32)) for i in range(8)]

        s_w = sem("weights_loaded")
        s_cast = sem("weights_cast")
        s_zero = sem("consts_zeroed")
        s_split = sem("weights_split")
        s_low = sem("weights_low_stored")
        s_flag = sem("flag_moved")
        filled = sem("psum_filled")
        act_emptied = sem("act_emptied")
        dve_emptied = sem("dve_emptied")
        x_loaded = [sem(f"x_loaded{i}") for i in (0, 1)]
        arena_set = sem("arena_set")
        ln_stat = [sem(f"ln_stat{k}") for k in range(4)]
        ln_aggr = [sem(f"ln_aggr{k}") for k in range(4)]
        ln_eps = [sem(f"ln_eps{k}") for k in range(4)]
        ln_rstd = [sem(f"ln_rstd{k}") for k in range(4)]
        ln_out = [sem(f"ln_out{k}") for k in range(4)]
        resid = [sem(f"resid{k}") for k in range(4)]
        roped = sem("roped")
        rot_chain = sem("rot_chain")
        hi_done = sem("hi_done")
        rem_done = sem("rem_done")
        mid_done = sem("mid_done")
        lo_done = sem("lo_done")
        parts_out = [sem(f"parts_out{m}") for m in (0, 1)]
        stacked = [sem(f"stacked{m}") for m in (0, 1)]
        aug_chain = sem("aug_chain")
        aug_loaded = [sem(f"aug_loaded{g}") for g in range(NG)]
        pv_units = sem("pv_units")
        pv_copied = sem("pv_copied")
        den_chain = sem("den_chain")
        attn_normed = sem("attn_normed")
        tanh_done = [sem("tanh_done1"), sem("tanh_done3")]
        gate_done = [sem("gate_done1"), sem("gate_done3")]
        x_high = [sem("x_high1"), sem("x_high3")]
        h_high = [sem("h_high1"), sem("h_high3")]
        h_low = [sem("h_low1"), sem("h_low3")]
        wlow_loaded = [sem("wlow_loaded1"), sem("wlow_loaded3")]
        xx_done = sem("xx_done")
        xxx_done = sem("xxx_done")
        mix_added = sem("mix_added")
        decay_exp = sem("decay_exp")
        qd_zeroed = sem("qd_zeroed")
        a_zeroed = sem("a_zeroed")
        ku_done = sem("ku_done")
        tot_done = sem("tot_done")
        q_updated = sem("q_updated")
        k_updated = sem("k_updated")
        s_zeroed = sem("s_zeroed")
        s_chain = sem("s_chain")
        gn_stat = sem("gn_stat")
        gn_aggr = sem("gn_aggr")
        gn_eps = sem("gn_eps")
        gn_rstd = sem("gn_rstd")
        gn_lng = sem("gn_lng")
        gn_chain = sem("gn_chain")
        stored = sem("stored")

        emptied = {"act": act_emptied, "dve": dve_emptied}

        def bank(kind, i):
            return PB[NTH[kind, i] % RING]

        def wait_filled(eng, kind, i):
            eng.wait_ge(filled, NTH[kind, i] + 1)

        def wait_emptied(eng, kind, i):
            n = NTH[kind, i]
            eng.wait_ge(emptied[PLAN[n][2]], RANK[n])

        def wait_bank(eng, kind, i):
            n = NTH[kind, i] - RING
            if n >= 0:
                eng.wait_ge(emptied[PLAN[n][2]], RANK[n])

        NW = 2 * NC * HID + NM * D
        WF_AT = 22 * 1024
        with nc.Block() as block:
            @block.sync
            def _(sp):
                def load(dst, src):
                    sp.dma_start(dst, src).then_inc(s_w, 16)
                for k, w in enumerate(w_at[0:3]):
                    load(wqkv[:, :, D * k:D * k + D], w.rearrange("(c p) n -> p c n", p=128))
                sp.wait_ge(s_zero, 7)
                for h in range(NH):
                    load(wo[32 * (h % HG):32 * (h % HG) + DH, h // HG, :], w_at[3][DH * h:DH * h + DH, :])
                load(rope[:, 0, :], cs[0])
                load(rope[:, 1, :], cs[1])
                for k in range(4):
                    load(bm[:, :, D * k:D * k + D], b_mat[k].rearrange("(c p) n -> p c n", p=128))
                load(mw1[:, :, :], b_mat[4].rearrange("(c p) n -> p c n", p=128))
                for f in range(NMIX):
                    r = 32 * f if f < 4 else 96
                    load(mw2[r:r + 32, f, :], b_mat[5][f, :, :])
                load(low1[:, :, 0:DLOW], b_mat[6].rearrange("(c p) n -> p c n", p=128))
                load(low1[:, :, DLOW:2 * DLOW], b_mat[8].rearrange("(c p) n -> p c n", p=128))
                load(low2[0:DLOW, 0, :], b_mat[7])
                load(low2[DLOW:128, 1, :], b_mat[9])
                load(vec[:, :, :], b_vec[0].rearrange("p (k c) -> p k c", c=NC))
                for k in range(2):
                    load(lng[:, k, :], b_vec[1 + k].partition_broadcast(128))
                load(ident[:, :], consts[0][:, 0:128])
                load(arena[:, 8192:8448], consts[0][:, 128:384])
                load(lmask[:, :, :], consts[1][:, 0:448].rearrange("p (l t) -> p l t", l=LEVELS))
                load(dmask[:, :], consts[1][:, 448:576])
                ai = arena[:, :].bitcast(i32)
                load(ai[:, 0:1536].rearrange("p (c n) -> p c n", c=NC), ffn_w[0].rearrange("(c p) n -> p c n", p=128))
                load(ai[:, 1536:3072].rearrange("p (c n) -> p c n", c=NC), ffn_w[1].rearrange("(c p) n -> p c n", p=128))
                load(ai[:, 3072:4608].rearrange("p (m n) -> p m n", m=NM), ffn_w[2].rearrange("(m p) n -> p m n", p=128))
                sp.wait_ge(s_split, 6)
                sp.dma_start(wlow_dram, wlow[:, 0, :].bitcast(f32)).then_inc(s_low, 16)
                sp.wait_ge(s_split, 8)
                sp.dma_start(wide_row[0:1, :], arena[:, WF_AT - 1:WF_AT]).then_inc(s_flag, 16)
                sp.wait_ge(s_low, 16)
            NLOAD = 3 + NH + 2 + 4 + 1 + NMIX + 4 + 1 + 2 + 4 + 3

            @block.gpsimd
            def _(pool):
                pool.memset(wo[:, :, :], 0.0).then_inc(s_zero, 1)
                pool.memset(mw2[:, :, :], 0.0).then_inc(s_zero, 1)
                pool.memset(low2[:, :, :], 0.0).then_inc(s_zero, 1)
                pool.memset(half_neg[:, :], -0.5).then_inc(s_zero, 1)
                pool.memset(xT[:, :, 0:1], 0.0).then_inc(s_zero, 1)
                pool.memset(arena[:, 10000:10001], 0.0).then_inc(s_zero, 1)
                pool.memset(augf[:, :], 0.0).then_inc(s_zero, 1)

            @block.vector
            def _(dve):
                dve.wait_ge(s_w, 16 * NLOAD)
                ai = arena[:, :].bitcast(i32)
                wf = arena[:, WF_AT:WF_AT + NW]
                gate, up = (wf[:, NC * HID * r:NC * HID * (r + 1)].rearrange("p (c n) -> p c n", c=NC) for r in (0, 1))
                down = wf[:, 2 * NC * HID:].rearrange("p (m n) -> p m n", m=NM)
                dve.tensor_copy(wf, ai[:, 0:NW]).then_inc(s_split, 1)
                dve.wait_ge(s_split, 1)
                dve.tensor_copy(wgu[:, :, 0:HID], gate)
                dve.tensor_copy(wgu[:, :, HID:2 * HID], up)
                dve.tensor_copy(wd[:, :, :], down).then_inc(s_split, 1)
                dve.wait_ge(s_split, 2)
                dve.tensor_tensor(wgul[:, :, 0:HID], gate, wgu[:, :, 0:HID].bitcast(f32), ALU.subtract).then_inc(s_split, 1)
                dve.tensor_tensor(wgul[:, :, HID:2 * HID], up, wgu[:, :, HID:2 * HID].bitcast(f32),
                                  ALU.subtract).then_inc(s_split, 1)
                dve.tensor_tensor(wdl, down, wd[:, :, :].bitcast(f32), ALU.subtract).then_inc(s_split, 1)
                dve.wait_ge(s_split, 5)
                dve.tensor_scalar(wf, wlow[:, 0, :].bitcast(f32), 0.0, None, ALU.not_equal).then_inc(s_split, 1)
                dve.wait_ge(s_split, 6)
                dve.reduce_max(arena[:, WF_AT - 1:WF_AT], wf, axis=AX.X).then_inc(s_split, 2)
                dve.wait_ge(s_flag, 16)
                dve.reduce_max(arena[0:1, WF_AT:WF_AT + 1], wide_row[0:1, :], axis=AX.X).then_inc(s_split, 1)
                dve.wait_ge(s_split, 9)
                dve.tensor_copy(wide_flag[0:1, :], arena[0:1, WF_AT:WF_AT + 1])
                dve.tensor_copy(causal[:, :, :], arena[:, 8192:8448].rearrange("p (a n) -> p a n", a=2))
                dve.tensor_copy(identb[:, :], ident[:, :]).then_inc(s_cast, 1)

        with nc.Fori(0, NB) as b:
            with nc.Block() as block:
                @block.sync
                def _(sp):
                    xv = x_in[bass.ds(b, 1), :, :].rearrange("a (i p) c -> p (a i) c", p=128)
                    ov = out[bass.ds(b, 1), :, :].rearrange("a (i p) c -> p (a i) c", p=128)
                    for f in (0, 1):
                        sp.dma_start(xres[:, 4 * f:4 * f + 4, :], xv[:, 4 * f:4 * f + 4, :]).then_inc(x_loaded[f], 16)
                    for m in (0, 1):
                        for q in (0, 1):
                            sp.wait_ge(lo_done, 4 * m + 3 + q)
                            sp.dma_start(parts[m, q, :, :, :].rearrange("s p t -> p s t"),
                                         spl[:, m, q, :, :]).then_inc(parts_out[m], 16)
                            sp.wait_ge(parts_out[m], 16 * q + 16)
                            for blk in range(6):
                                dst = (qst, kst)[q][DH * blk:DH * blk + DH, 8 * m:8 * m + 8, :]
                                part = (SPLIT_Q, SPLIT_K)[q][blk]
                                src = parts[m, q, part, :, :].rearrange("(h d) t -> d h t", d=DH)
                                sp.dma_start(dst, src).then_inc(stacked[m], 16)
                    for g in range(NG):
                        wait_emptied(sp, "aug", g)
                        for r in range(3):
                            sp.dma_start(qst[AUG + r:AUG + r + 1, HG * g:HG * g + HG, :],
                                         augT[32 * r:32 * r + 32, g % 2, :]).then_inc(aug_loaded[g], 16)
                    wide = sp.alloc_register(name="wide_sp")
                    sp.reg_load(wide, wide_flag[0:1, 0:1])
                    with sp.If_ne(wide, 0):
                        for s in (0, 1):
                            sp.wait_ge(resid[2 * s], 3)
                            sp.dma_start(wlow[:, 0, :].bitcast(f32), wlow_dram).then_inc(wlow_loaded[s], 16)
                    for f in (0, 1):
                        k = {1: 0, 2: 1, 3: 2}.get(stop_after, 3)
                        sp.wait_ge(resid[k], 2 * f + 2)
                        sp.dma_start(ov[:, 4 * f:4 * f + 4, :], xres[:, 4 * f:4 * f + 4, :]).then_inc(stored, 16)
                    sp.wait_ge(stored, 32)

                @block.gpsimd
                def _(pool):
                    pool.memset(vp[:, :, :, DH:2 * DH], 0.0).then_inc(arena_set, 1)
                    pool.wait_ge(arena_set, 1)
                    pool.memset(vp[:, :, :, DH:DH + 1], 1.0).then_inc(arena_set, 1)
                    pool.wait_ge(arena_set, 2)

                    def ln_scale(k, f):
                        pool.wait_ge(ln_aggr[k], 4 * f + 4)
                        v = mv[:, 4 * f:4 * f + 4, 1:2].rearrange("p i a -> p (i a)")
                        pool.tensor_scalar(v, v, 1e-5, 1.0, ALU.add, ALU.mult).then_inc(ln_eps[k], 1)
                        pool.wait_ge(ln_eps[k], f + 1)
                        pool.tensor_tensor(rstd[:, 4 * f:4 * f + 4], v, half_neg[:, 0:4], ALU.pow).then_inc(ln_rstd[k], 1)

                    ln_scale(0, 0)
                    ln_scale(0, 1)

                    def low(e):
                        m, f, q = e // 4, e // 2 % 2, e % 2
                        pool.wait_ge(mid_done, e + 1)
                        cols = slice(HALF * f, HALF * f + HALF)
                        pool.tensor_tensor(spl[:, m, q, 2, cols].rearrange("p (a n) -> p a n", a=2), ta[e % 2],
                                           spl[:, m, q, 1, cols].rearrange("p (a n) -> p a n", a=2),
                                           ALU.subtract).then_inc(lo_done, 1)

                    for e in range(8):
                        m, f, q = e // 4, e // 2 % 2, e % 2
                        pool.wait_ge(hi_done, e + 1)
                        pool.tensor_tensor(ta[e % 2], ta[e % 2],
                                           spl[:, m, q, 0, HALF * f:HALF * f + HALF].rearrange("p (a n) -> p a n", a=2),
                                           ALU.subtract).then_inc(rem_done, 1)
                        if e % 4:
                            low(e - 1)
                        if e == 3:
                            low(3)
                    low(7)
                    pool.wait_ge(lo_done, 8)
                    pool.memset(kst[AUG:AUG + 3, :, :], 1.0).then_inc(arena_set, 1)
                    pool.wait_ge(arena_set, 3)

                    def ffn(s):
                        for e in range(2 * NM):
                            f, m = e // NM, e % NM
                            cols = slice(HALF * f, HALF * f + HALF)
                            pool.wait_ge(h_high[s], e + 1)
                            pool.tensor_tensor(hl[:, m, cols], hb[:, e % 2, :], hh[:, m, cols].bitcast(f32),
                                               ALU.subtract).then_inc(h_low[s], 1)
                    for n in range(2 * NG):
                        g, f = n // 2, n % 2
                        pool.wait_ge(den_chain, 8 * g + 7 + f)
                        pool.wait_ge(pv_copied, n + 1)
                        a = attn[:, 4 * f:4 * f + 4, g, :]
                        pool.tensor_tensor(a, a, sumT[:, f, :].rearrange("p (i t) -> p i t", i=4),
                                           ALU.mult).then_inc(attn_normed, 1)
                    ln_scale(1, 0)
                    ln_scale(1, 1)
                    ffn(0)
                    ln_scale(2, 0)
                    ln_scale(2, 1)
                    pool.memset(qd[0:64, :, 1, :], 0.0).then_inc(qd_zeroed, 1)
                    pool.wait_ge(qd_zeroed, 1)
                    pool.memset(qd[64:128, :, 0, :], 0.0).then_inc(qd_zeroed, 1)
                    pool.wait_ge(qd_zeroed, 2)
                    for n in range(4 * NMIX):
                        c, f = n % 2, n // 2 % 2
                        wait_emptied(pool, "mix", n)
                        a = xf[:, n // 4 % 2, c, HALF * f:HALF * f + HALF]
                        pool.tensor_tensor(a, a, xT[:, c, 1 + HALF * f:1 + HALF * f + HALF], ALU.add).then_inc(mix_added, 1)
                    wait_emptied(pool, "w", 3)
                    src, at_, n = wdec, 0, 512
                    for l in range(LEVELS):
                        if l:
                            pool.wait_ge(tot_done, l)
                        dst = tot[:, :, at_:at_ + n]
                        s2 = src.rearrange("p c (n a) -> p c n a", a=2)
                        pool.tensor_tensor(dst, s2[:, :, :, 0], s2[:, :, :, 1], ALU.mult).then_inc(tot_done, 1)
                        src, at_, n = dst, at_ + n, n // 2
                    wait_filled(pool, "vb", 3)
                    pool.memset(A, 0.0).then_inc(a_zeroed, 1)
                    pool.memset(S[:, :, 0, :], 0.0).then_inc(s_zeroed, 1)
                    for l in range(LEVELS):
                        m = 1 << l
                        tm = wdec if l == 0 else tot[:, :, 1024 - 1024 // (m // 2) // 1:1024 - 1024 // m // 1 + 0]
                        for c in range(NC):
                            wait_filled(pool, "level", 4 * l + 2 * c + 1)
                            kv = kk[:, c, :].rearrange("p (n a m) -> p n a m", a=2, m=m)[:, :, 0, :]
                            w = tm[:, c, :].rearrange("p (n a) -> p n a", a=2)[:, :, 1:2].broadcast_to([128, 512 // m, m])
                            if l:
                                pool.wait_ge(k_updated, 2 * (l - 1) + c + 1)
                            pool.tensor_tensor(kv, kv, w, ALU.mult).then_inc(k_updated, 1)
                    for n in range(4):
                        pool.wait_ge(gn_aggr, 8 * n + 8)
                        v = gmv[:, n % 2, :, 1:2].rearrange("p i a -> p (i a)")
                        pool.tensor_scalar(v, v, 0.00064, 1.0, ALU.add, ALU.mult).then_inc(gn_eps, 1)
                        pool.wait_ge(gn_eps, n + 1)
                        pool.tensor_tensor(grs[:, n % 2, :], v, half_neg[:, :], ALU.pow).then_inc(gn_rstd, 1)
                        pool.wait_ge(gn_rstd, n + 1)
                        pool.wait_ge(gn_lng, n + 1)
                        z = xn[:, 2 * n:2 * n + 2, :]
                        zh = z.rearrange("p i (h j) -> p i h j", j=WH)
                        r = grs[:, n % 2, :].rearrange("p (i h a) -> p i h a", i=2, a=1).broadcast_to([128, 2, 4, WH])
                        pool.tensor_tensor(zh, zh, r, ALU.mult).then_inc(gn_chain, 1)
                        pool.wait_ge(gn_chain, 3 * n + 1)
                        pool.tensor_tensor(z, z, lng[:, 1:2, :].broadcast_to([128, 2, D]), ALU.add).then_inc(gn_chain, 1)
                        pool.wait_ge(gn_chain, 3 * n + 2)
                        pool.tensor_tensor(z, z, gt[:, 2 * n:2 * n + 2, :], ALU.mult).then_inc(gn_chain, 1)
                    ln_scale(3, 0)
                    ln_scale(3, 1)
                    ffn(1)

                @block.scalar
                def _(act):
                    def copy_xT(k, ns=range(4)):
                        for n in ns:
                            f, c = n // 2, n % 2
                            wait_filled(act, f"ln{k}", n)
                            act.activation(xT[:, c, 1 + HALF * f:1 + HALF * f + HALF], bank(f"ln{k}", n)[:, :],
                                           ACT.Copy).then_inc(act_emptied, 1)

                    copy_xT(0)

                    def mid(e):
                        act.wait_ge(rem_done, e + 1)
                        m, f, q = e // 4, e // 2 % 2, e % 2
                        act.activation(spl[:, m, q, 1, HALF * f:HALF * f + HALF].rearrange("p (a n) -> p a n", a=2),
                                       ta[e % 2], ACT.Copy).then_inc(mid_done, 1)

                    def high(e):
                        m, f, q = e // 4, e // 2 % 2, e % 2
                        act.wait_ge(roped, e + 1)
                        act.activation(spl[:, m, q, 0, HALF * f:HALF * f + HALF].rearrange("p (a n) -> p a n", a=2),
                                       ta[e % 2], ACT.Copy).then_inc(hi_done, 1)
                        if e % 4:
                            mid(e - 1)

                    def v_out(n):
                        wait_filled(act, "v", n)
                        act.activation(vp[:, 2 * n:2 * n + 2, :, 0:DH],
                                       bank("v", n)[:, :].rearrange("p (i h d) -> p i h d", i=2, h=NH),
                                       ACT.Copy).then_inc(act_emptied, 1)

                    act.wait_ge(arena_set, 2)
                    for e in range(4):
                        high(e)
                    mid(3)
                    for n in range(4):
                        v_out(n)
                    for e in range(4, 8):
                        high(e)
                    mid(7)
                    for g in range(NG):
                        for k in range(NPC):
                            u, h = k // HG, k % HG
                            j, f = UNITS[u]
                            n = HALF * (f + 1) - max(HALF * f, 128 * j)
                            U = g * len(UNITS) + u
                            wait_filled(act, "score", g * NPC + k)
                            if h == 0 and U >= 3:
                                act.wait_ge(pv_units, U - 2)
                            if U == 0 and h == 0:
                                act.wait_ge(parts_out[0], 32)
                                act.wait_ge(parts_out[1], 32)
                            act.activation(pt[:, U % 3, h, 0:n], bank("score", g * NPC + k)[:, 0:n], ACT.Exp,
                                           scale=DH ** -0.5).then_inc(act_emptied, 1)
                        act.wait_ge(pv_units, (g + 1) * len(UNITS))
                        for f in (0, 1):
                            act.activation(attn[:, 4 * f:4 * f + 4, g, :],
                                           PB[6 + f][:, :].rearrange("p (i t) -> p i t", i=4),
                                           ACT.Copy).then_inc(pv_copied, 1)

                    def ffn(k, s):
                        def x_parts(ns):
                            for n in ns:
                                f, c = n // 2, n % 2
                                wait_filled(act, f"ln{k}", n)
                                act.activation(xh[:, c, HALF * f:HALF * f + HALF], bank(f"ln{k}", n)[:, :],
                                               ACT.Copy).then_inc(x_high[s], 1)

                        def h_part(e):
                            f, m = e // NM, e % NM
                            wait_emptied(act, f"gu{k}", 2 * e + 1)
                            act.activation(hh[:, m, HALF * f:HALF * f + HALF], hb[:, e % 2, :],
                                           ACT.Copy).then_inc(h_high[s], 1)

                        x_parts((0, 1))
                        for e in range(2 * NM):
                            if e == 2:
                                x_parts((2, 3))
                            wait_filled(act, f"gu{k}", 2 * e)
                            if e >= 2:
                                act.wait_ge(gate_done[s], e - 1)
                            act.activation(tb[:, e % 2, :], bank(f"gu{k}", 2 * e)[:, :], ACT.Tanh,
                                           scale=0.5 * S8).then_inc(tanh_done[s], 1)
                            if e:
                                h_part(e - 1)
                        h_part(2 * NM - 1)

                    ffn(1, 0)
                    for n in range(4):
                        l, f = n % 2, n // 2
                        if l == 0:
                            copy_xT(2, (n, n + 1))
                        wait_filled(act, "lora", n)
                        act.activation(lora[:, l, HALF * f:HALF * f + HALF], bank("lora", n)[:, :],
                                       ACT.Tanh).then_inc(act_emptied, 1)
                    for kind, r in (("dech", 64), ("gateh", 0)):
                        for f in (0, 1):
                            wait_filled(act, kind, f)
                            act.activation(th[r:r + 64, HALF * f:HALF * f + HALF], bank(kind, f)[r:r + 64, :],
                                           ACT.Tanh).then_inc(act_emptied, 1)
                    for n in range(4):
                        c, f = n % 2, n // 2
                        w = wdec[:, c, HALF * f:HALF * f + HALF]
                        wait_filled(act, "w", n)
                        act.activation(w, bank("w", n)[:, :], ACT.Exp, bias=vec[:, 6, c:c + 1]).then_inc(decay_exp, 1)
                        act.wait_ge(decay_exp, n + 1)
                        act.activation(w, w, ACT.Exp, scale=-1.0).then_inc(act_emptied, 1)
                    act.wait_ge(qd_zeroed, 2)
                    for n in range(4):
                        c, f = n % 2, n // 2
                        wait_filled(act, "r", n)
                        act.activation(qd[0:64, c, 0, HALF * f:HALF * f + HALF], bank("r", n)[0:64, :], ACT.Copy)
                        act.activation(qd[64:128, c, 1, HALF * f:HALF * f + HALF], bank("r", n)[64:128, :],
                                       ACT.Copy).then_inc(act_emptied, 1)
                    for n in range(4):
                        wait_filled(act, "g", n)
                        act.activation(gt[:, 2 * n:2 * n + 2, :], bank("g", n)[:, :].rearrange("p (i n) -> p i n", i=2),
                                       ACT.Copy).then_inc(act_emptied, 1)
                    for n in range(4):
                        c, f = n % 2, n // 2
                        wait_filled(act, "k", n)
                        act.activation(kk[:, c, HALF * f:HALF * f + HALF], bank("k", n)[:, :],
                                       ACT.Copy).then_inc(act_emptied, 1)
                    for n in range(4):
                        wait_filled(act, "vb", n)
                        act.activation(vt[:, 2 * n:2 * n + 2, :], bank("vb", n)[:, :].rearrange("p (i n) -> p i n", i=2),
                                       ACT.Copy).then_inc(act_emptied, 1)
                    for n in range(4):
                        wait_filled(act, "kt", n)
                        act.activation(kn[:, n // 2, 4 * (n % 2):4 * (n % 2) + 4, :],
                                       bank("kt", n)[:, :].rearrange("p (n i) -> p n i", n=4),
                                       ACT.Copy).then_inc(act_emptied, 1)
                    for n in range(4):
                        f, c = n // 2, n % 2
                        wait_filled(act, "zt", n)
                        act.activation(zT[:, c, HALF * f:HALF * f + HALF], bank("zt", n)[:, :],
                                       ACT.Copy).then_inc(act_emptied, 1)
                    ffn(3, 1)

                @block.vector
                def _(dve):
                    def ln_tile(k, i):
                        dve.bn_stats(stats[:, i, :], xres[:, i, :]).then_inc(ln_stat[k], 1)

                    def ln_half(k, f):
                        dve.wait_ge(ln_stat[k], 4 * f + 4)
                        for i in range(4 * f, 4 * f + 4):
                            dve.bn_aggr(mv[:, i, :], stats[:, i, :]).then_inc(ln_aggr[k], 1)
                        dve.wait_ge(ln_aggr[k], 4 * f + 4)
                        dve.wait_ge(ln_rstd[k], f + 1)
                        for i in range(4 * f, 4 * f + 4):
                            dve.tensor_scalar(xn[:, i, :], xres[:, i, :], mv[:, i, 0:1], rstd[:, i:i + 1],
                                              ALU.subtract, ALU.mult).then_inc(ln_out[k], 1)

                    def residual(kind, n, s, scale=None):
                        wait_filled(dve, kind, n)
                        a = xres[:, 2 * n:2 * n + 2, :].rearrange("p i c -> p (i c)")
                        if scale is None:
                            dve.tensor_tensor(a, bank(kind, n)[:, :], a, ALU.add).then_inc(dve_emptied, 1)
                        else:
                            dve.scalar_tensor_tensor(out=a, in0=bank(kind, n)[:, :], scalar=scale, in1=a,
                                                     op0=ALU.mult, op1=ALU.add).then_inc(dve_emptied, 1)
                        dve.wait_ge(dve_emptied, RANK[NTH[kind, n]])
                        dve.engine_nop().then_inc(resid[s], 1)
                        if s < 3:
                            ln_tile(s + 1, 2 * n)
                            ln_tile(s + 1, 2 * n + 1)
                            if n % 2:
                                ln_half(s + 1, n // 2)

                    for f in (0, 1):
                        dve.wait_ge(x_loaded[f], 16)
                        for i in range(4 * f, 4 * f + 4):
                            ln_tile(0, i)
                        ln_half(0, f)

                    def rotary(e):
                        f = e // 2 % 2
                        ps = bank("qk", e)[:, :].rearrange("p (a n) -> p a n", a=2)
                        cos, sin = (rope[:, r, HALF * f:HALF * f + HALF].rearrange("p (a n) -> p a n", a=2) for r in (0, 1))
                        main, turned = ta[e % 2], ta[2 + e % 2]
                        if e >= 2:
                            dve.wait_ge(lo_done, e - 1)
                        wait_filled(dve, "qk", e)
                        dve.stream_shuffle(turned, ps, ROTATE).then_inc(rot_chain, 1)
                        dve.tensor_tensor(main, ps, cos, ALU.mult).then_inc(dve_emptied, 1)
                        dve.wait_ge(rot_chain, 2 * e + 1)
                        dve.tensor_tensor(turned, turned, sin, ALU.mult).then_inc(rot_chain, 1)
                        wait_emptied(dve, "qk", e)
                        dve.wait_ge(rot_chain, 2 * e + 2)
                        dve.tensor_tensor(main, main, turned, ALU.add).then_inc(roped, 1)

                    for e in range(8):
                        rotary(e)

                    def max_piece(g, k):
                        h, (i, s0, n, col) = k // len(PIECES), PIECES[k % len(PIECES)]
                        wait_filled(dve, "max", g * NPC + k)
                        dve.reduce_max(mxp[:, g % 2, h, col:col + 1], bank("max", g * NPC + k)[:, 0:n],
                                       axis=AX.X).then_inc(dve_emptied, 1)

                    def den(g, step):
                        for f in (0, 1):
                            if step == 0:
                                dve.wait_ge(pv_copied, 2 * g + f + 1)
                                if g:
                                    dve.wait_ge(attn_normed, 2 * g)
                                last = dve.transpose(sumT[:, f, :].rearrange("p (i t) -> p i t", i=4),
                                                     attn[:, 4 * f:4 * f + 4, g, :])
                            else:
                                dve.wait_ge(den_chain, 8 * g + 2 * step - 1 + f)
                            blocks = sumT[:, f, :].rearrange("p (a n) -> p a n", n=32)
                            one = recip[:, f, :].rearrange("p (a n) -> p a n", n=1)
                            wide = rden[:, f, :].rearrange("p (a n) -> p a n", n=32)
                            if step == 1:
                                last = dve.reciprocal(one, blocks[:, :, DH:DH + 1])
                            if step == 2:
                                last = dve.tensor_copy(wide, one.broadcast_to([128, HALF // 32, 32]))
                            if step == 3:
                                last = dve.transpose(sumT[:, f, :], rden[:, f, :])
                            last.then_inc(den_chain, 1)

                    for g in range(NG):
                        for k in range(NPC):
                            max_piece(g, k)
                            if g >= 2 and 2 <= k < 6:
                                den(g - 2, k - 2)
                        dve.wait_ge(dve_emptied, RANK[NTH["max", g * NPC + NPC - 1]])
                        mg, af = mxp[:, g % 2, :, :], augf[:, :].rearrange("p (h i) -> p h i", h=HG)
                        dve.tensor_tensor(mg[:, :, 4:8], mg[:, :, 4:8], mg[:, :, 8:12], ALU.max).then_inc(aug_chain, 1)
                        dve.wait_ge(aug_chain, 6 * g + 1)
                        dve.tensor_scalar(aug[:, 0, :, :], mg[:, :, 0:8], -1.0, None, ALU.mult).then_inc(aug_chain, 1)
                        dve.wait_ge(aug_chain, 6 * g + 2)
                        dve.scalar_tensor_tensor(out=af, in0=mg[:, :, 0:8], scalar=-1.0, in1=aug[:, 0, :, :],
                                                 op0=ALU.mult, op1=ALU.subtract).then_inc(aug_chain, 1)
                        dve.wait_ge(aug_chain, 6 * g + 3)
                        dve.tensor_copy(aug[:, 1, :, :], af).then_inc(aug_chain, 1)
                        dve.wait_ge(aug_chain, 6 * g + 4)
                        dve.tensor_tensor(af, af, aug[:, 1, :, :], ALU.subtract).then_inc(aug_chain, 1)
                        dve.wait_ge(aug_chain, 6 * g + 5)
                        dve.tensor_copy(aug[:, 2, :, :], af).then_inc(aug_chain, 1)
                        wait_filled(dve, "aug", g)
                        if g >= 2:
                            dve.wait_ge(aug_loaded[g - 2], 48)
                        dve.tensor_copy(augT[:, g % 2, :], bank("aug", g)[0:96, 0:64].bitcast(bf16)).then_inc(dve_emptied, 1)
                    for g in (NG - 2, NG - 1):
                        for step in range(4):
                            den(g, step)
                    for n in range(4):
                        residual("o", n, 0)

                    def ffn(k, s):
                        def down(n):
                            residual(f"dn{k}", n, k, 0.5 * S8 * S8 * S8)

                        def x_low(ns):
                            for n in ns:
                                f, c = n // 2, n % 2
                                cols = slice(HALF * f, HALF * f + HALF)
                                dve.wait_ge(x_high[s], n + 1)
                                dve.tensor_tensor(xl[:, c, cols], bank(f"ln{k}", n)[:, :], xh[:, c, cols].bitcast(f32),
                                                  ALU.subtract).then_inc(dve_emptied, 1)

                        x_low((0, 1))
                        for e in range(2 * NM):
                            if e == 2:
                                x_low((2, 3))
                            u = ub[:, e % 2, :]
                            dve.wait_ge(tanh_done[s], e + 1)
                            dve.scalar_tensor_tensor(out=u, in0=tb[:, e % 2, :], scalar=1.0,
                                                     in1=bank(f"gu{k}", 2 * e)[:, :], op0=ALU.add,
                                                     op1=ALU.mult).then_inc(dve_emptied, 1)
                            wait_filled(dve, f"gu{k}", 2 * e + 1)
                            dve.wait_ge(dve_emptied, RANK[NTH[f"gu{k}", 2 * e]])
                            if e >= 2:
                                dve.wait_ge(h_low[s], e - 1)
                            dve.tensor_tensor(hb[:, e % 2, :], bank(f"gu{k}", 2 * e + 1)[:, :], u,
                                              ALU.mult).then_inc(dve_emptied, 1)
                            dve.wait_ge(dve_emptied, RANK[NTH[f"gu{k}", 2 * e + 1]])
                            dve.engine_nop().then_inc(gate_done[s], 1)
                            if e == NM + DOWN_AT // 2:
                                down(0)
                        for n in (1, 2, 3):
                            down(n)

                    ffn(1, 0)
                    for n in range(4):
                        f, c = n // 2, n % 2
                        cols = slice(HALF * f, HALF * f + HALF)
                        now = xT[:, c, 1 + HALF * f:1 + HALF * f + HALF]
                        wait_emptied(dve, "ln2", n)
                        dve.tensor_tensor(xx[:, c, cols], xT[:, c, cols], now, ALU.subtract).then_inc(xx_done, 1)
                        dve.wait_ge(xx_done, n + 1)
                        dve.scalar_tensor_tensor(out=xxx[:, c, cols], in0=xx[:, c, cols], scalar=vec[:, 0, c:c + 1],
                                                 in1=now, op0=ALU.mult, op1=ALU.add).then_inc(xxx_done, 1)
                    for n in range(4 * NMIX):
                        mi, f, c = n // 4, n // 2 % 2, n % 2
                        cols = slice(HALF * f, HALF * f + HALF)
                        if mi == 2:
                            wait_filled(dve, "dech", 1)
                        if mi == 3:
                            wait_filled(dve, "gateh", 1)
                        if mi == 4:
                            wait_filled(dve, "r", 3)
                        wait_filled(dve, "mix", n)
                        fi = MIX_ORDER[mi]
                        dve.scalar_tensor_tensor(out=xf[:, mi % 2, c, cols], in0=bank("mix", n)[:, :],
                                                 scalar=vec[:, 1 + fi, c:c + 1], in1=xx[:, c, cols],
                                                 op0=ALU.add, op1=ALU.mult).then_inc(dve_emptied, 1)
                    for c in range(NC):
                        wait_emptied(dve, "k", 2 + c)
                        dve.tensor_scalar(ku[:, c, :], kk[:, c, :], vec[:, 7, c:c + 1], None, ALU.mult).then_inc(ku_done, 1)
                    dve.wait_ge(a_zeroed, 1)
                    for n in range(8):
                        c, q = n // 4, n % 4
                        wait_filled(dve, "diag", n)
                        a = A[:, c, 2 * q:2 * q + 2, :, :].rearrange("p n h t -> p (n h) t")
                        dve.copy_predicated(a, dmask[:, :].rearrange("p (a t) -> p a t", a=1).broadcast_to([128, 4, 128]),
                                            bank("diag", n)[:, :].rearrange("p (a t) -> p a t", a=4)).then_inc(dve_emptied, 1)
                    dve.wait_ge(tot_done, LEVELS)
                    for l in range(LEVELS):
                        m = 1 << l
                        tm = wdec if l == 0 else tot[:, :, 1024 - 1024 // (m // 2):1024 - 1024 // m]
                        for c in range(NC):
                            for q in (0, 1):
                                n = 4 * l + 2 * c + q
                                wait_filled(dve, "level", n)
                                dve.wait_ge(dve_emptied, RANK[NTH["level", n - 4] if l else NTH["diag", 7]])
                                a = A[:, c, 4 * q:4 * q + 4, :, :].rearrange("p n h (b s m) -> p (n h) b s m", s=2, m=m)[:, :, :, 1, :]
                                mk = lmask[:, l:l + 1, :].broadcast_to([128, 8, 64]).rearrange("p a (b m) -> p a b m", m=m)
                                dve.copy_predicated(a, mk, bank("level", n)[:, :].rearrange("p (a b m) -> p a b m", a=8, m=m)
                                                    ).then_inc(dve_emptied, 1)
                            for h in (0, 1):
                                p = slice(64 * h, 64 * h + 64)
                                qv = qd[p, c, h, :].rearrange("p (n s m) -> p n s m", s=2, m=m)[:, :, 1, :]
                                w = tm[p, c, :].rearrange("p (n s) -> p n s", s=2)[:, :, 0:1].broadcast_to([64, 512 // m, m])
                                if l:
                                    dve.wait_ge(q_updated, 4 * (l - 1) + 2 * c + h + 1)
                                dve.tensor_tensor(qv, qv, w, ALU.mult).then_inc(q_updated, 1)
                    dve.wait_ge(s_zeroed, 1)
                    for ch in range(NT - 1):
                        for c in range(NC):
                            n = 2 * c + ch // 4
                            wait_filled(dve, "kv", n)
                            if ch:
                                dve.wait_ge(s_chain, 2 * (ch - 1) + c + 1)
                            kv = bank("kv", n)[:, WH * (ch % 4):WH * (ch % 4) + WH]
                            dve.scalar_tensor_tensor(out=S[:, c, ch + 1, :], in0=S[:, c, ch, :],
                                                     scalar=tot[:, c, 1008 + ch:1009 + ch], in1=kv,
                                                     op0=ALU.mult, op1=ALU.add).then_inc(s_chain, 1)
                            if ch in (3, NT - 2):
                                dve.wait_ge(s_chain, 2 * ch + c + 1)
                                dve.engine_nop().then_inc(dve_emptied, 1)
                    for n in range(4):
                        wait_filled(dve, "y", n)
                        if n >= 2:
                            dve.wait_ge(gn_chain, 3 * (n - 2) + 1)
                        ps = bank("y", n)[:, :].rearrange("p (a j) -> p a j", j=WH)
                        for a in range(8):
                            dve.bn_stats(gst[:, a, :], ps[:, a, :]).then_inc(gn_stat, 1)
                        dve.wait_ge(gn_stat, 8 * n + 8)
                        for a in range(8):
                            dve.bn_aggr(gmv[:, n % 2, a, :], gst[:, a, :]).then_inc(gn_aggr, 1)
                        dve.wait_ge(gn_aggr, 8 * n + 8)
                        z = xn[:, 2 * n:2 * n + 2, :]
                        dve.tensor_tensor(z.rearrange("p i (h j) -> p i h j", j=WH),
                                          bank("y", n)[:, :].rearrange("p (i h j) -> p i h j", i=2, j=WH),
                                          gmv[:, n % 2, :, 0:1].rearrange("p (i h) a -> p i h a", i=2).broadcast_to([128, 2, 4, WH]),
                                          ALU.subtract).then_inc(dve_emptied, 1)
                        dve.wait_ge(dve_emptied, RANK[NTH["y", n]])
                        dve.tensor_tensor(z, z, lng[:, 0:1, :].broadcast_to([128, 2, D]), ALU.mult).then_inc(gn_lng, 1)
                    for n in range(4):
                        residual("ob", n, 2)
                    ffn(3, 1)

                @block.tensor
                def _(pe):
                    mm = pe.matmul

                    def transpose_x(k, ns=range(4)):
                        for n in ns:
                            f, c = n // 2, n % 2
                            wait_bank(pe, f"ln{k}", n)
                            for j in range(4):
                                i = 4 * f + j
                                pe.wait_ge(ln_out[k], i + 1)
                                last = pe.transpose(bank(f"ln{k}", n)[:, 128 * j:128 * j + 128],
                                                    xn[:, i, 128 * c:128 * c + 128], ident[:, :])
                            last.then_inc(filled, 1)

                    def xcols(c, f):
                        return xT[:, c, 1 + HALF * f:1 + HALF * f + HALF]

                    def xtile(c, i):
                        return xT[:, c, 1 + 128 * i:1 + 128 * i + 128]

                    def qk_item(e):
                        m, f, q = e // 4, e // 2 % 2, e % 2
                        wait_emptied(pe, "ln0", 2 * f + 1)
                        wait_bank(pe, "qk", e)
                        w0 = D * q + 128 * m
                        for c in range(NC):
                            last = mm(bank("qk", e)[:, :], wqkv[:, c, w0:w0 + 128], xcols(c, f),
                                      start=(c == 0), stop=(c == NC - 1))
                        last.then_inc(filled, 1)

                    def v_item(n):
                        wait_bank(pe, "v", n)
                        for a in (0, 1):
                            for c in range(NC):
                                last = mm(bank("v", n)[:, D * a:D * a + D], xtile(c, 2 * n + a), wqkv[:, c, 2 * D:3 * D],
                                          start=(c == 0), stop=(c == NC - 1))
                        last.then_inc(filled, 1)

                    def max_item(g, k):
                        h, (i, s0, n, col) = g * HG + k // len(PIECES), PIECES[k % len(PIECES)]
                        wait_bank(pe, "max", g * NPC + k)
                        ps = bank("max", g * NPC + k)
                        diag = s0 + n == 128 * (i + 1)
                        last = mm(ps[:, 0:n], qst[0:AUG, h, 128 * i:128 * i + 128], kst[0:AUG, h, s0:s0 + n],
                                  start=True, stop=not diag)
                        if diag:
                            last = mm(ps[:, n - 128:n], identb[:, :], causal[:, 0, :], start=False, stop=True)
                        last.then_inc(filled, 1)

                    def score_item(g, k):
                        u, h = k // HG, g * HG + k % HG
                        j, f = UNITS[u]
                        t0 = max(HALF * f, 128 * j)
                        n = HALF * (f + 1) - t0
                        wait_bank(pe, "score", g * NPC + k)
                        ps = bank("score", g * NPC + k)
                        diag = t0 == 128 * j
                        last = mm(ps[:, 0:n], kst[0:AUG + 3, h, 128 * j:128 * j + 128], qst[0:AUG + 3, h, t0:t0 + n],
                                  start=True, stop=not diag)
                        if diag:
                            last = mm(ps[:, 0:128], identb[:, :], causal[:, 1, :], start=False, stop=True)
                        last.then_inc(filled, 1)

                    def pv(g, u):
                        j, f = UNITS[u]
                        t0 = max(HALF * f, 128 * j)
                        n = HALF * (f + 1) - t0
                        U = g * len(UNITS) + u
                        wait_emptied(pe, "score", g * NPC + HG * u + HG - 1)
                        if j == 0 and g:
                            pe.wait_ge(pv_copied, 2 * g)
                        for h in range(HG):
                            last = mm(PB[6 + f][32 * h:32 * h + 32, t0 - HALF * f:HALF], vp[:, j, g * HG + h, :],
                                      pt[:, U % 3, h, 0:n], start=(j == 0), stop=(j == 4 * f + 3))
                        last.then_inc(pv_units, 1)

                    for f in (0, 1):
                        transpose_x(0, (2 * f, 2 * f + 1))
                        qk_item(2 * f)
                        qk_item(2 * f + 1)
                    for n in range(4):
                        v_item(n)
                    for e in range(4, 8):
                        qk_item(e)
                    for s in range(NG + 1):
                        if s in (0, 2):
                            pe.wait_ge(stacked[s // 2], 2 * 6 * 16)
                        for k in range(NPC + LAG):
                            if s < NG and k < NPC:
                                max_item(s, k)
                            if s >= 1 and k == LAG:
                                pe.wait_ge(aug_loaded[s - 1], 48)
                                pe.wait_ge(arena_set, 3)
                            if s >= 1 and k >= LAG:
                                score_item(s - 1, k - LAG)
                                if (k - LAG) % HG == HG - 1 and (k - LAG) // HG >= 2:
                                    pv(s - 1, (k - LAG) // HG - 2)
                        if s >= 1:
                            pv(s - 1, len(UNITS) - 2)
                            pv(s - 1, len(UNITS) - 1)
                        if s < NG:
                            pe.wait_ge(aug_chain, 6 * s + 6)
                            wait_bank(pe, "aug", s)
                            pe.transpose(bank("aug", s)[0:96, 0:64].bitcast(bf16),
                                         aug[:, :, :, :].rearrange("p r h i -> p (r h i)"), identb[:, :]).then_inc(filled, 1)
                    for n in range(4):
                        pe.wait_ge(attn_normed, 2 * NG - 1 + n // 2)
                        wait_bank(pe, "o", n)
                        for a in (0, 1):
                            for g in range(NG):
                                last = mm(bank("o", n)[:, D * a:D * a + D], attn[:, 2 * n + a, g, :], wo[:, g, :],
                                          start=(g == 0), stop=(g == NG - 1))
                        last.then_inc(filled, 1)

                    def ffn(k, s, general):
                        def products(dst, pairs):
                            for j, (lhs, rhs) in enumerate(pairs):
                                last = mm(dst, lhs, rhs, start=(j == 0), stop=(j == len(pairs) - 1))
                            return last

                        def down(n):
                            pe.wait_ge(h_low[s], NM * (n // 2 + 1))
                            wait_bank(pe, f"dn{k}", n)
                            for a in (0, 1):
                                t = slice(128 * (2 * n + a), 128 * (2 * n + a) + 128)
                                last = products(bank(f"dn{k}", n)[:, D * a:D * a + D],
                                                [(h[:, m, t], w[:, m, :]) for m in range(NM)
                                                 for w in ((wd, wdl) if general else (wd,)) for h in (hh, hl)])
                            last.then_inc(filled, 1)

                        if general:
                            pe.wait_ge(wlow_loaded[s], 16)
                        transpose_x(k, (0, 1))
                        for f in (0, 1):
                            cols = slice(HALF * f, HALF * f + HALF)
                            wait_emptied(pe, f"ln{k}", 2 * f + 1)
                            for e in range(2 * NM):
                                if f == 0 and e == 4:
                                    transpose_x(k, (2, 3))
                                m, r = e // 2, e % 2
                                rows = slice(HID * r + 128 * m, HID * r + 128 * m + 128)
                                wait_bank(pe, f"gu{k}", 2 * NM * f + e)
                                products(bank(f"gu{k}", 2 * NM * f + e)[:, :],
                                         [(w[:, c, rows], x[:, c, cols]) for c in range(NC)
                                          for w in ((wgu, wgul) if general else (wgu,)) for x in (xh, xl)]
                                         ).then_inc(filled, 1)
                                if f == 1 and e == DOWN_AT:
                                    down(0)
                        for n in (1, 2, 3):
                            down(n)

                    wide = pe.alloc_register(name="wide_pe")
                    pe.reg_load(wide, wide_flag[0:1, 0:1])
                    with pe.If_ne(wide, 0):
                        ffn(1, 0, True)
                    with pe.Else():
                        ffn(1, 0, False)
                    for n in range(4):
                        l, f = n % 2, n // 2
                        if l == 0:
                            transpose_x(2, (n, n + 1))
                        pe.wait_ge(xxx_done, 2 * f + 2)
                        wait_bank(pe, "lora", n)
                        for c in range(NC):
                            last = mm(bank("lora", n)[:, :], mw1[:, c, 32 * l:32 * l + 128],
                                      xxx[:, c, HALF * f:HALF * f + HALF], start=(c == 0), stop=(c == NC - 1))
                        last.then_inc(filled, 1)

                    def hidden(kind, r, w0, slot, n0):
                        for f in (0, 1):
                            pe.wait_ge(mix_added, 4 * n0 + 2 * f + 2)
                            wait_bank(pe, kind, f)
                            for c in range(NC):
                                last = mm(bank(kind, f)[r:r + 64, :], low1[:, c, w0:w0 + DLOW],
                                          xf[:, slot, c, HALF * f:HALF * f + HALF], start=(c == 0), stop=(c == NC - 1))
                            last.then_inc(filled, 1)

                    def channel_major(kind, w0, slot, n0):
                        for n in range(4):
                            co, f = n % 2, n // 2
                            pe.wait_ge(mix_added, 4 * n0 + 2 * f + 2)
                            wait_bank(pe, kind, n)
                            for c in range(NC):
                                last = mm(bank(kind, n)[:, :], bm[:, c, w0 + 128 * co:w0 + 128 * co + 128],
                                          xf[:, slot, c, HALF * f:HALF * f + HALF], start=(c == 0), stop=(c == NC - 1))
                            last.then_inc(filled, 1)

                    for mi in range(NMIX):
                        fi = MIX_ORDER[mi]
                        for q in range(4):
                            n, f, co = 4 * mi + q, q // 2, q % 2
                            wait_emptied(pe, "lora", 2 * f + 1)
                            wait_bank(pe, "mix", n)
                            mm(bank("mix", n)[:, :], mw2[:, fi, 128 * co:128 * co + 128],
                               lora[:, fi // 4, HALF * f:HALF * f + HALF], start=True, stop=True).then_inc(filled, 1)
                        if mi == 1:
                            hidden("dech", 64, DLOW, 0, 0)
                        if mi == 2:
                            hidden("gateh", 0, 0, 1, 1)
                        if mi == 3:
                            for n in range(4):
                                co, f = n % 2, n // 2
                                wait_emptied(pe, "gateh", f)
                                wait_bank(pe, "w", n)
                                mm(bank("w", n)[:, :], low2[:, 1, 128 * co:128 * co + 128],
                                   th[:, HALF * f:HALF * f + HALF], start=True, stop=True).then_inc(filled, 1)
                            channel_major("r", 0, 0, 2)
                        if mi == 4:
                            for n in range(4):
                                wait_bank(pe, "g", n)
                                for a in (0, 1):
                                    last = mm(bank("g", n)[:, D * a:D * a + D], th[:, 128 * (2 * n + a):128 * (2 * n + a) + 128],
                                              low2[:, 0, :], start=True, stop=True)
                                last.then_inc(filled, 1)
                            channel_major("k", D, 1, 3)
                            for n in range(4):
                                pe.wait_ge(mix_added, 16 + 2 * (n // 2) + 2)
                                wait_bank(pe, "vb", n)
                                for a in (0, 1):
                                    i = 2 * n + a
                                    for c in range(NC):
                                        last = mm(bank("vb", n)[:, D * a:D * a + D], xf[:, 0, c, 128 * i:128 * i + 128],
                                                  bm[:, c, 2 * D:3 * D], start=(c == 0), stop=(c == NC - 1))
                                last.then_inc(filled, 1)
                    wait_emptied(pe, "r", 3)
                    for n in range(8):
                        c, q = n // 4, n % 4
                        pe.wait_ge(ku_done, c + 1)
                        wait_bank(pe, "diag", n)
                        for a in (0, 1):
                            ch = 2 * q + a
                            last = mm(bank("diag", n)[:, 256 * a:256 * a + 256].rearrange("p (h t) -> p h t", h=2),
                                      ku[:, c, 128 * ch:128 * ch + 128], qd[:, c, :, 128 * ch:128 * ch + 128],
                                      start=True, stop=True)
                        last.then_inc(filled, 1)
                    for l in range(LEVELS):
                        m = 1 << l
                        for c in range(NC):
                            for q in (0, 1):
                                n = 4 * l + 2 * c + q
                                if l:
                                    pe.wait_ge(q_updated, 4 * (l - 1) + 2 * c + 2)
                                    pe.wait_ge(k_updated, 2 * (l - 1) + c + 1)
                                wait_bank(pe, "level", n)
                                for a in range(4):
                                    ch = 4 * q + a
                                    rhs = qd[:, c, :, 128 * ch:128 * ch + 128].rearrange("p h (b s m) -> p h b s m", s=2, m=m)[:, :, :, 1, :]
                                    last = mm(bank("level", n)[:, 128 * a:128 * a + 128].rearrange("p (h b m) -> p h b m", h=2, m=m),
                                              kk[:, c, 128 * ch:128 * ch + 128], rhs, start=True, stop=True)
                                last.then_inc(filled, 1)
                    for n in range(4):
                        c = n // 2
                        pe.wait_ge(k_updated, 2 * (LEVELS - 1) + c + 1)
                        wait_bank(pe, "kt", n)
                        for a in range(4):
                            ch = 4 * (n % 2) + a
                            last = pe.transpose(bank("kt", n)[:, 128 * a:128 * a + 128], kk[:, c, 128 * ch:128 * ch + 128],
                                                ident[:, :])
                        last.then_inc(filled, 1)
                    for n in KV_ORDER:
                        c = n // 2
                        wait_emptied(pe, "kt", n)
                        wait_bank(pe, "kv", n)
                        for a in range(4 if n % 2 == 0 else 3):
                            ch = 4 * (n % 2) + a
                            for h in (0, 1):
                                last = mm(bank("kv", n)[64 * h:64 * h + 64, WH * a:WH * a + WH],
                                          kn[:, c, ch, 64 * h:64 * h + 64], vt[:, ch, 128 * c + WH * h:128 * c + WH * h + WH],
                                          start=True, stop=True)
                        last.then_inc(filled, 1)
                    wait_emptied(pe, "level", LEVELS * 4 - 1)
                    pe.wait_ge(q_updated, 4 * LEVELS)
                    for n in range(4):
                        wait_bank(pe, "y", n)
                        pe.wait_ge(s_chain, 2 * (2 * n + 1))
                        for a in (0, 1):
                            ch = 2 * n + a
                            for hd in range(4):
                                c, h = hd // 2, hd % 2
                                o = bank("y", n)[:, D * a + WH * hd:D * a + WH * hd + WH]
                                last = mm(o, A[:, c, ch, h, :], vt[:, ch, WH * hd:WH * hd + WH], start=True, stop=(ch == 0))
                                if ch:
                                    last = mm(o, qd[:, c, h, 128 * ch:128 * ch + 128], S[:, c, ch, :], start=False, stop=True)
                        last.then_inc(filled, 1)
                    for f in (0, 1):
                        pe.wait_ge(gn_chain, 6 * f + 6)
                        for c in range(NC):
                            n = 2 * f + c
                            wait_bank(pe, "zt", n)
                            for j in range(4):
                                last = pe.transpose(bank("zt", n)[:, 128 * j:128 * j + 128],
                                                    xn[:, 4 * f + j, 128 * c:128 * c + 128], ident[:, :])
                            last.then_inc(filled, 1)
                        wait_emptied(pe, "zt", 2 * f + 1)
                        for n in (2 * f, 2 * f + 1):
                            wait_bank(pe, "ob", n)
                            for a in (0, 1):
                                i = 2 * n + a
                                for c in range(NC):
                                    last = mm(bank("ob", n)[:, D * a:D * a + D], zT[:, c, 128 * i:128 * i + 128],
                                              bm[:, c, 3 * D:4 * D], start=(c == 0), stop=(c == NC - 1))
                            last.then_inc(filled, 1)
                    with pe.If_ne(wide, 0):
                        ffn(3, 1, True)
                    with pe.Else():
                        ffn(3, 1, False)

            nc.sync.sem_clear(range(sems[6].num, sems[-1].num + 1))
            nc.all_engine_barrier()


STOP = None


def kernel(**inputs):
    import numpy as np
    import concourse.bacc as bacc
    from concourse.bass_utils import run_bass_kernel_spmd as run

    g = {k: np.asarray(v) for k, v in inputs.items()}
    arrays = {"x": g["L0_attn_a_x"]}
    wq, wk = g["L0_attn_a_Wq"], g["L0_attn_a_Wk"]
    for name, w in (("wq", wq), ("wk", wk), ("wv", g["L0_attn_a_Wv"]), ("wo", g["L0_attn_a_Wo"])):
        arrays[name] = w.T
    for name in ("Wr", "Wk", "Wv", "Wo", "maa_w1", "maa_w2", "gate_w1", "gate_w2", "decay_w1", "decay_w2"):
        arrays["b_" + name] = g["L0_attn_b_" + name]
    names = ("maa_x", "maa_w", "maa_k", "maa_v", "maa_r", "maa_g", "time_decay", "u")
    arrays["vec"] = np.stack([g["L0_attn_b_" + n].reshape(NC, 128) for n in names]).transpose(2, 0, 1).reshape(128, -1)
    arrays["ln_g"], arrays["ln_b"] = g["L0_attn_b_ln_g"], g["L0_attn_b_ln_b"]
    for name in ("w_gate", "w_up", "w_down"):
        arrays["f_" + name] = g["L0_ffn_" + name].T
    inv = (np.float32(1.0) / np.float32(10000.0) ** (np.arange(0, DH, 2, dtype=np.float32) / np.float32(DH))).astype(np.float32)
    ang = (np.arange(T, dtype=np.float32)[:, None] * inv[None, :]).astype(np.float32)
    cos = np.concatenate([np.cos(ang)] * 2, 1).T
    sin = np.concatenate([-np.sin(ang), np.sin(ang)], 1).T
    arrays["cos"] = np.tile(cos, (128 // DH, 1)).astype(np.float32)
    arrays["sin"] = np.tile(sin, (128 // DH, 1)).astype(np.float32)
    p, q = np.arange(128)[:, None], np.arange(128)[None, :]
    arrays["cf"] = np.concatenate([p == q, np.where(q > p, NEG, 0), np.where(q < p, NEG, 0)], 1).astype(np.float32)
    masks = []
    for l in range(LEVELS):
        m = 1 << l
        t = np.array([2 * m * b + m + r for b in range(64 // m) for r in range(m)])[None, :]
        masks.append((p // (2 * m) == t // (2 * m)) & (p % (2 * m) < m))
    arrays["ci"] = np.concatenate(masks + [p == q], 1).astype(np.int32)
    arrays = {"in_" + k: np.ascontiguousarray(v) for k, v in arrays.items()}

    nc = bacc.Bacc("TRN2", target_bir_lowering=False, num_devices=1)
    d = {k: nc.dram_tensor(k, v.shape, mybir.dt.from_np(v.dtype), kind="ExternalInput").ap() for k, v in arrays.items()}
    out = nc.dram_tensor("out", (NB, T, D), mybir.dt.float32, kind="ExternalOutput").ap()
    build(nc, d["in_x"], [d["in_" + k] for k in ("wq", "wk", "wv", "wo")], [d["in_cos"], d["in_sin"]],
          [d["in_vec"], d["in_ln_g"], d["in_ln_b"]],
          [d["in_b_" + k] for k in ("Wr", "Wk", "Wv", "Wo", "maa_w1", "maa_w2", "gate_w1", "gate_w2", "decay_w1", "decay_w2")],
          [d["in_f_" + k] for k in ("w_gate", "w_up", "w_down")], [d["in_cf"], d["in_ci"]], out, STOP)
    return run(nc, [arrays], core_ids=[0]).results[0]["out"]
```

```python
import concourse.bass as bass
from concourse import mybir
from contextlib import ExitStack

NB, T, D = 8, 1024, 256
NT = T // 128
HALF = 512
NC = D // 128
NH, DH = 16, 16
HG = 4
NG = NH // HG
HID = 768
NM = HID // 128
DMIX, NMIX = 32, 5
DLOW = 64
WH = 64
NEG = -1.0e38
RING = 6
RUNS = [(0, 3), (3, 2), (5, 1)]
AUG = DH * 6
MIX_ORDER = [0, 4, 3, 1, 2]
LEVELS = 7


ROTATE = [16 * (i // 16) + (i + 8) % 16 for i in range(32)]


def score_units():
    return [(j, f) for j in range(NT) for f in (0, 1) if 128 * j < HALF * (f + 1)]


def max_pieces():
    out = []
    for i in range(NT):
        out.append((i, 0, min(HALF, 128 * (i + 1)), i))
        if i >= 4:
            out.append((i, HALF, 128 * (i + 1) - HALF, NT + i - 4))
    return out


UNITS = score_units()
DIAG_UNITS = [len(UNITS) * g + u for g in range(NG) for u, (j, f) in enumerate(UNITS) if 128 * j >= HALF * f]
PIECES = max_pieces()
NPC = len(PIECES) * HG
KV_ORDER = [0, 2, 1, 3]
DOWN_AT = 7


def max_item_of(k):
    return k // len(PIECES), PIECES[k % len(PIECES)]


NSC = NG * NPC
LAG = 12
DELAY = NPC + LAG
AUG_AT = 3
NORM_AT = 6
DEN_AT = LAG + 12


def psum_plan():
    p = []

    def add(kind, n, who):
        p.extend((kind, i, who) for i in range(n))

    def ffn(k):
        for f in (0, 1):
            for e in range(2 * NM):
                if f == 0 and e == 4:
                    p.extend((f"ln{k}", i, "dve") for i in (2, 3))
                p.append((f"gu{k}", 2 * NM * f + e, "dve"))
                if f == 1 and e == DOWN_AT:
                    p.append((f"dn{k}", 0, "dve"))
        p.extend((f"dn{k}", i, "dve") for i in ((1, 2) if k == 1 else (1, 2, 3)))

    for f in (0, 1):
        p.extend(("ln0", 2 * f + i, "act") for i in (0, 1))
        p.extend(("qk", 2 * f + i, "dve") for i in (0, 1))
    add("v", 4, "act")
    p.extend(("qk", i, "dve") for i in range(4, 8))
    for t in range(NSC + DELAY):
        if t < NSC:
            p.append(("max", t, "dve"))
        if NPC <= t < NSC + NPC and t % NPC == AUG_AT:
            p.append(("aug", t // NPC - 1, "dve"))
        if t >= DELAY:
            p.append(("score", t - DELAY, "act"))
    add("o", 3, "dve")
    p.extend(("ln1", i, "dve") for i in (0, 1))
    p.append(("o", 3, "dve"))
    ffn(1)
    p.extend(("ln2", i, "act") for i in (0, 1))
    p.append(("dn1", 3, "dve"))
    p.extend(("lora", i, "act") for i in (0, 1))
    p.extend(("ln2", i, "act") for i in (2, 3))
    p.extend(("mix", i, "dve") for i in (0, 1))
    p.extend(("lora", i, "act") for i in (2, 3))
    mixed = {0: [], 1: [("dech", 2, "act")], 2: [("gateh", 2, "act")], 3: [("w", 4, "act"), ("r", 4, "act")],
             4: [("g", 4, "act"), ("k", 4, "act"), ("vb", 4, "act")]}
    for n in range(NMIX):
        p.extend(("mix", 4 * n + i, "dve") for i in range(2 if n == 0 else 0, 4))
        for m in mixed[n]:
            add(*m)
    add("diag", 8, "dve")
    add("level", LEVELS * 4, "dve")
    add("kt", 4, "act")
    p.extend(("kv", n, "dve") for n in KV_ORDER)
    add("y", 4, "dve")
    for f in (0, 1):
        p.extend(("zt", 2 * f + i, "act") for i in (0, 1))
        if f == 0:
            add("ob", 2, "dve")
    p.append(("ob", 2, "dve"))
    p.extend(("ln3", i, "dve") for i in (0, 1))
    p.append(("ob", 3, "dve"))
    ffn(3)
    return p


PLAN = psum_plan()
NTH = {(kind, i): n for n, (kind, i, _) in enumerate(PLAN)}
_seen = {"act": 0, "dve": 0}
RANK = []
for _, _, _who in PLAN:
    _seen[_who] += 1
    RANK.append(_seen[_who])


def build(nc, x_in, w_at, cs, b_vec, b_mat, ffn_w, consts, out, stop_after=None):
    f32, bf16, i32, f32r = mybir.dt.float32, mybir.dt.bfloat16, mybir.dt.int32, mybir.dt.float32r
    ALU, ACT, AX = mybir.AluOpType, mybir.ActivationFunctionType, mybir.AxisListType
    S8 = 1.0 / 127.0
    ctx = ExitStack()
    with ctx:
        def sb(name, shape, dt=f32):
            return ctx.enter_context(nc.sbuf_tensor(name, shape, dt))

        sems = []

        def sem(name):
            s = ctx.enter_context(nc.semaphore(name))
            sems.append(s)
            return s

        xres = sb("xres", [128, NT, D])
        xT = sb("xT", [128, NC, 1 + T])
        attn = sb("attn", [128, NT, HG, 128])
        xn = attn[:, :, :, :].rearrange("p i g t -> p i (g t)")[:, :, 0:D]
        spare = attn[:, :, :, :].rearrange("p i g t -> p i (g t)")[:, :, D:2 * D]
        rope = sb("rope", [128, 2, T])
        wqkv = sb("wqkv", [128, NC, 3 * D])
        wo = sb("wo", [128, NG, D])
        wgu = sb("wgu", [128, NC, 2 * HID], f32r)
        wd = sb("wd", [128, NM, D], f32r)
        wide_row = sb("wide_row", [128, 128])
        wide_flag = sb("wide_flag", [128, 1], i32)
        bm = sb("bm", [128, NC, 4 * D])
        mw1 = sb("mw1", [128, NC, NMIX * DMIX])
        mw2 = sb("mw2", [128, NMIX, D])
        low1 = sb("low1", [128, NC, 2 * DLOW])
        low2 = sb("low2", [128, 2, D])
        lng = sb("lng", [128, 2, D])
        vec = sb("vec", [128, 8, NC])
        ident = sb("ident", [128, 128])
        identb = sb("identb", [128, 128], bf16)
        causal = sb("causal", [128, 128], bf16)
        sumT = sb("sumT", [128, 2, HALF])
        recip = sb("recip", [128, 2, HALF // 32])
        lmask = sb("lmask", [128, LEVELS, 64], i32)
        dmask = sb("dmask", [128, 128], i32)
        half_neg = sb("half_neg", [128, 8])
        stats = sb("stats", [128, NT, 6])
        mv = sb("mv", [128, NT, 2])
        rstd = sb("rstd", [128, NT])
        mxp = sb("mxp", [128, 2, HG, 12])
        augf = sb("augf", [128, HG * NT])
        aug = sb("aug", [128, 3, HG, NT], bf16)
        augT = sb("augT", [96, 2, 128], bf16)
        gst = sb("gst", [128, 8, 6])
        gmv = sb("gmv", [128, 2, 8, 2])
        grs = sb("grs", [128, 2, 8])

        ARENA = 27 * 1024
        ARENA_AT = -(-nc.sbuf_base // 32) * 32
        arena = sb("arena", [128, ARENA])
        at = [0]

        def take(n, dt=f32, first=None):
            if first is not None:
                at[0] = first
            a = arena[:, at[0]:at[0] + n]
            at[0] += n
            assert at[0] <= ARENA, at[0]
            return a if dt == f32 else a.bitcast(dt)

        qst = take(8192, bf16, 0).rearrange("p (h t) -> p h t", h=NH)
        kst = take(8192, bf16).rearrange("p (h t) -> p h t", h=NH)
        ptf = take(6144)
        pt = ptf.rearrange("p (u h t) -> p u h t", u=3, h=HG)
        spl = ptf.bitcast(bf16).rearrange("p (m q s t) -> p m q s t", m=2, q=2, s=3)
        vp = take(4096).rearrange("p (i h d) -> p i h d", i=NT, h=NH)
        rden = take(1024).rearrange("p (f t) -> p f t", f=2)
        ta = [spare[:, 2 * k:2 * k + 2, :] for k in range(4)]
        turned_half = [rden[:, k, :].rearrange("p (a n) -> p a n", a=2) for k in (0, 1)]

        def part(name, shape):
            n = shape[1] * shape[2]
            a = nc.alloc_sbuf_tensor_at(name, shape, f32r, offset=ARENA_AT + 4 * at[0])
            at[0] += n
            assert at[0] <= ARENA, at[0]
            return a

        at[0] = 0
        hh = part("hh", [128, NM, T])
        hl = part("hl", [128, NM, T])
        xh = part("xh", [128, NC, T])
        xl = part("xl", [128, NC, T])
        WLOW_AT = at[0]
        wlow = part("wlow", [128, 1, 2 * NC * HID + NM * D])
        wgul = wlow[:, 0, 0:2 * NC * HID].rearrange("p (c n) -> p c n", c=NC)
        wdl = wlow[:, 0, 2 * NC * HID:].rearrange("p (m n) -> p m n", m=NM)
        tb = take(1024).rearrange("p (f t) -> p f t", f=2)
        ub = take(1024).rearrange("p (f t) -> p f t", f=2)
        hb = take(1024).rearrange("p (f t) -> p f t", f=2)

        def ct(a):
            return a.rearrange("p (c t) -> p c t", c=NC)

        xx_f = take(2048, f32, 0)
        xx, zT = ct(xx_f), ct(xx_f)
        xxx_f = take(2048)
        xxx, kn = ct(xxx_f), xxx_f.rearrange("p (c n i) -> p c n i", c=NC, n=NT)
        lora_f = take(2048)
        lora, S = ct(lora_f), lora_f[:, 0:1024].rearrange("p (c n j) -> p c n j", c=NC, n=NT)
        xf_f = take(4096)
        xf = xf_f.rearrange("p (b c t) -> p b c t", b=2, c=NC)
        A = xf_f.rearrange("p (c n h t) -> p c n h t", c=NC, n=NT, h=2)
        th = take(1024)
        wdec = ct(take(2048))
        kk = ct(take(2048))
        ku = ct(take(2048))
        tot = ct(take(2048))
        vt = take(2048).rearrange("p (i n) -> p i n", i=NT)
        gt = take(2048).rearrange("p (i n) -> p i n", i=NT)
        qd = take(4096).rearrange("p (c h t) -> p c h t", c=NC, h=2)

        parts = nc.dram_tensor("parts", (2, 2, 3, DH, NH // 2, T), bf16).ap()
        wlow_dram = nc.dram_tensor("wlow_dram", (128, 2 * NC * HID + NM * D), f32).ap()
        PB = [ctx.enter_context(nc.psum_tensor(f"PB{i}", [128, 512], f32)) for i in range(8)]

        s_w = sem("weights_loaded")
        s_cast = sem("weights_cast")
        s_zero = sem("consts_zeroed")
        s_split = sem("weights_split")
        s_low = sem("weights_low_stored")
        s_flag = sem("flag_moved")
        filled = sem("psum_filled")
        act_emptied = sem("act_emptied")
        dve_emptied = sem("dve_emptied")
        x_loaded = [sem(f"x_loaded{i}") for i in (0, 1)]
        arena_set = sem("arena_set")
        ln_stat = [sem(f"ln_stat{k}") for k in range(4)]
        ln_aggr = [sem(f"ln_aggr{k}") for k in range(4)]
        ln_eps = [sem(f"ln_eps{k}") for k in range(4)]
        ln_rstd = [sem(f"ln_rstd{k}") for k in range(4)]
        ln_out = [sem(f"ln_out{k}") for k in range(4)]
        resid = [sem(f"resid{k}") for k in range(4)]
        roped = sem("roped")
        rot_chain = sem("rot_chain")
        hi_done = sem("hi_done")
        rem_done = sem("rem_done")
        mid_done = sem("mid_done")
        lo_done = sem("lo_done")
        q_out = [sem(f"q_out{m}") for m in (0, 1)]
        k_out = [sem(f"k_out{m}") for m in (0, 1)]
        stacked = [sem(f"stacked{m}") for m in (0, 1)]
        aug_chain = sem("aug_chain")
        aug_loaded = [sem(f"aug_loaded{g}") for g in range(NG)]
        masked = sem("masked")
        pv_units = sem("pv_units")
        pv_copied = sem("pv_copied")
        den_chain = sem("den_chain")
        attn_normed = sem("attn_normed")
        tanh_done = [sem("tanh_done1"), sem("tanh_done3")]
        gate_done = [sem("gate_done1"), sem("gate_done3")]
        x_high = [sem("x_high1"), sem("x_high3")]
        h_high = [sem("h_high1"), sem("h_high3")]
        h_low = [sem("h_low1"), sem("h_low3")]
        wlow_loaded = [sem("wlow_loaded1"), sem("wlow_loaded3")]
        xx_done = sem("xx_done")
        xxx_done = sem("xxx_done")
        mix_added = sem("mix_added")
        decay_exp = sem("decay_exp")
        qd_zeroed = sem("qd_zeroed")
        a_zeroed = sem("a_zeroed")
        ku_done = sem("ku_done")
        tot_done = sem("tot_done")
        q_updated = sem("q_updated")
        k_updated = sem("k_updated")
        s_zeroed = sem("s_zeroed")
        s_chain = sem("s_chain")
        gn_stat = sem("gn_stat")
        gn_aggr = sem("gn_aggr")
        gn_eps = sem("gn_eps")
        gn_rstd = sem("gn_rstd")
        gn_lng = sem("gn_lng")
        gn_chain = sem("gn_chain")
        stored = sem("stored")

        emptied = {"act": act_emptied, "dve": dve_emptied}

        def bank(kind, i):
            return PB[NTH[kind, i] % RING]

        def wait_filled(eng, kind, i):
            eng.wait_ge(filled, NTH[kind, i] + 1)

        def wait_emptied(eng, kind, i):
            n = NTH[kind, i]
            eng.wait_ge(emptied[PLAN[n][2]], RANK[n])

        def wait_bank(eng, kind, i):
            n = NTH[kind, i] - RING
            if n >= 0:
                eng.wait_ge(emptied[PLAN[n][2]], RANK[n])

        NW = 2 * NC * HID + NM * D
        WF_AT = 22 * 1024
        with nc.Block() as block:
            @block.sync
            def _(sp):
                def load(dst, src):
                    sp.dma_start(dst, src).then_inc(s_w, 16)
                for k, w in enumerate(w_at[0:3]):
                    load(wqkv[:, :, D * k:D * k + D], w.rearrange("(c p) n -> p c n", p=128))
                sp.wait_ge(s_zero, 7)
                for h in range(NH):
                    load(wo[32 * (h % HG):32 * (h % HG) + DH, h // HG, :], w_at[3][DH * h:DH * h + DH, :])
                load(rope[:, 0, :], cs[0])
                load(rope[:, 1, :], cs[1])
                for k in range(4):
                    load(bm[:, :, D * k:D * k + D], b_mat[k].rearrange("(c p) n -> p c n", p=128))
                load(mw1[:, :, :], b_mat[4].rearrange("(c p) n -> p c n", p=128))
                for f in range(NMIX):
                    r = 32 * f if f < 4 else 96
                    load(mw2[r:r + 32, f, :], b_mat[5][f, :, :])
                load(low1[:, :, 0:DLOW], b_mat[6].rearrange("(c p) n -> p c n", p=128))
                load(low1[:, :, DLOW:2 * DLOW], b_mat[8].rearrange("(c p) n -> p c n", p=128))
                load(low2[0:DLOW, 0, :], b_mat[7])
                load(low2[DLOW:128, 1, :], b_mat[9])
                load(vec[:, :, :], b_vec[0].rearrange("p (k c) -> p k c", c=NC))
                for k in range(2):
                    load(lng[:, k, :], b_vec[1 + k].partition_broadcast(128))
                load(ident[:, :], consts[0][:, 0:128])
                load(arena[:, 8192:8320], consts[0][:, 128:256])
                load(lmask[:, :, :], consts[1][:, 0:448].rearrange("p (l t) -> p l t", l=LEVELS))
                load(dmask[:, :], consts[1][:, 448:576])
                ai = arena[:, :].bitcast(i32)
                load(ai[:, 0:1536].rearrange("p (c n) -> p c n", c=NC), ffn_w[0].rearrange("(c p) n -> p c n", p=128))
                load(ai[:, 1536:3072].rearrange("p (c n) -> p c n", c=NC), ffn_w[1].rearrange("(c p) n -> p c n", p=128))
                load(ai[:, 3072:4608].rearrange("p (m n) -> p m n", m=NM), ffn_w[2].rearrange("(m p) n -> p m n", p=128))
                sp.wait_ge(s_split, 6)
                sp.dma_start(wlow_dram, wlow[:, 0, :].bitcast(f32)).then_inc(s_low, 16)
                sp.wait_ge(s_split, 8)
                sp.dma_start(wide_row[0:1, :], arena[:, WF_AT - 1:WF_AT]).then_inc(s_flag, 16)
                sp.wait_ge(s_low, 16)
            NLOAD = 3 + NH + 2 + 4 + 1 + NMIX + 4 + 1 + 2 + 4 + 3

            @block.gpsimd
            def _(pool):
                pool.memset(wo[:, :, :], 0.0).then_inc(s_zero, 1)
                pool.memset(mw2[:, :, :], 0.0).then_inc(s_zero, 1)
                pool.memset(low2[:, :, :], 0.0).then_inc(s_zero, 1)
                pool.memset(half_neg[:, :], -0.5).then_inc(s_zero, 1)
                pool.memset(xT[:, :, 0:1], 0.0).then_inc(s_zero, 1)
                pool.memset(arena[:, 10000:10001], 0.0).then_inc(s_zero, 1)
                pool.memset(augf[:, :], 0.0).then_inc(s_zero, 1)

            @block.vector
            def _(dve):
                dve.wait_ge(s_w, 16 * NLOAD)
                ai = arena[:, :].bitcast(i32)
                wf = arena[:, WF_AT:WF_AT + NW]
                gate, up = (wf[:, NC * HID * r:NC * HID * (r + 1)].rearrange("p (c n) -> p c n", c=NC) for r in (0, 1))
                down = wf[:, 2 * NC * HID:].rearrange("p (m n) -> p m n", m=NM)
                dve.tensor_copy(wf, ai[:, 0:NW]).then_inc(s_split, 1)
                dve.wait_ge(s_split, 1)
                dve.tensor_copy(wgu[:, :, 0:HID], gate)
                dve.tensor_copy(wgu[:, :, HID:2 * HID], up)
                dve.tensor_copy(wd[:, :, :], down).then_inc(s_split, 1)
                dve.wait_ge(s_split, 2)
                dve.tensor_tensor(wgul[:, :, 0:HID], gate, wgu[:, :, 0:HID].bitcast(f32), ALU.subtract).then_inc(s_split, 1)
                dve.tensor_tensor(wgul[:, :, HID:2 * HID], up, wgu[:, :, HID:2 * HID].bitcast(f32),
                                  ALU.subtract).then_inc(s_split, 1)
                dve.tensor_tensor(wdl, down, wd[:, :, :].bitcast(f32), ALU.subtract).then_inc(s_split, 1)
                dve.wait_ge(s_split, 5)
                dve.tensor_scalar(wf, wlow[:, 0, :].bitcast(f32), 0.0, None, ALU.not_equal).then_inc(s_split, 1)
                dve.wait_ge(s_split, 6)
                dve.reduce_max(arena[:, WF_AT - 1:WF_AT], wf, axis=AX.X).then_inc(s_split, 2)
                dve.wait_ge(s_flag, 16)
                dve.reduce_max(arena[0:1, WF_AT:WF_AT + 1], wide_row[0:1, :], axis=AX.X).then_inc(s_split, 1)
                dve.wait_ge(s_split, 9)
                dve.tensor_copy(wide_flag[0:1, :], arena[0:1, WF_AT:WF_AT + 1])
                dve.tensor_copy(causal[:, :], arena[:, 8192:8320])
                dve.tensor_copy(identb[:, :], ident[:, :]).then_inc(s_cast, 1)

        with nc.Fori(0, NB) as b:
            with nc.Block() as block:
                @block.sync
                def _(sp):
                    xv = x_in[bass.ds(b, 1), :, :].rearrange("a (i p) c -> p (a i) c", p=128)
                    ov = out[bass.ds(b, 1), :, :].rearrange("a (i p) c -> p (a i) c", p=128)
                    for f in (0, 1):
                        sp.dma_start(xres[:, 4 * f:4 * f + 4, :], xv[:, 4 * f:4 * f + 4, :]).then_inc(x_loaded[f], 16)
                    for m in (0, 1):
                        heads = slice(8 * m, 8 * m + 8)
                        for q in (0, 1):
                            for which, done in enumerate((hi_done, mid_done, lo_done)):
                                sp.wait_ge(done, 4 * m + 3 + q)
                                sp.dma_start(parts[m, q, which, :, :, :].rearrange("d h t -> h d t"),
                                             spl[:, m, q, which, :]).then_inc((q_out, k_out)[q][m], 16)
                        sp.wait_ge(q_out[m], 48)
                        for run, (first, n) in enumerate(RUNS):
                            for blk in range(first, first + n):
                                sp.dma_start(qst[DH * blk:DH * blk + DH, heads, :],
                                             parts[m, 0, run, :, :, :]).then_inc(stacked[m], 16)
                        sp.wait_ge(k_out[m], 48)
                        for first, n in RUNS:
                            sp.dma_start(kst[DH * first:DH * (first + n), heads, :],
                                         parts[m, 1, 0:n, :, :, :].rearrange("s d h t -> (s d) h t")
                                         ).then_inc(stacked[m], 16)
                    for g in range(NG):
                        wait_emptied(sp, "aug", g)
                        for r in range(3):
                            sp.dma_start(qst[AUG + r:AUG + r + 1, HG * g:HG * g + HG, :],
                                         augT[32 * r:32 * r + 32, g % 2, :]).then_inc(aug_loaded[g], 16)
                    wide = sp.alloc_register(name="wide_sp")
                    sp.reg_load(wide, wide_flag[0:1, 0:1])
                    with sp.If_ne(wide, 0):
                        for s in (0, 1):
                            sp.wait_ge(resid[2 * s], 3)
                            sp.dma_start(wlow[:, 0, :].bitcast(f32), wlow_dram).then_inc(wlow_loaded[s], 16)
                    for f in (0, 1):
                        k = {1: 0, 2: 1, 3: 2}.get(stop_after, 3)
                        sp.wait_ge(resid[k], 2 * f + 2)
                        sp.dma_start(ov[:, 4 * f:4 * f + 4, :], xres[:, 4 * f:4 * f + 4, :]).then_inc(stored, 16)
                    sp.wait_ge(stored, 32)

                @block.gpsimd
                def _(pool):
                    pool.memset(vp[:, :, :, DH:2 * DH], 0.0).then_inc(arena_set, 1)
                    pool.wait_ge(arena_set, 1)
                    pool.memset(vp[:, :, :, DH:DH + 1], 1.0).then_inc(arena_set, 1)
                    pool.wait_ge(arena_set, 2)

                    def ln_scale(k, f):
                        pool.wait_ge(ln_aggr[k], 4 * f + 4)
                        v = mv[:, 4 * f:4 * f + 4, 1:2].rearrange("p i a -> p (i a)")
                        pool.tensor_scalar(v, v, 1e-5, 1.0, ALU.add, ALU.mult).then_inc(ln_eps[k], 1)
                        pool.wait_ge(ln_eps[k], f + 1)
                        pool.tensor_tensor(rstd[:, 4 * f:4 * f + 4], v, half_neg[:, 0:4], ALU.pow).then_inc(ln_rstd[k], 1)

                    ln_scale(0, 0)
                    ln_scale(0, 1)

                    def low(e):
                        m, f, q = e // 4, e // 2 % 2, e % 2
                        pool.wait_ge(mid_done, e + 1)
                        cols = slice(HALF * f, HALF * f + HALF)
                        pool.tensor_tensor(spl[:, m, q, 2, cols].rearrange("p (a n) -> p a n", a=2), ta[e % 4],
                                           spl[:, m, q, 1, cols].rearrange("p (a n) -> p a n", a=2),
                                           ALU.subtract).then_inc(lo_done, 1)

                    for e in range(8):
                        m, f, q = e // 4, e // 2 % 2, e % 2
                        pool.wait_ge(hi_done, e + 1)
                        pool.tensor_tensor(ta[e % 4], ta[e % 4],
                                           spl[:, m, q, 0, HALF * f:HALF * f + HALF].rearrange("p (a n) -> p a n", a=2),
                                           ALU.subtract).then_inc(rem_done, 1)
                        if e % 4:
                            low(e - 1)
                        if e == 3:
                            low(3)
                    low(7)
                    pool.wait_ge(lo_done, 8)
                    pool.memset(kst[AUG:AUG + 3, :, :], 1.0).then_inc(arena_set, 1)
                    pool.wait_ge(arena_set, 3)

                    def ffn(s):
                        for e in range(2 * NM):
                            f, m = e // NM, e % NM
                            cols = slice(HALF * f, HALF * f + HALF)
                            pool.wait_ge(h_high[s], e + 1)
                            pool.tensor_tensor(hl[:, m, cols], hb[:, e % 2, :], hh[:, m, cols].bitcast(f32),
                                               ALU.subtract).then_inc(h_low[s], 1)

                    def over_sums(g):
                        for f in (0, 1):
                            pool.wait_ge(den_chain, 8 * g + 7 + f)
                            pool.wait_ge(pv_copied, 2 * g + f + 1)
                            a = attn[:, 4 * f:4 * f + 4, g, :]
                            pool.tensor_tensor(a, a, sumT[:, f, :].rearrange("p (i t) -> p i t", i=4),
                                               ALU.mult).then_inc(attn_normed, 1)

                    for U in DIAG_UNITS:
                        g, u = U // len(UNITS), U % len(UNITS)
                        wait_emptied(pool, "score", HG * U + HG - 1)
                        a = pt[:, U % 3, :, 0:128]
                        pool.affine_select(out=a, in_=a, compare_op=ALU.is_ge, fill=0.0, base=0,
                                           pattern=[[0, HG], [1, 128]], channel_multiplier=-1).then_inc(masked, 1)
                        if g and u == NORM_AT:
                            over_sums(g - 1)
                    over_sums(NG - 1)
                    ln_scale(1, 0)
                    ln_scale(1, 1)
                    ffn(0)
                    ln_scale(2, 0)
                    ln_scale(2, 1)
                    pool.memset(qd[0:64, :, 1, :], 0.0).then_inc(qd_zeroed, 1)
                    pool.wait_ge(qd_zeroed, 1)
                    pool.memset(qd[64:128, :, 0, :], 0.0).then_inc(qd_zeroed, 1)
                    pool.wait_ge(qd_zeroed, 2)
                    for n in range(4 * NMIX):
                        c, f = n % 2, n // 2 % 2
                        wait_emptied(pool, "mix", n)
                        a = xf[:, n // 4 % 2, c, HALF * f:HALF * f + HALF]
                        pool.tensor_tensor(a, a, xT[:, c, 1 + HALF * f:1 + HALF * f + HALF], ALU.add).then_inc(mix_added, 1)
                    wait_emptied(pool, "w", 3)
                    src, at_, n = wdec, 0, 512
                    for l in range(LEVELS):
                        if l:
                            pool.wait_ge(tot_done, l)
                        dst = tot[:, :, at_:at_ + n]
                        s2 = src.rearrange("p c (n a) -> p c n a", a=2)
                        pool.tensor_tensor(dst, s2[:, :, :, 0], s2[:, :, :, 1], ALU.mult).then_inc(tot_done, 1)
                        src, at_, n = dst, at_ + n, n // 2
                    wait_filled(pool, "vb", 3)
                    pool.memset(A, 0.0).then_inc(a_zeroed, 1)
                    pool.memset(S[:, :, 0, :], 0.0).then_inc(s_zeroed, 1)
                    for l in range(LEVELS):
                        m = 1 << l
                        tm = wdec if l == 0 else tot[:, :, 1024 - 1024 // (m // 2) // 1:1024 - 1024 // m // 1 + 0]
                        for c in range(NC):
                            wait_filled(pool, "level", 4 * l + 2 * c + 1)
                            kv = kk[:, c, :].rearrange("p (n a m) -> p n a m", a=2, m=m)[:, :, 0, :]
                            w = tm[:, c, :].rearrange("p (n a) -> p n a", a=2)[:, :, 1:2].broadcast_to([128, 512 // m, m])
                            if l:
                                pool.wait_ge(k_updated, 2 * (l - 1) + c + 1)
                            pool.tensor_tensor(kv, kv, w, ALU.mult).then_inc(k_updated, 1)
                    for n in range(4):
                        pool.wait_ge(gn_aggr, 8 * n + 8)
                        v = gmv[:, n % 2, :, 1:2].rearrange("p i a -> p (i a)")
                        pool.tensor_scalar(v, v, 0.00064, 1.0, ALU.add, ALU.mult).then_inc(gn_eps, 1)
                        pool.wait_ge(gn_eps, n + 1)
                        pool.tensor_tensor(grs[:, n % 2, :], v, half_neg[:, :], ALU.pow).then_inc(gn_rstd, 1)
                        pool.wait_ge(gn_rstd, n + 1)
                        pool.wait_ge(gn_lng, n + 1)
                        z = xn[:, 2 * n:2 * n + 2, :]
                        zh = z.rearrange("p i (h j) -> p i h j", j=WH)
                        r = grs[:, n % 2, :].rearrange("p (i h a) -> p i h a", i=2, a=1).broadcast_to([128, 2, 4, WH])
                        pool.tensor_tensor(zh, zh, r, ALU.mult).then_inc(gn_chain, 1)
                        pool.wait_ge(gn_chain, 3 * n + 1)
                        pool.tensor_tensor(z, z, lng[:, 1:2, :].broadcast_to([128, 2, D]), ALU.add).then_inc(gn_chain, 1)
                        pool.wait_ge(gn_chain, 3 * n + 2)
                        pool.tensor_tensor(z, z, gt[:, 2 * n:2 * n + 2, :], ALU.mult).then_inc(gn_chain, 1)
                    ln_scale(3, 0)
                    ln_scale(3, 1)
                    ffn(1)

                @block.scalar
                def _(act):
                    def copy_xT(k, ns=range(4)):
                        for n in ns:
                            f, c = n // 2, n % 2
                            wait_filled(act, f"ln{k}", n)
                            act.activation(xT[:, c, 1 + HALF * f:1 + HALF * f + HALF], bank(f"ln{k}", n)[:, :],
                                           ACT.Copy).then_inc(act_emptied, 1)

                    copy_xT(0)

                    def mid(e):
                        act.wait_ge(rem_done, e + 1)
                        m, f, q = e // 4, e // 2 % 2, e % 2
                        act.activation(spl[:, m, q, 1, HALF * f:HALF * f + HALF].rearrange("p (a n) -> p a n", a=2),
                                       ta[e % 4], ACT.Copy).then_inc(mid_done, 1)

                    def high(e):
                        m, f, q = e // 4, e // 2 % 2, e % 2
                        act.wait_ge(roped, e + 1)
                        act.activation(spl[:, m, q, 0, HALF * f:HALF * f + HALF].rearrange("p (a n) -> p a n", a=2),
                                       ta[e % 4], ACT.Copy).then_inc(hi_done, 1)
                        if e % 4:
                            mid(e - 1)

                    def v_out(n):
                        wait_filled(act, "v", n)
                        act.activation(vp[:, 2 * n:2 * n + 2, :, 0:DH],
                                       bank("v", n)[:, :].rearrange("p (i h d) -> p i h d", i=2, h=NH),
                                       ACT.Copy).then_inc(act_emptied, 1)

                    act.wait_ge(arena_set, 2)
                    for e in range(4):
                        high(e)
                    mid(3)
                    for n in range(4):
                        v_out(n)
                    for e in range(4, 8):
                        high(e)
                    mid(7)
                    def pv_out(g):
                        act.wait_ge(pv_units, (g + 1) * len(UNITS))
                        for f in (0, 1):
                            act.activation(attn[:, 4 * f:4 * f + 4, g, :],
                                           PB[6 + f][:, :].rearrange("p (i t) -> p i t", i=4),
                                           ACT.Copy).then_inc(pv_copied, 1)

                    for m in (0, 1):
                        act.wait_ge(q_out[m], 48)
                        act.wait_ge(k_out[m], 48)
                    for t in range(NSC):
                        U, h = t // HG, t % HG
                        j, f = UNITS[U % len(UNITS)]
                        n = HALF * (f + 1) - max(HALF * f, 128 * j)
                        wait_filled(act, "score", t)
                        if h == 0 and U >= 3:
                            act.wait_ge(pv_units, U - 2)
                        act.activation(pt[:, U % 3, h, 0:n], bank("score", t)[:, 0:n], ACT.Exp,
                                       scale=DH ** -0.5).then_inc(act_emptied, 1)
                        if t >= NPC and t % NPC == 2 * HG - 1:
                            pv_out(t // NPC - 1)
                    pv_out(NG - 1)

                    def ffn(k, s):
                        def x_parts(ns):
                            for n in ns:
                                f, c = n // 2, n % 2
                                wait_filled(act, f"ln{k}", n)
                                act.activation(xh[:, c, HALF * f:HALF * f + HALF], bank(f"ln{k}", n)[:, :],
                                               ACT.Copy).then_inc(x_high[s], 1)

                        def h_part(e):
                            f, m = e // NM, e % NM
                            wait_emptied(act, f"gu{k}", 2 * e + 1)
                            act.activation(hh[:, m, HALF * f:HALF * f + HALF], hb[:, e % 2, :],
                                           ACT.Copy).then_inc(h_high[s], 1)

                        x_parts((0, 1))
                        for e in range(2 * NM):
                            if e == 2:
                                x_parts((2, 3))
                            wait_filled(act, f"gu{k}", 2 * e)
                            if e >= 2:
                                act.wait_ge(gate_done[s], e - 1)
                            act.activation(tb[:, e % 2, :], bank(f"gu{k}", 2 * e)[:, :], ACT.Tanh,
                                           scale=0.5 * S8).then_inc(tanh_done[s], 1)
                            if e:
                                h_part(e - 1)
                        h_part(2 * NM - 1)

                    ffn(1, 0)
                    for n in range(4):
                        l, f = n % 2, n // 2
                        if l == 0:
                            copy_xT(2, (n, n + 1))
                        wait_filled(act, "lora", n)
                        act.activation(lora[:, l, HALF * f:HALF * f + HALF], bank("lora", n)[:, :],
                                       ACT.Tanh).then_inc(act_emptied, 1)
                    for kind, r in (("dech", 64), ("gateh", 0)):
                        for f in (0, 1):
                            wait_filled(act, kind, f)
                            act.activation(th[r:r + 64, HALF * f:HALF * f + HALF], bank(kind, f)[r:r + 64, :],
                                           ACT.Tanh).then_inc(act_emptied, 1)
                    for n in range(4):
                        c, f = n % 2, n // 2
                        w = wdec[:, c, HALF * f:HALF * f + HALF]
                        wait_filled(act, "w", n)
                        act.activation(w, bank("w", n)[:, :], ACT.Exp, bias=vec[:, 6, c:c + 1]).then_inc(decay_exp, 1)
                        act.wait_ge(decay_exp, n + 1)
                        act.activation(w, w, ACT.Exp, scale=-1.0).then_inc(act_emptied, 1)
                    act.wait_ge(qd_zeroed, 2)
                    for n in range(4):
                        c, f = n % 2, n // 2
                        wait_filled(act, "r", n)
                        act.activation(qd[0:64, c, 0, HALF * f:HALF * f + HALF], bank("r", n)[0:64, :], ACT.Copy)
                        act.activation(qd[64:128, c, 1, HALF * f:HALF * f + HALF], bank("r", n)[64:128, :],
                                       ACT.Copy).then_inc(act_emptied, 1)
                    for n in range(4):
                        wait_filled(act, "g", n)
                        act.activation(gt[:, 2 * n:2 * n + 2, :], bank("g", n)[:, :].rearrange("p (i n) -> p i n", i=2),
                                       ACT.Copy).then_inc(act_emptied, 1)
                    for n in range(4):
                        c, f = n % 2, n // 2
                        wait_filled(act, "k", n)
                        act.activation(kk[:, c, HALF * f:HALF * f + HALF], bank("k", n)[:, :],
                                       ACT.Copy).then_inc(act_emptied, 1)
                    for n in range(4):
                        wait_filled(act, "vb", n)
                        act.activation(vt[:, 2 * n:2 * n + 2, :], bank("vb", n)[:, :].rearrange("p (i n) -> p i n", i=2),
                                       ACT.Copy).then_inc(act_emptied, 1)
                    for n in range(4):
                        wait_filled(act, "kt", n)
                        act.activation(kn[:, n // 2, 4 * (n % 2):4 * (n % 2) + 4, :],
                                       bank("kt", n)[:, :].rearrange("p (n i) -> p n i", n=4),
                                       ACT.Copy).then_inc(act_emptied, 1)
                    for n in range(4):
                        f, c = n // 2, n % 2
                        wait_filled(act, "zt", n)
                        act.activation(zT[:, c, HALF * f:HALF * f + HALF], bank("zt", n)[:, :],
                                       ACT.Copy).then_inc(act_emptied, 1)
                    ffn(3, 1)

                @block.vector
                def _(dve):
                    def ln_tile(k, i):
                        dve.bn_stats(stats[:, i, :], xres[:, i, :]).then_inc(ln_stat[k], 1)

                    def ln_half(k, f):
                        dve.wait_ge(ln_stat[k], 4 * f + 4)
                        for i in range(4 * f, 4 * f + 4):
                            dve.bn_aggr(mv[:, i, :], stats[:, i, :]).then_inc(ln_aggr[k], 1)
                        dve.wait_ge(ln_aggr[k], 4 * f + 4)
                        dve.wait_ge(ln_rstd[k], f + 1)
                        for i in range(4 * f, 4 * f + 4):
                            dve.tensor_scalar(xn[:, i, :], xres[:, i, :], mv[:, i, 0:1], rstd[:, i:i + 1],
                                              ALU.subtract, ALU.mult).then_inc(ln_out[k], 1)

                    def residual(kind, n, s, scale=None):
                        wait_filled(dve, kind, n)
                        a = xres[:, 2 * n:2 * n + 2, :].rearrange("p i c -> p (i c)")
                        if scale is None:
                            dve.tensor_tensor(a, bank(kind, n)[:, :], a, ALU.add).then_inc(dve_emptied, 1)
                        else:
                            dve.scalar_tensor_tensor(out=a, in0=bank(kind, n)[:, :], scalar=scale, in1=a,
                                                     op0=ALU.mult, op1=ALU.add).then_inc(dve_emptied, 1)
                        dve.wait_ge(dve_emptied, RANK[NTH[kind, n]])
                        dve.engine_nop().then_inc(resid[s], 1)
                        if s < 3:
                            ln_tile(s + 1, 2 * n)
                            ln_tile(s + 1, 2 * n + 1)
                            if n % 2:
                                ln_half(s + 1, n // 2)

                    for f in (0, 1):
                        dve.wait_ge(x_loaded[f], 16)
                        for i in range(4 * f, 4 * f + 4):
                            ln_tile(0, i)
                        ln_half(0, f)

                    def rotary(e):
                        f = e // 2 % 2
                        ps = bank("qk", e)[:, :].rearrange("p (a n) -> p a n", a=2)
                        cos, sin = (rope[:, r, HALF * f:HALF * f + HALF].rearrange("p (a n) -> p a n", a=2) for r in (0, 1))
                        main, turned = ta[e % 4], turned_half[e % 2]
                        if e >= 4:
                            dve.wait_ge(lo_done, e - 3)
                        if e >= 2:
                            dve.wait_ge(roped, e - 1)
                        wait_filled(dve, "qk", e)
                        dve.stream_shuffle(turned, ps, ROTATE).then_inc(rot_chain, 1)
                        dve.tensor_tensor(main, ps, cos, ALU.mult).then_inc(dve_emptied, 1)
                        dve.wait_ge(rot_chain, 2 * e + 1)
                        dve.tensor_tensor(turned, turned, sin, ALU.mult).then_inc(rot_chain, 1)
                        wait_emptied(dve, "qk", e)
                        dve.wait_ge(rot_chain, 2 * e + 2)
                        dve.tensor_tensor(main, main, turned, ALU.add).then_inc(roped, 1)

                    for e in range(8):
                        rotary(e)

                    def max_piece(g, k):
                        h, (i, s0, n, col) = max_item_of(k)
                        wait_filled(dve, "max", g * NPC + k)
                        dve.reduce_max(mxp[:, g % 2, h, col:col + 1], bank("max", g * NPC + k)[:, 0:n],
                                       axis=AX.X).then_inc(dve_emptied, 1)

                    def den(g, step):
                        for f in (0, 1):
                            if step == 0:
                                dve.wait_ge(pv_copied, 2 * g + f + 1)
                                if g:
                                    dve.wait_ge(attn_normed, 2 * g)
                                last = dve.transpose(sumT[:, f, :].rearrange("p (i t) -> p i t", i=4),
                                                     attn[:, 4 * f:4 * f + 4, g, :])
                            else:
                                dve.wait_ge(den_chain, 8 * g + 2 * step - 1 + f)
                            blocks = sumT[:, f, :].rearrange("p (a n) -> p a n", n=32)
                            one = recip[:, f, :].rearrange("p (a n) -> p a n", n=1)
                            wide = rden[:, f, :].rearrange("p (a n) -> p a n", n=32)
                            if step == 1:
                                last = dve.reciprocal(one, blocks[:, :, DH:DH + 1])
                            if step == 2:
                                last = dve.tensor_copy(wide, one.broadcast_to([128, HALF // 32, 32]))
                            if step == 3:
                                last = dve.transpose(sumT[:, f, :], rden[:, f, :])
                            last.then_inc(den_chain, 1)

                    def aug_out(g):
                        wait_filled(dve, "aug", g)
                        if g >= 2:
                            dve.wait_ge(aug_loaded[g - 2], 48)
                        dve.tensor_copy(augT[:, g % 2, :], bank("aug", g)[0:96, 0:64].bitcast(bf16)).then_inc(dve_emptied, 1)

                    for g in range(NG):
                        for k in range(NPC):
                            max_piece(g, k)
                            if g and k == AUG_AT:
                                aug_out(g - 1)
                            if g >= 2 and 0 <= k - DEN_AT < 4:
                                den(g - 2, k - DEN_AT)
                        dve.wait_ge(dve_emptied, RANK[NTH["max", g * NPC + NPC - 1]])
                        mg, af = mxp[:, g % 2, :, :], augf[:, :].rearrange("p (h i) -> p h i", h=HG)
                        dve.tensor_tensor(mg[:, :, 4:8], mg[:, :, 4:8], mg[:, :, 8:12], ALU.max).then_inc(aug_chain, 1)
                        dve.wait_ge(aug_chain, 6 * g + 1)
                        dve.tensor_scalar(aug[:, 0, :, :], mg[:, :, 0:8], -1.0, None, ALU.mult).then_inc(aug_chain, 1)
                        dve.wait_ge(aug_chain, 6 * g + 2)
                        dve.scalar_tensor_tensor(out=af, in0=mg[:, :, 0:8], scalar=-1.0, in1=aug[:, 0, :, :],
                                                 op0=ALU.mult, op1=ALU.subtract).then_inc(aug_chain, 1)
                        dve.wait_ge(aug_chain, 6 * g + 3)
                        dve.tensor_copy(aug[:, 1, :, :], af).then_inc(aug_chain, 1)
                        dve.wait_ge(aug_chain, 6 * g + 4)
                        dve.tensor_tensor(af, af, aug[:, 1, :, :], ALU.subtract).then_inc(aug_chain, 1)
                        dve.wait_ge(aug_chain, 6 * g + 5)
                        dve.tensor_copy(aug[:, 2, :, :], af).then_inc(aug_chain, 1)
                    aug_out(NG - 1)
                    for g in (NG - 2, NG - 1):
                        for step in range(4):
                            den(g, step)
                    def x_low(k, s, ns):
                        for n in ns:
                            f, c = n // 2, n % 2
                            cols = slice(HALF * f, HALF * f + HALF)
                            dve.wait_ge(x_high[s], n + 1)
                            dve.tensor_tensor(xl[:, c, cols], bank(f"ln{k}", n)[:, :], xh[:, c, cols].bitcast(f32),
                                              ALU.subtract).then_inc(dve_emptied, 1)

                    for n in range(4):
                        if n == 3:
                            x_low(1, 0, (0, 1))
                        residual("o", n, 0)

                    def ffn(k, s):
                        def down(n):
                            residual(f"dn{k}", n, k, 0.5 * S8 * S8 * S8)

                        for e in range(2 * NM):
                            if e == 2:
                                x_low(k, s, (2, 3))
                            u = ub[:, e % 2, :]
                            dve.wait_ge(tanh_done[s], e + 1)
                            dve.scalar_tensor_tensor(out=u, in0=tb[:, e % 2, :], scalar=1.0,
                                                     in1=bank(f"gu{k}", 2 * e)[:, :], op0=ALU.add,
                                                     op1=ALU.mult).then_inc(dve_emptied, 1)
                            wait_filled(dve, f"gu{k}", 2 * e + 1)
                            dve.wait_ge(dve_emptied, RANK[NTH[f"gu{k}", 2 * e]])
                            if e >= 2:
                                dve.wait_ge(h_low[s], e - 1)
                            dve.tensor_tensor(hb[:, e % 2, :], bank(f"gu{k}", 2 * e + 1)[:, :], u,
                                              ALU.mult).then_inc(dve_emptied, 1)
                            dve.wait_ge(dve_emptied, RANK[NTH[f"gu{k}", 2 * e + 1]])
                            dve.engine_nop().then_inc(gate_done[s], 1)
                            if e == NM + DOWN_AT // 2:
                                down(0)
                        for n in ((1, 2) if k == 1 else (1, 2, 3)):
                            down(n)

                    ffn(1, 0)

                    def differences(n):
                        f, c = n // 2, n % 2
                        cols = slice(HALF * f, HALF * f + HALF)
                        now = xT[:, c, 1 + HALF * f:1 + HALF * f + HALF]
                        wait_emptied(dve, "ln2", n)
                        dve.tensor_tensor(xx[:, c, cols], xT[:, c, cols], now, ALU.subtract).then_inc(xx_done, 1)
                        dve.wait_ge(xx_done, n + 1)
                        dve.scalar_tensor_tensor(out=xxx[:, c, cols], in0=xx[:, c, cols], scalar=vec[:, 0, c:c + 1],
                                                 in1=now, op0=ALU.mult, op1=ALU.add).then_inc(xxx_done, 1)
                    def mixed(n):
                        mi, f, c = n // 4, n // 2 % 2, n % 2
                        cols = slice(HALF * f, HALF * f + HALF)
                        if mi == 2:
                            wait_filled(dve, "dech", 1)
                        if mi == 3:
                            wait_filled(dve, "gateh", 1)
                        if mi == 4:
                            wait_filled(dve, "r", 3)
                        wait_filled(dve, "mix", n)
                        fi = MIX_ORDER[mi]
                        dve.scalar_tensor_tensor(out=xf[:, mi % 2, c, cols], in0=bank("mix", n)[:, :],
                                                 scalar=vec[:, 1 + fi, c:c + 1], in1=xx[:, c, cols],
                                                 op0=ALU.add, op1=ALU.mult).then_inc(dve_emptied, 1)

                    differences(0)
                    differences(1)
                    residual("dn1", 3, 1, 0.5 * S8 * S8 * S8)
                    differences(2)
                    differences(3)
                    mixed(0)
                    mixed(1)
                    for n in range(2, 4 * NMIX):
                        mixed(n)
                    for c in range(NC):
                        wait_emptied(dve, "k", 2 + c)
                        dve.tensor_scalar(ku[:, c, :], kk[:, c, :], vec[:, 7, c:c + 1], None, ALU.mult).then_inc(ku_done, 1)
                    dve.wait_ge(a_zeroed, 1)
                    for n in range(8):
                        c, q = n // 4, n % 4
                        wait_filled(dve, "diag", n)
                        a = A[:, c, 2 * q:2 * q + 2, :, :].rearrange("p n h t -> p (n h) t")
                        dve.copy_predicated(a, dmask[:, :].rearrange("p (a t) -> p a t", a=1).broadcast_to([128, 4, 128]),
                                            bank("diag", n)[:, :].rearrange("p (a t) -> p a t", a=4)).then_inc(dve_emptied, 1)
                    dve.wait_ge(tot_done, LEVELS)
                    for l in range(LEVELS):
                        m = 1 << l
                        tm = wdec if l == 0 else tot[:, :, 1024 - 1024 // (m // 2):1024 - 1024 // m]
                        for c in range(NC):
                            for q in (0, 1):
                                n = 4 * l + 2 * c + q
                                wait_filled(dve, "level", n)
                                dve.wait_ge(dve_emptied, RANK[NTH["level", n - 4] if l else NTH["diag", 7]])
                                a = A[:, c, 4 * q:4 * q + 4, :, :].rearrange("p n h (b s m) -> p (n h) b s m", s=2, m=m)[:, :, :, 1, :]
                                mk = lmask[:, l:l + 1, :].broadcast_to([128, 8, 64]).rearrange("p a (b m) -> p a b m", m=m)
                                dve.copy_predicated(a, mk, bank("level", n)[:, :].rearrange("p (a b m) -> p a b m", a=8, m=m)
                                                    ).then_inc(dve_emptied, 1)
                            for h in (0, 1):
                                p = slice(64 * h, 64 * h + 64)
                                qv = qd[p, c, h, :].rearrange("p (n s m) -> p n s m", s=2, m=m)[:, :, 1, :]
                                w = tm[p, c, :].rearrange("p (n s) -> p n s", s=2)[:, :, 0:1].broadcast_to([64, 512 // m, m])
                                if l:
                                    dve.wait_ge(q_updated, 4 * (l - 1) + 2 * c + h + 1)
                                dve.tensor_tensor(qv, qv, w, ALU.mult).then_inc(q_updated, 1)
                    dve.wait_ge(s_zeroed, 1)
                    for ch in range(NT - 1):
                        for c in range(NC):
                            n = 2 * c + ch // 4
                            wait_filled(dve, "kv", n)
                            if ch:
                                dve.wait_ge(s_chain, 2 * (ch - 1) + c + 1)
                            kv = bank("kv", n)[:, WH * (ch % 4):WH * (ch % 4) + WH]
                            dve.scalar_tensor_tensor(out=S[:, c, ch + 1, :], in0=S[:, c, ch, :],
                                                     scalar=tot[:, c, 1008 + ch:1009 + ch], in1=kv,
                                                     op0=ALU.mult, op1=ALU.add).then_inc(s_chain, 1)
                            if ch in (3, NT - 2):
                                dve.wait_ge(s_chain, 2 * ch + c + 1)
                                dve.engine_nop().then_inc(dve_emptied, 1)
                    for n in range(4):
                        wait_filled(dve, "y", n)
                        if n >= 2:
                            dve.wait_ge(gn_chain, 3 * (n - 2) + 1)
                        ps = bank("y", n)[:, :].rearrange("p (a j) -> p a j", j=WH)
                        for a in range(8):
                            dve.bn_stats(gst[:, a, :], ps[:, a, :]).then_inc(gn_stat, 1)
                        dve.wait_ge(gn_stat, 8 * n + 8)
                        for a in range(8):
                            dve.bn_aggr(gmv[:, n % 2, a, :], gst[:, a, :]).then_inc(gn_aggr, 1)
                        dve.wait_ge(gn_aggr, 8 * n + 8)
                        z = xn[:, 2 * n:2 * n + 2, :]
                        dve.tensor_tensor(z.rearrange("p i (h j) -> p i h j", j=WH),
                                          bank("y", n)[:, :].rearrange("p (i h j) -> p i h j", i=2, j=WH),
                                          gmv[:, n % 2, :, 0:1].rearrange("p (i h) a -> p i h a", i=2).broadcast_to([128, 2, 4, WH]),
                                          ALU.subtract).then_inc(dve_emptied, 1)
                        dve.wait_ge(dve_emptied, RANK[NTH["y", n]])
                        dve.tensor_tensor(z, z, lng[:, 0:1, :].broadcast_to([128, 2, D]), ALU.mult).then_inc(gn_lng, 1)
                    for n in range(4):
                        if n == 3:
                            x_low(3, 1, (0, 1))
                        residual("ob", n, 2)
                    ffn(3, 1)

                @block.tensor
                def _(pe):
                    mm = pe.matmul

                    def transpose_x(k, ns=range(4)):
                        for n in ns:
                            f, c = n // 2, n % 2
                            wait_bank(pe, f"ln{k}", n)
                            for j in range(4):
                                i = 4 * f + j
                                pe.wait_ge(ln_out[k], i + 1)
                                last = pe.transpose(bank(f"ln{k}", n)[:, 128 * j:128 * j + 128],
                                                    xn[:, i, 128 * c:128 * c + 128], ident[:, :])
                            last.then_inc(filled, 1)

                    def xcols(c, f):
                        return xT[:, c, 1 + HALF * f:1 + HALF * f + HALF]

                    def xtile(c, i):
                        return xT[:, c, 1 + 128 * i:1 + 128 * i + 128]

                    def qk_item(e):
                        m, f, q = e // 4, e // 2 % 2, e % 2
                        wait_emptied(pe, "ln0", 2 * f + 1)
                        wait_bank(pe, "qk", e)
                        w0 = D * q + 128 * m
                        for c in range(NC):
                            last = mm(bank("qk", e)[:, :], wqkv[:, c, w0:w0 + 128], xcols(c, f),
                                      start=(c == 0), stop=(c == NC - 1))
                        last.then_inc(filled, 1)

                    def v_item(n):
                        wait_bank(pe, "v", n)
                        for a in (0, 1):
                            for c in range(NC):
                                last = mm(bank("v", n)[:, D * a:D * a + D], xtile(c, 2 * n + a), wqkv[:, c, 2 * D:3 * D],
                                          start=(c == 0), stop=(c == NC - 1))
                        last.then_inc(filled, 1)

                    def max_item(g, k):
                        h, (i, s0, n, col) = max_item_of(k)
                        h += g * HG
                        wait_bank(pe, "max", g * NPC + k)
                        ps = bank("max", g * NPC + k)
                        diag = s0 + n == 128 * (i + 1)
                        last = mm(ps[:, 0:n], qst[0:AUG, h, 128 * i:128 * i + 128], kst[0:AUG, h, s0:s0 + n],
                                  start=True, stop=not diag)
                        if diag:
                            last = mm(ps[:, n - 128:n], identb[:, :], causal[:, :], start=False, stop=True)
                        last.then_inc(filled, 1)

                    def score_item(g, k):
                        u, h = k // HG, g * HG + k % HG
                        j, f = UNITS[u]
                        t0 = max(HALF * f, 128 * j)
                        n = HALF * (f + 1) - t0
                        wait_bank(pe, "score", g * NPC + k)
                        ps = bank("score", g * NPC + k)
                        mm(ps[:, 0:n], kst[0:AUG + 3, h, 128 * j:128 * j + 128], qst[0:AUG + 3, h, t0:t0 + n],
                           start=True, stop=True).then_inc(filled, 1)

                    def pv(g, u):
                        j, f = UNITS[u]
                        t0 = max(HALF * f, 128 * j)
                        n = HALF * (f + 1) - t0
                        U = g * len(UNITS) + u
                        wait_emptied(pe, "score", g * NPC + HG * u + HG - 1)
                        if t0 == 128 * j:
                            pe.wait_ge(masked, DIAG_UNITS.index(U) + 1)
                        if j == 0 and g:
                            pe.wait_ge(pv_copied, 2 * g)
                        for h in range(HG):
                            last = mm(PB[6 + f][32 * h:32 * h + 32, t0 - HALF * f:HALF], vp[:, j, g * HG + h, :],
                                      pt[:, U % 3, h, 0:n], start=(j == 0), stop=(j == 4 * f + 3))
                        last.then_inc(pv_units, 1)

                    for f in (0, 1):
                        transpose_x(0, (2 * f, 2 * f + 1))
                        qk_item(2 * f)
                        qk_item(2 * f + 1)
                    for n in range(4):
                        v_item(n)
                    for e in range(4, 8):
                        qk_item(e)
                    for t in range(NSC + DELAY):
                        if t in (0, 2 * NPC):
                            pe.wait_ge(stacked[t // (2 * NPC)], 9 * 16)
                        if t < NSC:
                            max_item(t // NPC, t % NPC)
                        if NPC <= t < NSC + NPC and t % NPC == AUG_AT:
                            g = t // NPC - 1
                            pe.wait_ge(aug_chain, 6 * g + 6)
                            wait_bank(pe, "aug", g)
                            pe.transpose(bank("aug", g)[0:96, 0:64].bitcast(bf16),
                                         aug[:, :, :, :].rearrange("p r h i -> p (r h i)"), identb[:, :]).then_inc(filled, 1)
                        if t >= DELAY:
                            g, k = (t - DELAY) // NPC, (t - DELAY) % NPC
                            if k == 0:
                                pe.wait_ge(aug_loaded[g], 48)
                                pe.wait_ge(arena_set, 3)
                            score_item(g, k)
                            U = (t - DELAY) // HG
                            if k % HG == HG - 1 and U >= 2:
                                pv((U - 2) // len(UNITS), (U - 2) % len(UNITS))
                    pv(NG - 1, len(UNITS) - 2)
                    pv(NG - 1, len(UNITS) - 1)

                    def out_proj(n, a, gs):
                        for g in gs:
                            last = mm(bank("o", n)[:, D * a:D * a + D], attn[:, 2 * n + a, g, :], wo[:, g, :],
                                      start=(g == 0), stop=(g == NG - 1))
                        return last

                    pe.wait_ge(attn_normed, 2 * NG - 2)
                    for n in range(4):
                        wait_bank(pe, "o", n)
                        out_proj(n, 0, range(NG - 1))
                    for n in range(4):
                        pe.wait_ge(attn_normed, 2 * NG - 1 + n // 2)
                        out_proj(n, 0, (NG - 1,))
                        out_proj(n, 1, range(NG)).then_inc(filled, 1)
                        if n == 2:
                            transpose_x(1, (0, 1))

                    def ffn(k, s, general):
                        def products(dst, pairs):
                            for j, (lhs, rhs) in enumerate(pairs):
                                last = mm(dst, lhs, rhs, start=(j == 0), stop=(j == len(pairs) - 1))
                            return last

                        def down(n):
                            pe.wait_ge(h_low[s], NM * (n // 2 + 1))
                            wait_bank(pe, f"dn{k}", n)
                            for a in (0, 1):
                                t = slice(128 * (2 * n + a), 128 * (2 * n + a) + 128)
                                last = products(bank(f"dn{k}", n)[:, D * a:D * a + D],
                                                [(h[:, m, t], w[:, m, :]) for m in range(NM)
                                                 for w in ((wd, wdl) if general else (wd,)) for h in (hh, hl)])
                            last.then_inc(filled, 1)

                        if general:
                            pe.wait_ge(wlow_loaded[s], 16)
                        for f in (0, 1):
                            cols = slice(HALF * f, HALF * f + HALF)
                            wait_emptied(pe, f"ln{k}", 2 * f + 1)
                            for e in range(2 * NM):
                                if f == 0 and e == 4:
                                    transpose_x(k, (2, 3))
                                m, r = e // 2, e % 2
                                rows = slice(HID * r + 128 * m, HID * r + 128 * m + 128)
                                wait_bank(pe, f"gu{k}", 2 * NM * f + e)
                                products(bank(f"gu{k}", 2 * NM * f + e)[:, :],
                                         [(w[:, c, rows], x[:, c, cols]) for c in range(NC)
                                          for w in ((wgu, wgul) if general else (wgu,)) for x in (xh, xl)]
                                         ).then_inc(filled, 1)
                                if f == 1 and e == DOWN_AT:
                                    down(0)
                        down(1)
                        down(2)
                        if k == 1:
                            transpose_x(2, (0, 1))
                        down(3)

                    wide = pe.alloc_register(name="wide_pe")
                    pe.reg_load(wide, wide_flag[0:1, 0:1])
                    with pe.If_ne(wide, 0):
                        ffn(1, 0, True)
                    with pe.Else():
                        ffn(1, 0, False)
                    def mix_item(mi, q):
                        n, f, co = 4 * mi + q, q // 2, q % 2
                        fi = MIX_ORDER[mi]
                        wait_emptied(pe, "lora", 2 * f + 1)
                        wait_bank(pe, "mix", n)
                        mm(bank("mix", n)[:, :], mw2[:, fi, 128 * co:128 * co + 128],
                           lora[:, fi // 4, HALF * f:HALF * f + HALF], start=True, stop=True).then_inc(filled, 1)

                    for n in range(4):
                        l, f = n % 2, n // 2
                        if n == 2:
                            transpose_x(2, (2, 3))
                            mix_item(0, 0)
                            mix_item(0, 1)
                        pe.wait_ge(xxx_done, 2 * f + 2)
                        wait_bank(pe, "lora", n)
                        for c in range(NC):
                            last = mm(bank("lora", n)[:, :], mw1[:, c, 32 * l:32 * l + 128],
                                      xxx[:, c, HALF * f:HALF * f + HALF], start=(c == 0), stop=(c == NC - 1))
                        last.then_inc(filled, 1)

                    def hidden(kind, r, w0, slot, n0):
                        for f in (0, 1):
                            pe.wait_ge(mix_added, 4 * n0 + 2 * f + 2)
                            wait_bank(pe, kind, f)
                            for c in range(NC):
                                last = mm(bank(kind, f)[r:r + 64, :], low1[:, c, w0:w0 + DLOW],
                                          xf[:, slot, c, HALF * f:HALF * f + HALF], start=(c == 0), stop=(c == NC - 1))
                            last.then_inc(filled, 1)

                    def channel_major(kind, w0, slot, n0):
                        for n in range(4):
                            co, f = n % 2, n // 2
                            pe.wait_ge(mix_added, 4 * n0 + 2 * f + 2)
                            wait_bank(pe, kind, n)
                            for c in range(NC):
                                last = mm(bank(kind, n)[:, :], bm[:, c, w0 + 128 * co:w0 + 128 * co + 128],
                                          xf[:, slot, c, HALF * f:HALF * f + HALF], start=(c == 0), stop=(c == NC - 1))
                            last.then_inc(filled, 1)

                    for mi in range(NMIX):
                        for q in range(2 if mi == 0 else 0, 4):
                            mix_item(mi, q)
                        if mi == 1:
                            hidden("dech", 64, DLOW, 0, 0)
                        if mi == 2:
                            hidden("gateh", 0, 0, 1, 1)
                        if mi == 3:
                            for n in range(4):
                                co, f = n % 2, n // 2
                                wait_emptied(pe, "gateh", f)
                                wait_bank(pe, "w", n)
                                mm(bank("w", n)[:, :], low2[:, 1, 128 * co:128 * co + 128],
                                   th[:, HALF * f:HALF * f + HALF], start=True, stop=True).then_inc(filled, 1)
                            channel_major("r", 0, 0, 2)
                        if mi == 4:
                            for n in range(4):
                                wait_bank(pe, "g", n)
                                for a in (0, 1):
                                    last = mm(bank("g", n)[:, D * a:D * a + D], th[:, 128 * (2 * n + a):128 * (2 * n + a) + 128],
                                              low2[:, 0, :], start=True, stop=True)
                                last.then_inc(filled, 1)
                            channel_major("k", D, 1, 3)
                            for n in range(4):
                                pe.wait_ge(mix_added, 16 + 2 * (n // 2) + 2)
                                wait_bank(pe, "vb", n)
                                for a in (0, 1):
                                    i = 2 * n + a
                                    for c in range(NC):
                                        last = mm(bank("vb", n)[:, D * a:D * a + D], xf[:, 0, c, 128 * i:128 * i + 128],
                                                  bm[:, c, 2 * D:3 * D], start=(c == 0), stop=(c == NC - 1))
                                last.then_inc(filled, 1)
                    wait_emptied(pe, "r", 3)
                    for n in range(8):
                        c, q = n // 4, n % 4
                        pe.wait_ge(ku_done, c + 1)
                        wait_bank(pe, "diag", n)
                        for a in (0, 1):
                            ch = 2 * q + a
                            last = mm(bank("diag", n)[:, 256 * a:256 * a + 256].rearrange("p (h t) -> p h t", h=2),
                                      ku[:, c, 128 * ch:128 * ch + 128], qd[:, c, :, 128 * ch:128 * ch + 128],
                                      start=True, stop=True)
                        last.then_inc(filled, 1)
                    for l in range(LEVELS):
                        m = 1 << l
                        for c in range(NC):
                            for q in (0, 1):
                                n = 4 * l + 2 * c + q
                                if l:
                                    pe.wait_ge(q_updated, 4 * (l - 1) + 2 * c + 2)
                                    pe.wait_ge(k_updated, 2 * (l - 1) + c + 1)
                                wait_bank(pe, "level", n)
                                for a in range(4):
                                    ch = 4 * q + a
                                    rhs = qd[:, c, :, 128 * ch:128 * ch + 128].rearrange("p h (b s m) -> p h b s m", s=2, m=m)[:, :, :, 1, :]
                                    last = mm(bank("level", n)[:, 128 * a:128 * a + 128].rearrange("p (h b m) -> p h b m", h=2, m=m),
                                              kk[:, c, 128 * ch:128 * ch + 128], rhs, start=True, stop=True)
                                last.then_inc(filled, 1)
                    for n in range(4):
                        c = n // 2
                        pe.wait_ge(k_updated, 2 * (LEVELS - 1) + c + 1)
                        wait_bank(pe, "kt", n)
                        for a in range(4):
                            ch = 4 * (n % 2) + a
                            last = pe.transpose(bank("kt", n)[:, 128 * a:128 * a + 128], kk[:, c, 128 * ch:128 * ch + 128],
                                                ident[:, :])
                        last.then_inc(filled, 1)
                    for n in KV_ORDER:
                        c = n // 2
                        wait_emptied(pe, "kt", n)
                        wait_bank(pe, "kv", n)
                        for a in range(4 if n % 2 == 0 else 3):
                            ch = 4 * (n % 2) + a
                            for h in (0, 1):
                                last = mm(bank("kv", n)[64 * h:64 * h + 64, WH * a:WH * a + WH],
                                          kn[:, c, ch, 64 * h:64 * h + 64], vt[:, ch, 128 * c + WH * h:128 * c + WH * h + WH],
                                          start=True, stop=True)
                        last.then_inc(filled, 1)
                    wait_emptied(pe, "level", LEVELS * 4 - 1)
                    pe.wait_ge(q_updated, 4 * LEVELS)
                    for n in range(4):
                        wait_bank(pe, "y", n)
                        pe.wait_ge(s_chain, 2 * (2 * n + 1))
                        for a in (0, 1):
                            ch = 2 * n + a
                            for hd in range(4):
                                c, h = hd // 2, hd % 2
                                o = bank("y", n)[:, D * a + WH * hd:D * a + WH * hd + WH]
                                last = mm(o, A[:, c, ch, h, :], vt[:, ch, WH * hd:WH * hd + WH], start=True, stop=(ch == 0))
                                if ch:
                                    last = mm(o, qd[:, c, h, 128 * ch:128 * ch + 128], S[:, c, ch, :], start=False, stop=True)
                        last.then_inc(filled, 1)
                    for f in (0, 1):
                        pe.wait_ge(gn_chain, 6 * f + 6)
                        for c in range(NC):
                            n = 2 * f + c
                            wait_bank(pe, "zt", n)
                            for j in range(4):
                                last = pe.transpose(bank("zt", n)[:, 128 * j:128 * j + 128],
                                                    xn[:, 4 * f + j, 128 * c:128 * c + 128], ident[:, :])
                            last.then_inc(filled, 1)
                        wait_emptied(pe, "zt", 2 * f + 1)
                        for n in (2 * f, 2 * f + 1):
                            wait_bank(pe, "ob", n)
                            for a in (0, 1):
                                i = 2 * n + a
                                for c in range(NC):
                                    last = mm(bank("ob", n)[:, D * a:D * a + D], zT[:, c, 128 * i:128 * i + 128],
                                              bm[:, c, 3 * D:4 * D], start=(c == 0), stop=(c == NC - 1))
                            last.then_inc(filled, 1)
                            if n == 2:
                                transpose_x(3, (0, 1))
                    with pe.If_ne(wide, 0):
                        ffn(3, 1, True)
                    with pe.Else():
                        ffn(3, 1, False)

            nc.sync.sem_clear(range(sems[6].num, sems[-1].num + 1))
            nc.all_engine_barrier()


STOP = None


def kernel(**inputs):
    import numpy as np
    import concourse.bacc as bacc
    from concourse.bass_utils import run_bass_kernel_spmd as run

    g = {k: np.asarray(v) for k, v in inputs.items()}
    arrays = {"x": g["L0_attn_a_x"]}
    wq, wk = g["L0_attn_a_Wq"], g["L0_attn_a_Wk"]
    for name, w in (("wq", wq), ("wk", wk), ("wv", g["L0_attn_a_Wv"]), ("wo", g["L0_attn_a_Wo"])):
        arrays[name] = w.T
    for name in ("Wr", "Wk", "Wv", "Wo", "maa_w1", "maa_w2", "gate_w1", "gate_w2", "decay_w1", "decay_w2"):
        arrays["b_" + name] = g["L0_attn_b_" + name]
    names = ("maa_x", "maa_w", "maa_k", "maa_v", "maa_r", "maa_g", "time_decay", "u")
    arrays["vec"] = np.stack([g["L0_attn_b_" + n].reshape(NC, 128) for n in names]).transpose(2, 0, 1).reshape(128, -1)
    arrays["ln_g"], arrays["ln_b"] = g["L0_attn_b_ln_g"], g["L0_attn_b_ln_b"]
    for name in ("w_gate", "w_up", "w_down"):
        arrays["f_" + name] = g["L0_ffn_" + name].T
    inv = (np.float32(1.0) / np.float32(10000.0) ** (np.arange(0, DH, 2, dtype=np.float32) / np.float32(DH))).astype(np.float32)
    ang = (np.arange(T, dtype=np.float32)[:, None] * inv[None, :]).astype(np.float32)
    cos = np.concatenate([np.cos(ang)] * 2, 1).T
    sin = np.concatenate([-np.sin(ang), np.sin(ang)], 1).T
    arrays["cos"] = np.tile(cos, (128 // DH, 1)).astype(np.float32)
    arrays["sin"] = np.tile(sin, (128 // DH, 1)).astype(np.float32)
    p, q = np.arange(128)[:, None], np.arange(128)[None, :]
    arrays["cf"] = np.concatenate([p == q, np.where(q > p, NEG, 0)], 1).astype(np.float32)
    masks = []
    for l in range(LEVELS):
        m = 1 << l
        t = np.array([2 * m * b + m + r for b in range(64 // m) for r in range(m)])[None, :]
        masks.append((p // (2 * m) == t // (2 * m)) & (p % (2 * m) < m))
    arrays["ci"] = np.concatenate(masks + [p == q], 1).astype(np.int32)
    arrays = {"in_" + k: np.ascontiguousarray(v) for k, v in arrays.items()}

    nc = bacc.Bacc("TRN2", target_bir_lowering=False, num_devices=1)
    d = {k: nc.dram_tensor(k, v.shape, mybir.dt.from_np(v.dtype), kind="ExternalInput").ap() for k, v in arrays.items()}
    out = nc.dram_tensor("out", (NB, T, D), mybir.dt.float32, kind="ExternalOutput").ap()
    build(nc, d["in_x"], [d["in_" + k] for k in ("wq", "wk", "wv", "wo")], [d["in_cos"], d["in_sin"]],
          [d["in_vec"], d["in_ln_g"], d["in_ln_b"]],
          [d["in_b_" + k] for k in ("Wr", "Wk", "Wv", "Wo", "maa_w1", "maa_w2", "gate_w1", "gate_w2", "decay_w1", "decay_w2")],
          [d["in_f_" + k] for k in ("w_gate", "w_up", "w_down")], [d["in_cf"], d["in_ci"]], out, STOP)
    return run(nc, [arrays], core_ids=[0]).results[0]["out"]
```
